# Optimizing a Trainium2 kernel written in Bass

```python
import numpy as np
import jax
import jax.numpy as jnp

def _softmax(x, axis=-1):
    return jax.nn.softmax(x, axis=axis)
def _gelu(x):
    return jax.nn.gelu(x, approximate=True)
def _silu(x):
    return jax.nn.silu(x)
def _sigmoid(x):
    return jax.nn.sigmoid(x)
def _layernorm(x, axis=-1, eps=1e-5):
    m = jnp.mean(x, axis=axis, keepdims=True)
    v = jnp.var(x, axis=axis, keepdims=True)
    return (x - m) / jnp.sqrt(v + eps)
def _scatter_add(tgt, idx, src, axis=0):
    return tgt.at[idx].add(src)
def _segment_sum(src, seg, n):
    return jax.ops.segment_sum(src, seg, n)

kernel_name = 'mk_conv_attn_hybrid_d2_conv_nhwc128_337ffe'

def setup_inputs(seed: int = 0):
    np.random.seed(seed)
    _w = jnp.asarray
    def _rec_inputs():
        import jax
        import jax.numpy as jnp
        _gk = jax.random.key(seed)
        x = -0.0005207 + 1.001 * jax.random.normal(jax.random.fold_in(_gk, 1), (4, 64, 64, 128), jnp.float32)
        return x
    x = _rec_inputs()
    def _L0_conv_setup():
        import jax, jax.numpy as jnp
        import numpy as np
        from jax import lax
        D_MODEL, D_INNER, D_STATE, DT_RANK, KDIR = (64, 128, 16, 4, 4)

        def _silu(x):
            return x * jax.nn.sigmoid(x)

        def _conv1x1(x, w):
            return jnp.einsum('bhwc,oc->bhwo', x, w)

        def _bn(x, g, b):
            return x * g + b

        def _conv3x3(x, w, b):
            y = lax.conv_general_dilated(x, w, (1, 1), 'SAME', dimension_numbers=('NHWC', 'HWIO', 'NHWC'))
            return y + b

        def _ss2d(x, in_proj_w, dw_w, dw_b, x_proj_w, dt_w, dt_b, A_logs, Ds, ln_g, ln_b, out_proj_w):
            B, H, W, _ = x.shape
            L = H * W
            xz = jnp.einsum('bhwd,ed->bhwe', x, in_proj_w)
            xh, z = jnp.split(xz, 2, axis=-1)
            xh = lax.conv_general_dilated(xh, dw_w, (1, 1), 'SAME', dimension_numbers=('NHWC', 'HWIO', 'NHWC'), feature_group_count=D_INNER) + dw_b
            xh = _silu(xh)
            x1 = xh.transpose(0, 3, 1, 2).reshape(B, D_INNER, L)
            x2 = xh.transpose(0, 3, 2, 1).reshape(B, D_INNER, L)
            xs = jnp.stack([x1, x2, x1[:, :, ::-1], x2[:, :, ::-1]], axis=1)
            x_dbl = jnp.einsum('bkdl,kcd->bkcl', xs, x_proj_w)
            dts = jnp.einsum('bkrl,kdr->bkdl', x_dbl[:, :, :DT_RANK], dt_w) + dt_b[None, :, :, None]
            Bs = x_dbl[:, :, DT_RANK:DT_RANK + D_STATE]
            Cs = x_dbl[:, :, DT_RANK + D_STATE:]
            delta = jax.nn.softplus(dts)
            A = -jnp.exp(A_logs).reshape(KDIR, D_INNER, D_STATE)
            Dk = Ds.reshape(KDIR, D_INNER)

            def step(h, inp):
                d, u, b, c = inp
                dA = jnp.exp(d[..., None] * A)
                h = dA * h + (d * u)[..., None] * b[:, :, None, :]
                y = jnp.sum(h * c[:, :, None, :], axis=-1)
                return (h, y)
            h0 = jnp.zeros((B, KDIR, D_INNER, D_STATE), xh.dtype)
            seq = (delta.transpose(3, 0, 1, 2), xs.transpose(3, 0, 1, 2), Bs.transpose(3, 0, 1, 2), Cs.transpose(3, 0, 1, 2))
            _, ys = lax.scan(step, h0, seq)
            y = ys.transpose(1, 2, 3, 0) + Dk[None, :, :, None] * xs
            wh = y[:, 1].reshape(B, D_INNER, W, H).transpose(0, 1, 3, 2).reshape(B, D_INNER, L)
            iwh = y[:, 3, :, ::-1].reshape(B, D_INNER, W, H).transpose(0, 1, 3, 2).reshape(B, D_INNER, L)
            yc = y[:, 0] + y[:, 2, :, ::-1] + wh + iwh
            yc = yc.transpose(0, 2, 1).reshape(B, H, W, D_INNER)
            mu = yc.mean(-1, keepdims=True)
            var = yc.var(-1, keepdims=True)
            yc = (yc - mu) / jnp.sqrt(var + 1e-05) * ln_g + ln_b
            yc = yc * _silu(z)
            return jnp.einsum('bhwe,de->bhwd', yc, out_proj_w)

        def _forward(x, cv1_w, cv1_g, cv1_b, in_proj_w, dw_w, dw_b, x_proj_w, dt_w, dt_b, A_logs, Ds, ln_g, ln_b, out_proj_w, cv2_w, cv2_g, cv2_b, bn0_g, bn0_b, c1_w, c1_b, bn1_g, bn1_b, c2_w, c2_b, bn2_g, bn2_b, c3_w, c3_b, cv_w, cv_g, cv_b, cv3_w, cv3_g, cv3_b):
            left, right = jnp.split(x, 2, axis=-1)
            right = _silu(_bn(_conv1x1(right, cv1_w), cv1_g, cv1_b))
            xr = _ss2d(right, in_proj_w, dw_w, dw_b, x_proj_w, dt_w, dt_b, A_logs, Ds, ln_g, ln_b, out_proj_w)
            l = _silu(_bn(_conv1x1(left, cv2_w), cv2_g, cv2_b))
            l = _bn(l, bn0_g, bn0_b)
            l = jax.nn.relu(_bn(_conv3x3(l, c1_w, c1_b), bn1_g, bn1_b))
            l = jax.nn.relu(_bn(_conv3x3(l, c2_w, c2_b), bn2_g, bn2_b))
            l = jax.nn.relu(_conv1x1(l, c3_w) + c3_b)
            xr = _silu(_bn(_conv1x1(xr, cv_w), cv_g, cv_b))
            out = jnp.concatenate([l, xr], axis=-1)
            out = _silu(_bn(_conv1x1(out, cv3_w), cv3_g, cv3_b))
            B, H, W, C = out.shape
            out = out.reshape(B, H, W, 2, C // 2).swapaxes(-1, -2).reshape(B, H, W, C)
            return out + x
        ks = iter(jax.random.split(jax.random.key(seed), 64))

        def rn(shape, s):
            return jax.random.normal(next(ks), shape, jnp.float32) * s
        D, DI, N, R, Kd = (D_MODEL, D_INNER, D_STATE, DT_RANK, KDIR)
        inp = {}
        inp['x'] = jax.random.normal(next(ks), (4, 64, 64, 128), jnp.float32)
        inp['cv1_w'] = rn((D, D), 0.1)
        inp['cv1_g'] = 1.0 + rn((D,), 0.05)
        inp['cv1_b'] = rn((D,), 0.05)
        inp['in_proj_w'] = rn((2 * DI, D), 0.08)
        inp['dw_w'] = rn((3, 3, 1, DI), 0.1)
        inp['dw_b'] = rn((DI,), 0.05)
        inp['x_proj_w'] = rn((Kd, R + 2 * N, DI), 0.08)
        inp['dt_w'] = rn((Kd, DI, R), 0.1)
        inp['dt_b'] = rn((Kd, DI), 0.1)
        inp['A_logs'] = jnp.tile(jnp.log(jnp.arange(1.0, N + 1.0, dtype=jnp.float32)), (Kd * DI, 1))
        inp['Ds'] = jnp.ones((Kd * DI,), jnp.float32)
        inp['ln_g'] = jnp.ones((DI,), jnp.float32)
        inp['ln_b'] = jnp.zeros((DI,), jnp.float32)
        inp['out_proj_w'] = rn((D, DI), 0.08)
        inp['cv2_w'] = rn((D, D), 0.1)
        inp['cv2_g'] = 1.0 + rn((D,), 0.05)
        inp['cv2_b'] = rn((D,), 0.05)
        inp['bn0_g'] = 1.0 + rn((D,), 0.05)
        inp['bn0_b'] = rn((D,), 0.05)
        inp['c1_w'] = rn((3, 3, D, D), 0.06)
        inp['c1_b'] = rn((D,), 0.05)
        inp['bn1_g'] = 1.0 + rn((D,), 0.05)
        inp['bn1_b'] = rn((D,), 0.05)
        inp['c2_w'] = rn((3, 3, D, D), 0.06)
        inp['c2_b'] = rn((D,), 0.05)
        inp['bn2_g'] = 1.0 + rn((D,), 0.05)
        inp['bn2_b'] = rn((D,), 0.05)
        inp['c3_w'] = rn((D, D), 0.1)
        inp['c3_b'] = rn((D,), 0.05)
        inp['cv_w'] = rn((D, D), 0.1)
        inp['cv_g'] = 1.0 + rn((D,), 0.05)
        inp['cv_b'] = rn((D,), 0.05)
        inp['cv3_w'] = rn((2 * D, 2 * D), 0.08)
        inp['cv3_g'] = 1.0 + rn((2 * D,), 0.05)
        inp['cv3_b'] = rn((2 * D,), 0.05)
        return inp
    _L0_conv_all = _L0_conv_setup()
    _L0_conv_in = {k: v for k, v in _L0_conv_all.items() if k in ('cv1_w', 'cv1_g', 'cv1_b', 'in_proj_w', 'dw_w', 'dw_b', 'x_proj_w', 'dt_w', 'dt_b', 'A_logs', 'Ds', 'ln_g', 'ln_b', 'out_proj_w', 'cv2_w', 'cv2_g', 'cv2_b', 'bn0_g', 'bn0_b', 'c1_w', 'c1_b', 'bn1_g', 'bn1_b', 'c2_w', 'c2_b', 'bn2_g', 'bn2_b', 'c3_w', 'c3_b', 'cv_w', 'cv_g', 'cv_b', 'cv3_w', 'cv3_g', 'cv3_b', )}
    del _L0_conv_all

    def _L1_attn_setup():
        import jax, jax.numpy as jnp
        import numpy as np
        B, T, C = (4096, 64, 128)
        N_HEAD = 8
        D_HEAD = C // N_HEAD
        key = jax.random.key(seed)
        k1, k2, k3 = jax.random.split(key, 3)
        x = jax.random.normal(k1, (B, T, C), dtype=jnp.float32)
        w_attn = jax.random.normal(k2, (C, 3 * C), dtype=jnp.float32) * 0.02
        w_proj = jax.random.normal(k3, (C, C), dtype=jnp.float32) * 0.02
        return {'x': x, 'w_attn': w_attn, 'w_proj': w_proj}
    _L1_attn_all = _L1_attn_setup()
    _L1_attn_in = {k: v for k, v in _L1_attn_all.items() if k in ('w_attn', 'w_proj', )}
    del _L1_attn_all

    def _L1_ffn_setup():
        import jax, jax.numpy as jnp
        import numpy as np
        B, N, D, C, E, K = (8, 8192, 128, 128, 8, 2)
        key = jax.random.key(seed)
        k0, k1, k2 = jax.random.split(key, 3)
        x = jax.random.normal(k0, (B, N, D), dtype=jnp.float32)
        router_w = jax.random.normal(k1, (D, E), dtype=jnp.float32) * 0.05
        router_b = jnp.zeros((E,), dtype=jnp.float32)
        expert_w = jax.random.normal(k2, (E, D, C), dtype=jnp.float32) * (1.0 / np.sqrt(D))
        expert_b = jnp.zeros((E, C), dtype=jnp.float32)
        return {'x': x, 'router_w': router_w, 'router_b': router_b, 'expert_w': expert_w, 'expert_b': expert_b}
    _L1_ffn_all = _L1_ffn_setup()
    _L1_ffn_in = {k: v for k, v in _L1_ffn_all.items() if k in ('router_w', 'router_b', 'expert_w', 'expert_b', )}
    del _L1_ffn_all

    return {
        "x": x,
        "L0_conv_cv1_w": _L0_conv_in["cv1_w"],
        "L0_conv_cv1_g": _L0_conv_in["cv1_g"],
        "L0_conv_cv1_b": _L0_conv_in["cv1_b"],
        "L0_conv_in_proj_w": _L0_conv_in["in_proj_w"],
        "L0_conv_dw_w": _L0_conv_in["dw_w"],
        "L0_conv_dw_b": _L0_conv_in["dw_b"],
        "L0_conv_x_proj_w": _L0_conv_in["x_proj_w"],
        "L0_conv_dt_w": _L0_conv_in["dt_w"],
        "L0_conv_dt_b": _L0_conv_in["dt_b"],
        "L0_conv_A_logs": _L0_conv_in["A_logs"],
        "L0_conv_Ds": _L0_conv_in["Ds"],
        "L0_conv_ln_g": _L0_conv_in["ln_g"],
        "L0_conv_ln_b": _L0_conv_in["ln_b"],
        "L0_conv_out_proj_w": _L0_conv_in["out_proj_w"],
        "L0_conv_cv2_w": _L0_conv_in["cv2_w"],
        "L0_conv_cv2_g": _L0_conv_in["cv2_g"],
        "L0_conv_cv2_b": _L0_conv_in["cv2_b"],
        "L0_conv_bn0_g": _L0_conv_in["bn0_g"],
        "L0_conv_bn0_b": _L0_conv_in["bn0_b"],
        "L0_conv_c1_w": _L0_conv_in["c1_w"],
        "L0_conv_c1_b": _L0_conv_in["c1_b"],
        "L0_conv_bn1_g": _L0_conv_in["bn1_g"],
        "L0_conv_bn1_b": _L0_conv_in["bn1_b"],
        "L0_conv_c2_w": _L0_conv_in["c2_w"],
        "L0_conv_c2_b": _L0_conv_in["c2_b"],
        "L0_conv_bn2_g": _L0_conv_in["bn2_g"],
        "L0_conv_bn2_b": _L0_conv_in["bn2_b"],
        "L0_conv_c3_w": _L0_conv_in["c3_w"],
        "L0_conv_c3_b": _L0_conv_in["c3_b"],
        "L0_conv_cv_w": _L0_conv_in["cv_w"],
        "L0_conv_cv_g": _L0_conv_in["cv_g"],
        "L0_conv_cv_b": _L0_conv_in["cv_b"],
        "L0_conv_cv3_w": _L0_conv_in["cv3_w"],
        "L0_conv_cv3_g": _L0_conv_in["cv3_g"],
        "L0_conv_cv3_b": _L0_conv_in["cv3_b"],
        "L1_attn_w_attn": _L1_attn_in["w_attn"],
        "L1_attn_w_proj": _L1_attn_in["w_proj"],
        "L1_ffn_router_w": _L1_ffn_in["router_w"],
        "L1_ffn_router_b": _L1_ffn_in["router_b"],
        "L1_ffn_expert_w": _L1_ffn_in["expert_w"],
        "L1_ffn_expert_b": _L1_ffn_in["expert_b"],
    }

def reference(x, L0_conv_cv1_w, L0_conv_cv1_g, L0_conv_cv1_b, L0_conv_in_proj_w, L0_conv_dw_w, L0_conv_dw_b, L0_conv_x_proj_w, L0_conv_dt_w, L0_conv_dt_b, L0_conv_A_logs, L0_conv_Ds, L0_conv_ln_g, L0_conv_ln_b, L0_conv_out_proj_w, L0_conv_cv2_w, L0_conv_cv2_g, L0_conv_cv2_b, L0_conv_bn0_g, L0_conv_bn0_b, L0_conv_c1_w, L0_conv_c1_b, L0_conv_bn1_g, L0_conv_bn1_b, L0_conv_c2_w, L0_conv_c2_b, L0_conv_bn2_g, L0_conv_bn2_b, L0_conv_c3_w, L0_conv_c3_b, L0_conv_cv_w, L0_conv_cv_g, L0_conv_cv_b, L0_conv_cv3_w, L0_conv_cv3_g, L0_conv_cv3_b, L1_attn_w_attn, L1_attn_w_proj, L1_ffn_router_w, L1_ffn_router_b, L1_ffn_expert_w, L1_ffn_expert_b):
    import jax
    import jax.numpy as jnp
    def _L0_conv_ref(x, cv1_w, cv1_g, cv1_b, in_proj_w, dw_w, dw_b, x_proj_w, dt_w, dt_b, A_logs, Ds, ln_g, ln_b, out_proj_w, cv2_w, cv2_g, cv2_b, bn0_g, bn0_b, c1_w, c1_b, bn1_g, bn1_b, c2_w, c2_b, bn2_g, bn2_b, c3_w, c3_b, cv_w, cv_g, cv_b, cv3_w, cv3_g, cv3_b):
        import jax, jax.numpy as jnp
        import numpy as np
        from jax import lax
        D_MODEL, D_INNER, D_STATE, DT_RANK, KDIR = (64, 128, 16, 4, 4)

        def _silu(x):
            return x * jax.nn.sigmoid(x)

        def _conv1x1(x, w):
            return jnp.einsum('bhwc,oc->bhwo', x, w)

        def _bn(x, g, b):
            return x * g + b

        def _conv3x3(x, w, b):
            y = lax.conv_general_dilated(x, w, (1, 1), 'SAME', dimension_numbers=('NHWC', 'HWIO', 'NHWC'))
            return y + b

        def _ss2d(x, in_proj_w, dw_w, dw_b, x_proj_w, dt_w, dt_b, A_logs, Ds, ln_g, ln_b, out_proj_w):
            B, H, W, _ = x.shape
            L = H * W
            xz = jnp.einsum('bhwd,ed->bhwe', x, in_proj_w)
            xh, z = jnp.split(xz, 2, axis=-1)
            xh = lax.conv_general_dilated(xh, dw_w, (1, 1), 'SAME', dimension_numbers=('NHWC', 'HWIO', 'NHWC'), feature_group_count=D_INNER) + dw_b
            xh = _silu(xh)
            x1 = xh.transpose(0, 3, 1, 2).reshape(B, D_INNER, L)
            x2 = xh.transpose(0, 3, 2, 1).reshape(B, D_INNER, L)
            xs = jnp.stack([x1, x2, x1[:, :, ::-1], x2[:, :, ::-1]], axis=1)
            x_dbl = jnp.einsum('bkdl,kcd->bkcl', xs, x_proj_w)
            dts = jnp.einsum('bkrl,kdr->bkdl', x_dbl[:, :, :DT_RANK], dt_w) + dt_b[None, :, :, None]
            Bs = x_dbl[:, :, DT_RANK:DT_RANK + D_STATE]
            Cs = x_dbl[:, :, DT_RANK + D_STATE:]
            delta = jax.nn.softplus(dts)
            A = -jnp.exp(A_logs).reshape(KDIR, D_INNER, D_STATE)
            Dk = Ds.reshape(KDIR, D_INNER)

            def step(h, inp):
                d, u, b, c = inp
                dA = jnp.exp(d[..., None] * A)
                h = dA * h + (d * u)[..., None] * b[:, :, None, :]
                y = jnp.sum(h * c[:, :, None, :], axis=-1)
                return (h, y)
            h0 = jnp.zeros((B, KDIR, D_INNER, D_STATE), xh.dtype)
            seq = (delta.transpose(3, 0, 1, 2), xs.transpose(3, 0, 1, 2), Bs.transpose(3, 0, 1, 2), Cs.transpose(3, 0, 1, 2))
            _, ys = lax.scan(step, h0, seq)
            y = ys.transpose(1, 2, 3, 0) + Dk[None, :, :, None] * xs
            wh = y[:, 1].reshape(B, D_INNER, W, H).transpose(0, 1, 3, 2).reshape(B, D_INNER, L)
            iwh = y[:, 3, :, ::-1].reshape(B, D_INNER, W, H).transpose(0, 1, 3, 2).reshape(B, D_INNER, L)
            yc = y[:, 0] + y[:, 2, :, ::-1] + wh + iwh
            yc = yc.transpose(0, 2, 1).reshape(B, H, W, D_INNER)
            mu = yc.mean(-1, keepdims=True)
            var = yc.var(-1, keepdims=True)
            yc = (yc - mu) / jnp.sqrt(var + 1e-05) * ln_g + ln_b
            yc = yc * _silu(z)
            return jnp.einsum('bhwe,de->bhwd', yc, out_proj_w)

        def _forward(x, cv1_w, cv1_g, cv1_b, in_proj_w, dw_w, dw_b, x_proj_w, dt_w, dt_b, A_logs, Ds, ln_g, ln_b, out_proj_w, cv2_w, cv2_g, cv2_b, bn0_g, bn0_b, c1_w, c1_b, bn1_g, bn1_b, c2_w, c2_b, bn2_g, bn2_b, c3_w, c3_b, cv_w, cv_g, cv_b, cv3_w, cv3_g, cv3_b):
            left, right = jnp.split(x, 2, axis=-1)
            right = _silu(_bn(_conv1x1(right, cv1_w), cv1_g, cv1_b))
            xr = _ss2d(right, in_proj_w, dw_w, dw_b, x_proj_w, dt_w, dt_b, A_logs, Ds, ln_g, ln_b, out_proj_w)
            l = _silu(_bn(_conv1x1(left, cv2_w), cv2_g, cv2_b))
            l = _bn(l, bn0_g, bn0_b)
            l = jax.nn.relu(_bn(_conv3x3(l, c1_w, c1_b), bn1_g, bn1_b))
            l = jax.nn.relu(_bn(_conv3x3(l, c2_w, c2_b), bn2_g, bn2_b))
            l = jax.nn.relu(_conv1x1(l, c3_w) + c3_b)
            xr = _silu(_bn(_conv1x1(xr, cv_w), cv_g, cv_b))
            out = jnp.concatenate([l, xr], axis=-1)
            out = _silu(_bn(_conv1x1(out, cv3_w), cv3_g, cv3_b))
            B, H, W, C = out.shape
            out = out.reshape(B, H, W, 2, C // 2).swapaxes(-1, -2).reshape(B, H, W, C)
            return out + x
        return _forward(x, cv1_w, cv1_g, cv1_b, in_proj_w, dw_w, dw_b, x_proj_w, dt_w, dt_b, A_logs, Ds, ln_g, ln_b, out_proj_w, cv2_w, cv2_g, cv2_b, bn0_g, bn0_b, c1_w, c1_b, bn1_g, bn1_b, c2_w, c2_b, bn2_g, bn2_b, c3_w, c3_b, cv_w, cv_g, cv_b, cv3_w, cv3_g, cv3_b)

    def _L1_attn_ref(x, w_attn, w_proj):
        import jax, jax.numpy as jnp
        import numpy as np
        B, T, C = (4096, 64, 128)
        N_HEAD = 8
        D_HEAD = C // N_HEAD
        Bt, Tt, Ct = x.shape
        qkv = x @ w_attn
        q, k, v = jnp.split(qkv, 3, axis=-1)
        q = q.reshape(Bt, Tt, N_HEAD, D_HEAD)
        k = k.reshape(Bt, Tt, N_HEAD, D_HEAD)
        v = v.reshape(Bt, Tt, N_HEAD, D_HEAD)
        scale = 1.0 / jnp.sqrt(jnp.float32(D_HEAD))
        att = jnp.einsum('bqhd,bkhd->bhqk', q, k) * scale
        causal = jnp.tril(jnp.ones((Tt, Tt), dtype=bool))
        att = jnp.where(causal[None, None, :, :], att, -jnp.inf)
        att = jax.nn.softmax(att, axis=-1)
        out = jnp.einsum('bhqk,bkhd->bqhd', att, v).reshape(Bt, Tt, Ct)
        return out @ w_proj

    def _L1_ffn_ref(x, router_w, router_b, expert_w, expert_b):
        import jax, jax.numpy as jnp
        import numpy as np
        B, N, D, C, E, K = (8, 8192, 128, 128, 8, 2)
        router_probs = jax.nn.softmax(x @ router_w + router_b, axis=-1)
        top_p, top_i = jax.lax.top_k(router_probs, K)
        top_p = top_p / jnp.sum(top_p, axis=-1, keepdims=True)
        expert_out = jnp.einsum('bnd,edc->bnec', x, expert_w) + expert_b
        gathered = jnp.take_along_axis(expert_out, top_i[..., None], axis=2)
        return jnp.einsum('bnk,bnkc->bnc', top_p, gathered)

    def _gn(v, G=32, eps=1e-5):
        B_, H_, W_, C_ = v.shape
        g = v.reshape(B_, H_, W_, G, C_ // G)
        m = jnp.mean(g, axis=(1, 2, 4), keepdims=True)
        s = jnp.var(g, axis=(1, 2, 4), keepdims=True)
        return ((g - m) / jnp.sqrt(s + eps)).reshape(v.shape)

    def _ln_c(v, eps=1e-6):
        m = jnp.mean(v, axis=-1, keepdims=True)
        s = jnp.var(v, axis=-1, keepdims=True)
        return (v - m) / jnp.sqrt(s + eps)

    def _ln_t(v, eps=1e-5):
        m = jnp.mean(v, axis=-1, keepdims=True)
        s = jnp.var(v, axis=-1, keepdims=True)
        return (v - m) / jnp.sqrt(s + eps)

    def _to_tokens(v):
        B_, H_, W_, C_ = v.shape
        return v.reshape(B_, H_ * W_, C_)
    def _from_tokens(t, like):
        return t.reshape(like.shape)

    x = _L0_conv_ref(x, L0_conv_cv1_w, L0_conv_cv1_g, L0_conv_cv1_b, L0_conv_in_proj_w, L0_conv_dw_w, L0_conv_dw_b, L0_conv_x_proj_w, L0_conv_dt_w, L0_conv_dt_b, L0_conv_A_logs, L0_conv_Ds, L0_conv_ln_g, L0_conv_ln_b, L0_conv_out_proj_w, L0_conv_cv2_w, L0_conv_cv2_g, L0_conv_cv2_b, L0_conv_bn0_g, L0_conv_bn0_b, L0_conv_c1_w, L0_conv_c1_b, L0_conv_bn1_g, L0_conv_bn1_b, L0_conv_c2_w, L0_conv_c2_b, L0_conv_bn2_g, L0_conv_bn2_b, L0_conv_c3_w, L0_conv_c3_b, L0_conv_cv_w, L0_conv_cv_g, L0_conv_cv_b, L0_conv_cv3_w, L0_conv_cv3_g, L0_conv_cv3_b)
    t = _to_tokens(x)
    t = t + _L1_attn_ref(_ln_t(t), L1_attn_w_attn, L1_attn_w_proj)
    t = t + _L1_ffn_ref(_ln_t(t), L1_ffn_router_w, L1_ffn_router_b, L1_ffn_expert_w, L1_ffn_expert_b)
    x = _from_tokens(t, x)
    return x


_drawn_inputs = setup_inputs


def setup_inputs(seed=0):
    import zlib

    import numpy as np

    out = dict(_drawn_inputs(seed))
    spreads = {'L0_conv_Ds': (1.0, 0.6),
     'L0_conv_ln_g': (1.0, 0.2),
     'L0_conv_ln_b': (0.0, 0.396),
     'L1_ffn_router_b': (0.0, 0.1),
     'L1_ffn_expert_b': (0.0, 0.1)}
    factors = {'L0_conv_cv1_g': 3.266,
     'L0_conv_cv1_b': 3.286,
     'L0_conv_x_proj_w': 8.0,
     'L0_conv_dt_w': 8.0,
     'L0_conv_dt_b': 8.0,
     'L0_conv_A_logs': 8.0,
     'L0_conv_cv_g': 4.035}
    for name, (base, spread) in spreads.items():
        noise = np.random.default_rng([zlib.crc32(name.encode()), seed]).standard_normal(out[name].shape)
        drawn = base * np.exp(spread * noise) if base else spread * noise
        out[name] = jnp.asarray(drawn.astype(out[name].dtype))
    for name, factor in factors.items():
        out[name] = (out[name] * factor).astype(out[name].dtype)
    return out
```

```python
import numpy as np
from contextlib import ExitStack

import concourse.bass as bass
from concourse import mybir

F32 = mybir.dt.float32
BF16 = mybir.dt.bfloat16
ALU = mybir.AluOpType
ACT = mybir.ActivationFunctionType
AX = mybir.AxisListType
ds = bass.ds

P = 128
IMAGES, SIDE, CH = 4, 64, 128
HALF = CH // 2
TOK = SIDE * SIDE
BANK = 512
PAD = SIDE + 2
ROWS = BANK // SIDE
CHUNKS = TOK // BANK
TILES = TOK // P
TAPS = 9

DIRS, STATES, DT_RANK = 4, 16, 4
STEP = 1024
SCAN_CHUNKS = TOK // STEP
ALL_CHUNKS = IMAGES * DIRS * SCAN_CHUNKS
PARTS = 3

HEADS, HEAD = 8, 16
EXPERTS = 8


class Columns:

    def __init__(self, widths):
        self.at, self.n = {}, 0
        for name, width in widths:
            self.at[name] = (self.n, width)
            self.n += width

    def of(self, tensor, name, rows=P, start=0):
        at, width = self.at[name]
        return tensor[start:rows, at:at + width]


WEIGHTS = Columns([
    ("in1x1", P), ("in_scale", 1), ("in_bias", 1), ("bn0_scale", 1), ("bn0_bias", 1),
    ("xh", P), ("gate", P), ("dw", TAPS * P), ("dw_b", 1),
    ("c1", TAPS * HALF), ("c1_b", 1), ("bn1_g", 1), ("bn1_b", 1),
    ("c2", TAPS * HALF), ("c2_b", 1), ("bn2_g", 1), ("bn2_b", 1),
    ("c3", HALF), ("c3_b", 1),
    ("bc", DIRS * 96), ("xp_dt", DIRS * P), ("dt_w", DIRS * P), ("dt_b", DIRS),
    ("a_logs", DIRS * STATES), ("skip", DIRS),
    ("ln_g", 1), ("ln_b", 1), ("out_proj", P), ("cv", P), ("cv_g", 1), ("cv_b", 1),
    ("cv3", P), ("cv3_g", 1), ("cv3_b", 1),
    ("qkv", 3 * P), ("w_proj", 2 * P),
    ("router", EXPERTS), ("router_b", EXPERTS), ("experts", EXPERTS * P), ("expert_b", EXPERTS * P),
])
CONSTANTS = Columns([
    ("ident", P), ("mean", P), ("part_a", 1), ("part_b", 1), ("row_a", 1), ("row_b", 1),
    ("head_sum", P),
])
CONSTANTS16 = Columns([("select", 2 * STATES * P), ("ident", P), ("above", P), ("below", P), ("ones", P)])
MASKED = -1e30
DERIVED = Columns([
    ("taps", TAPS * P), ("dt", DIRS * P), ("neg_a", DIRS * STATES), ("cv_out", P),
    ("c1_bias", 1), ("c2_bias", 1),
])


def scan_slot(tensor):
    return tensor[:, 0:P], tensor[:, P:P + 96], tensor[:, P + 96:P + 97]


def prepare(nc, weights, constants, constants16, w, c, c16, d, bias16):
    with ExitStack() as ctx:
        sb = lambda name, shape, dt=F32: ctx.enter_context(nc.sbuf_tensor(name, shape, dt))
        sem = lambda name: ctx.enter_context(nc.semaphore(name))
        hi = sb("pre_hi", [P, EXPERTS * P], BF16)
        rest = sb("pre_rest", [P, EXPERTS * P])
        exp_a = sb("pre_exp_a", [P, DIRS * STATES])
        ps = ctx.enter_context(nc.psum_tensor("pre_ps", [P, (DIRS + 1) * BANK], F32))
        loaded, products, exp_done, chain = (sem(f"pre_{n}") for n in ("loaded", "products", "exp", "chain"))
        block = ctx.enter_context(nc.Block())

        @block.sync
        def _(sp):
            sp.dma_start(w[:, :], weights).then_inc(loaded, 16)
            sp.dma_start(c[:, :], constants).then_inc(loaded, 16)
            sp.dma_start(c16[:, :], constants16).then_inc(loaded, 16)
            sp.wait_ge(loaded, 48)

        @block.tensor
        def _(pe):
            pe.wait_ge(loaded, 48)
            xp, dt = WEIGHTS.of(w, "xp_dt"), WEIGHTS.of(w, "dt_w")
            for k in range(DIRS):
                nc.tensor.matmul(ps[:, k * BANK:k * BANK + P], xp[:, k * P:(k + 1) * P],
                                 dt[:, k * P:(k + 1) * P], start=True, stop=True)
            nc.tensor.matmul(ps[:, DIRS * BANK:DIRS * BANK + P], WEIGHTS.of(w, "out_proj"),
                             WEIGHTS.of(w, "cv"), start=True, stop=True).then_inc(products, 1)

        @block.scalar
        def _(act):
            act.wait_ge(loaded, 48)
            nc.scalar.activation(exp_a[:, :], WEIGHTS.of(w, "a_logs"), ACT.Exp).then_inc(exp_done, 1)
            nc.scalar.activation(hi[:, :], WEIGHTS.of(w, "expert_b"), ACT.Copy).then_inc(exp_done, 1)

        @block.vector
        def _(dve):
            dve.wait_ge(loaded, 48)
            for t in range(TAPS):
                nc.vector.tensor_tensor(DERIVED.of(d, "taps")[:, t * P:(t + 1) * P], WEIGHTS.of(w, "xh"),
                                        WEIGHTS.of(w, "dw")[:, t * P:(t + 1) * P], ALU.mult)
            for n in ("1", "2"):
                nc.vector.scalar_tensor_tensor(
                    out=DERIVED.of(d, f"c{n}_bias"), in0=WEIGHTS.of(w, f"c{n}_b"),
                    scalar=WEIGHTS.of(w, f"bn{n}_g"), in1=WEIGHTS.of(w, f"bn{n}_b"),
                    op0=ALU.mult, op1=ALU.add)
            dve.wait_ge(exp_done, 1)
            nc.vector.tensor_scalar(DERIVED.of(d, "neg_a"), exp_a[:, :], -1.0, None, ALU.mult)
            dve.wait_ge(exp_done, 2)
            part_a, part_b = CONSTANTS.of(c, "row_a"), CONSTANTS.of(c, "row_b")
            nc.vector.scalar_tensor_tensor(out=rest[:, :], in0=hi[:, :], scalar=part_a,
                                           in1=WEIGHTS.of(w, "expert_b"), op0=ALU.mult, op1=ALU.add).then_inc(chain, 1)
            dve.wait_ge(chain, 1)
            nc.vector.tensor_copy(hi[:, :], rest[:, :]).then_inc(chain, 1)
            dve.wait_ge(chain, 2)
            nc.vector.scalar_tensor_tensor(out=bias16[:, :], in0=hi[:, :], scalar=part_b, in1=rest[:, :],
                                           op0=ALU.mult, op1=ALU.add)
            dve.wait_ge(products, 1)
            nc.vector.tensor_copy(DERIVED.of(d, "dt").rearrange("p (k n) -> p k n", n=P),
                                  ps[:, 0:DIRS * BANK].rearrange("p (k n) -> p k n", n=BANK)[:, :, 0:P])
            nc.vector.tensor_copy(DERIVED.of(d, "cv_out"), ps[:, DIRS * BANK:DIRS * BANK + P])


X_PARTS = [(slice(t, t + 4), slice(t * P, (t + 4) * P)) for t in range(0, TILES, 4)]
X_COUNT = 16 * len(X_PARTS)


def worked_out(engine, value):
    return value if isinstance(value, int) else engine.to_reg(value)


def conv_front(nc, x, w, c, d, scan_in, gate, left):
    with ExitStack() as ctx:
        sb = lambda name, shape: ctx.enter_context(nc.sbuf_tensor("cf_" + name, shape, F32))
        pb = lambda name: ctx.enter_context(nc.psum_tensor("cf_" + name, [P, BANK], F32))
        sem = lambda name: ctx.enter_context(nc.semaphore("cf_" + name))
        x_tok = sb("x_tok", [P, TILES, CH])
        x_ch = sb("x_ch", [P, TOK])
        act_in = sb("act_in", [P, 2, BANK])
        pad1 = sb("pad1", [P, PAD, PAD])
        pad2 = sb("pad2", [P, PAD, PAD])
        conv2 = sb("conv2", [P, 2, BANK])
        left_sb = sb("left_sb", [P, 2, BANK])
        gate_sb = sb("gate_sb", [P, 2, BANK])
        dirs = [sb(f"dir{k}", [P, TOK]) for k in range(DIRS)]
        ps_tr = [pb(f"ps_tr{i}") for i in range(2)]
        ps_in, ps_xh, ps_gate, ps_c1, ps_c2, ps_c3 = (pb(n) for n in ("ps_in", "ps_xh", "ps_gate", "ps_c1", "ps_c2", "ps_c3"))

        x_loaded, cleared = sem("x_loaded"), sem("cleared")
        transposed, x_copied = sem("transposed"), sem("x_copied")
        in_done, in_silu, padded = sem("in_done"), sem("in_silu"), sem("padded")
        xh_done, xh_silu, gate_done, gate_silu = sem("xh_done"), sem("xh_silu"), sem("gate_done"), sem("gate_silu")
        c1_done, c1_relu, c2_done, c2_relu = sem("c1_done"), sem("c1_relu"), sem("c2_done"), sem("c2_relu")
        c3_done, c3_relu, turned = sem("c3_done"), sem("c3_relu"), sem("turned")
        gate_stored, left_stored = [sem(f"gate_stored{i}") for i in range(2)], [sem(f"left_stored{i}") for i in range(2)]
        dirs_stored = sem("dirs_stored")
        block = ctx.enter_context(nc.Block())

        def window(pad, g, dy, dx):
            return pad[:, g * ROWS + dy:g * ROWS + dy + ROWS, dx:dx + SIDE]

        def inner(pad, g, rows=P):
            return pad[0:rows, g * ROWS + 1:(g + 1) * ROWS + 1, 1:SIDE + 1]

        def rows_of(tile):
            return tile.rearrange("p (r s) -> p r s", s=SIDE)

        @block.sync
        def _(sp):
            def load_x(b):
                for tiles, rows in X_PARTS:
                    sp.dma_start(x_tok[:, tiles, :], x[b, rows].rearrange("(t p) c -> p t c", p=P)).then_inc(x_loaded, 16)

            load_x(0)
            with sp.Fori(0, IMAGES) as b:
                sp.wait_ge(transposed, b * CHUNKS + CHUNKS)
                load_x((b + 1) % IMAGES)
                for g in range(CHUNKS):
                    sp.wait_ge(gate_silu, b * CHUNKS + g + 1)
                    sp.dma_start(gate[b, :, g * BANK:(g + 1) * BANK], gate_sb[:, g % 2, :]).then_inc(gate_stored[g % 2], 16)
                sp.dma_start(scan_in[b, 0], dirs[0][:, :].rearrange("p (c t) -> p c t", t=STEP)).then_inc(dirs_stored, 16)
                for k in range(1, DIRS):
                    sp.wait_ge(turned, b * (DIRS - 1) + k)
                    sp.dma_start(scan_in[b, k], dirs[k][:, :].rearrange("p (c t) -> p c t", t=STEP)).then_inc(dirs_stored, 16)
                for g in range(CHUNKS):
                    sp.wait_ge(c3_relu, b * CHUNKS + g + 1)
                    sp.dma_start(left[b, :, g * BANK:(g + 1) * BANK], left_sb[0:HALF, g % 2, :]).then_inc(left_stored[g % 2], 16)
            sp.wait_ge(x_loaded, X_COUNT * (IMAGES + 1))
            sp.wait_ge(dirs_stored, 16 * IMAGES * DIRS)
            for i in range(2):
                sp.wait_ge(gate_stored[i], 16 * IMAGES * CHUNKS // 2)
                sp.wait_ge(left_stored[i], 16 * IMAGES * CHUNKS // 2)

        @block.gpsimd
        def _(pool):
            nc.gpsimd.memset(pad1[:, :, :], 0.0).then_inc(cleared, 1)
            nc.gpsimd.memset(pad2[:, :, :], 0.0).then_inc(cleared, 1)

        @block.tensor
        def _(pe):
            in1x1, gate_w, c3 = WEIGHTS.of(w, "in1x1"), WEIGHTS.of(w, "gate"), WEIGHTS.of(w, "c3")
            taps, c1, c2 = DERIVED.of(d, "taps"), WEIGHTS.of(w, "c1"), WEIGHTS.of(w, "c2")
            ident = CONSTANTS.of(c, "ident")

            def conv(out, pad, g, stationary, width):
                for t in range(TAPS):
                    last = nc.tensor.matmul(out, stationary[:, t * width:(t + 1) * width],
                                            window(pad, g, t // 3, t % 3), start=(t == 0), stop=(t == TAPS - 1))
                return last

            pe.wait_ge(cleared, 2)
            with pe.Fori(0, IMAGES) as b:
                first = b * CHUNKS
                pe.wait_ge(x_loaded, b * X_COUNT + X_COUNT)
                for g in range(CHUNKS):
                    pe.wait_ge(x_copied, first + max(g - 1, 0))
                    for t in range(BANK // P):
                        last = nc.tensor.transpose(ps_tr[g % 2][:, t * P:(t + 1) * P], x_tok[:, g * (BANK // P) + t, :], ident)
                    last.then_inc(transposed, 1)
                for g in range(CHUNKS):
                    pe.wait_ge(x_copied, first + g + 1)
                    pe.wait_ge(in_silu, first + g)
                    nc.tensor.matmul(ps_in[:, :], in1x1, x_ch[:, g * BANK:(g + 1) * BANK], start=True, stop=True).then_inc(in_done, 1)
                for g in range(CHUNKS):
                    pe.wait_ge(padded, first + min(g + 2, CHUNKS))
                    pe.wait_ge(xh_silu, first + g)
                    conv(ps_xh[:, :], pad1, g, taps, P).then_inc(xh_done, 1)
                    pe.wait_ge(gate_silu, first + g)
                    nc.tensor.matmul(ps_gate[:, :], gate_w, window(pad1, g, 1, 1), start=True, stop=True).then_inc(gate_done, 1)
                    pe.wait_ge(c1_relu, first + g)
                    conv(ps_c1[0:HALF, :], pad1, g, c1, HALF).then_inc(c1_done, 1)
                for g in range(CHUNKS + 1):
                    if g < CHUNKS:
                        pe.wait_ge(c1_relu, first + min(g + 2, CHUNKS))
                        pe.wait_ge(c2_relu, first + g)
                        conv(ps_c2[0:HALF, :], pad2, g, c2, HALF).then_inc(c2_done, 1)
                    if g:
                        pe.wait_ge(cleared, 2)
                        pe.wait_ge(c2_relu, first + g)
                        pe.wait_ge(c3_relu, first + g - 1)
                        nc.tensor.matmul(ps_c3[0:HALF, :], c3[0:HALF, :], conv2[0:HALF, (g - 1) % 2, :],
                                         start=True, stop=True).then_inc(c3_done, 1)

        @block.scalar
        def _(act):
            act.wait_ge(cleared, 2)
            with act.Fori(0, IMAGES) as b:
                first = b * CHUNKS
                for g in range(CHUNKS):
                    act.wait_ge(in_done, first + g + 1)
                    act.wait_ge(padded, first + max(g - 1, 0))
                    nc.scalar.activation(act_in[:, g % 2, :], ps_in[:, :], ACT.Silu, bias=WEIGHTS.of(w, "in_bias"),
                                         scale=WEIGHTS.of(w, "in_scale")).then_inc(in_silu, 1)
                act.wait_ge(dirs_stored, b * DIRS * 16)
                act.wait_ge(c2_done, first)
                for g in range(CHUNKS):
                    act.wait_ge(xh_done, first + g + 1)
                    nc.scalar.activation(dirs[0][:, g * BANK:(g + 1) * BANK], ps_xh[:, :], ACT.Silu,
                                         bias=WEIGHTS.of(w, "dw_b")).then_inc(xh_silu, 1)
                    act.wait_ge(gate_done, first + g + 1)
                    act.wait_ge(gate_stored[g % 2], (b * (CHUNKS // 2) + g // 2) * 16)
                    nc.scalar.activation(gate_sb[:, g % 2, :], ps_gate[:, :], ACT.Silu).then_inc(gate_silu, 1)
                    act.wait_ge(c1_done, first + g + 1)
                    nc.scalar.activation(inner(pad2, g, HALF), rows_of(ps_c1[0:HALF, :]), ACT.Relu,
                                         bias=DERIVED.of(d, "c1_bias", HALF), scale=WEIGHTS.of(w, "bn1_g", HALF)).then_inc(c1_relu, 1)
                for g in range(CHUNKS + 1):
                    if g < CHUNKS:
                        act.wait_ge(c2_done, first + g + 1)
                        act.wait_ge(c3_done, first + max(g - 1, 0))
                        nc.scalar.activation(conv2[0:HALF, g % 2, :], ps_c2[0:HALF, :], ACT.Relu,
                                             bias=DERIVED.of(d, "c2_bias", HALF), scale=WEIGHTS.of(w, "bn2_g", HALF)).then_inc(c2_relu, 1)
                    if g:
                        i = (g - 1) % 2
                        act.wait_ge(c3_done, first + g)
                        act.wait_ge(left_stored[i], (b * (CHUNKS // 2) + (g - 1) // 2) * 16)
                        nc.scalar.activation(left_sb[0:HALF, i, :], ps_c3[0:HALF, :], ACT.Relu,
                                             bias=WEIGHTS.of(w, "c3_b", HALF)).then_inc(c3_relu, 1)

        @block.vector
        def _(dve):
            dve.wait_ge(cleared, 2)
            with dve.Fori(0, IMAGES) as b:
                first = b * CHUNKS
                dve.wait_ge(in_done, first)
                for g in range(CHUNKS):
                    dve.wait_ge(transposed, first + g + 1)
                    nc.vector.tensor_copy(x_ch[:, g * BANK:(g + 1) * BANK], ps_tr[g % 2][:, :]).then_inc(x_copied, 1)
                dve.wait_ge(c1_done, first)
                for g in range(CHUNKS):
                    dve.wait_ge(in_silu, first + g + 1)
                    nc.vector.tensor_scalar(inner(pad1, g), rows_of(act_in[:, g % 2, :]), WEIGHTS.of(w, "bn0_scale"),
                                            WEIGHTS.of(w, "bn0_bias"), ALU.mult, ALU.add).then_inc(padded, 1)
                dve.wait_ge(xh_silu, first + CHUNKS)
                nc.vector.tensor_copy(dirs[1][:, :].rearrange("p (s r) -> p s r", r=SIDE),
                                      dirs[0][:, :].rearrange("p (r s) -> p s r", s=SIDE)).then_inc(turned, 1)
                nc.vector.tensor_copy(dirs[2][:, :], dirs[0][:, ::-1]).then_inc(turned, 1)
                dve.wait_ge(turned, b * (DIRS - 1) + 1)
                nc.vector.tensor_copy(dirs[3][:, :], dirs[1][:, ::-1]).then_inc(turned, 1)


RING = 4


def state_scan(nc, w, c, c16, d, scan_in, scan_out):
    with ExitStack() as ctx:
        sb = lambda name, shape, dt=F32: ctx.enter_context(nc.sbuf_tensor("ss_" + name, shape, dt))
        pb = lambda name: ctx.enter_context(nc.psum_tensor("ss_" + name, [P, STEP], F32))
        sem = lambda name: ctx.enter_context(nc.semaphore("ss_" + name))
        x_in = sb("x_in", [P, 2 * STEP])
        slot = sb("slot", [P, P + 96 + 1])
        mag, pos, small, log1 = (sb(n, [P, STEP]) for n in ("mag", "pos", "small", "log1"))
        one, rest_e = sb("one", [P, STEP]), sb("rest_e", [P, STEP])
        hi, mid, rest = sb("hi", [96, STEP], BF16), sb("mid", [96, STEP], BF16), sb("rest", [96, STEP])
        delta, dx = sb("delta", [P, 2 * STEP]), sb("dx", [P, 2 * STEP])
        bc = sb("bc", [96, 2 * STEP], BF16)
        b_sb, decay, drive = (sb(n, [P, RING, STEP]) for n in ("b_sb", "decay", "drive"))
        h, hc = sb("h", [P, 2, STEP]), sb("hc", [P, 2, STEP])
        carry = sb("carry", [P, 2 * STATES])
        y_sb = sb("y_sb", [P, STEP])
        ps_prep, ps_b, ps_c, ps_y = pb("ps_prep"), pb("ps_b"), pb("ps_c"), pb("ps_y")

        x_loaded, y_stored, start = sem("x_loaded"), sem("y_stored"), sem("start")
        slot_filled, dt_done, dt_read, exp_small, log_done = (sem(n) for n in ("slot_filled", "dt_done", "dt_read", "exp_small", "log_done"))
        bc_done, hi_done, rest_done, mid_done, bc_split = (sem(n) for n in ("bc_done", "hi_done", "rest_done", "mid_done", "bc_split"))
        dve_prep, delta_done, dx_done = sem("dve_prep"), sem("delta_done"), sem("dx_done")
        b_done, b_copied, decayed, driven = (sem(n) for n in ("b_done", "b_copied", "decayed", "driven"))
        scanned, carried, c_done, multiplied, summed, y_done = (sem(n) for n in ("scanned", "carried", "c_done", "multiplied", "summed", "y_done"))
        act_prep = sem("act_prep")
        block = ctx.enter_context(nc.Block())

        slot_dt, slot_bc, slot_bias = scan_slot(slot)
        PREP_DVE = 3

        def direction(q):
            return (q // SCAN_CHUNKS) % DIRS

        def half(q):
            return (q % 2) * STEP

        @block.sync
        def _(sp):
            sp.dma_start(x_in[:, 0:STEP], scan_in[0]).then_inc(x_loaded, 16)
            with sp.Fori(0, ALL_CHUNKS) as j:
                q = j + 1
                sp.wait_ge(x_loaded, j * 16 + 16)
                sp.wait_ge(y_done, j)
                sp.dma_start(x_in[:, ds(half(q), STEP)], scan_in[q % ALL_CHUNKS]).then_inc(x_loaded, 16)
                sp.wait_ge(y_done, j + 1)
                sp.dma_start(scan_out[j], y_sb[:, :]).then_inc(y_stored, 16)
            sp.wait_ge(y_stored, 16 * ALL_CHUNKS)
            sp.wait_ge(x_loaded, 16 * (ALL_CHUNKS + 1))

        @block.tensor
        def _(pe):
            ident = CONSTANTS.of(c, "ident")
            select = CONSTANTS16.of(c16, "select", 96)

            def prep_dt(q):
                pe.wait_ge(slot_filled, q + 1)
                pe.wait_ge(x_loaded, q * 16 + 16)
                pe.wait_ge(rest_done, q)
                for i in range(STEP // BANK):
                    last = nc.tensor.matmul(ps_prep[:, i * BANK:(i + 1) * BANK], slot_dt,
                                            x_in[:, ds(half(q) + i * BANK, BANK)], start=True, stop=True)
                last.then_inc(dt_done, 1)

            def prep_bc(q):
                pe.wait_ge(dt_read, q + 1)
                for i in range(STEP // BANK):
                    last = nc.tensor.matmul(ps_prep[0:96, i * BANK:(i + 1) * BANK], slot_bc,
                                            x_in[:, ds(half(q) + i * BANK, BANK)], start=True, stop=True)
                last.then_inc(bc_done, 1)

            def spread(out, n, q):
                for i in range(STEP // BANK):
                    last = nc.tensor.matmul(out[:, i * BANK:(i + 1) * BANK], select[:, n * P:(n + 1) * P],
                                            bc[:, ds(half(q) + i * BANK, BANK)], start=True, stop=True)
                return last

            prep_dt(0)
            prep_bc(0)
            pe.wait_ge(bc_split, 1)
            for n in range(4):
                if n:
                    pe.wait_ge(b_copied, n)
                spread(ps_b, n, 0).then_inc(b_done, 1)
            spread(ps_c, STATES, 0).then_inc(c_done, 1)
            with pe.Fori(0, ALL_CHUNKS) as j:
                m0 = j * STATES
                for n in range(STATES):
                    pe.wait_ge(multiplied, m0 + n + 1)
                    nn, q = (n + 1) % STATES, j + (n + 1) // STATES
                    spread(ps_c, STATES + nn, q).then_inc(c_done, 1)
                    if n == 0:
                        pe.wait_ge(y_done, j)
                    for i in range(STEP // BANK):
                        last = nc.tensor.matmul(ps_y[:, i * BANK:(i + 1) * BANK], ident,
                                                hc[:, n % 2, i * BANK:(i + 1) * BANK],
                                                start=(n == 0), stop=(n == STATES - 1))
                    last.then_inc(summed, 1)
                    if n == 2:
                        prep_dt(j + 1)
                    if n == 4:
                        prep_bc(j + 1)
                    nn, q = (n + 4) % STATES, j + (n + 4) // STATES
                    if nn == 0:
                        pe.wait_ge(bc_split, j + 2)
                    pe.wait_ge(b_copied, m0 + n + 4)
                    spread(ps_b, nn, q).then_inc(b_done, 1)

        @block.scalar
        def _(act):
            neg_a, dt, bc_w, dt_b = DERIVED.of(d, "neg_a"), DERIVED.of(d, "dt"), WEIGHTS.of(w, "bc"), WEIGHTS.of(w, "dt_b")

            def prep_slot(q):
                k = direction(q)
                act.wait_ge(bc_done, q)
                act.wait_ge(dt_read, q)
                nc.scalar.activation(slot_dt, dt[:, ds(k * P, P)], ACT.Copy)
                nc.scalar.activation(slot_bc, bc_w[:, ds(k * 96, 96)], ACT.Copy)
                nc.scalar.activation(slot_bias, dt_b[:, ds(k, 1)], ACT.Copy).then_inc(slot_filled, 1)

            def prep_softplus(q):
                act.wait_ge(slot_filled, q + 1)
                act.wait_ge(dt_done, q + 1)
                act.wait_ge(dve_prep, q * PREP_DVE)
                act.wait_ge(exp_small, q)
                nc.scalar.activation(mag[:, :], ps_prep[:, :], ACT.Abs, bias=slot_bias).then_inc(act_prep, 1)
                nc.scalar.activation(pos[:, :], ps_prep[:, :], ACT.Relu, bias=slot_bias).then_inc(dt_read, 1)
                act.wait_ge(act_prep, q + 1)
                act.wait_ge(log_done, q)
                nc.scalar.activation(small[:, :], mag[:, :], ACT.Exp, scale=-1.0).then_inc(exp_small, 1)

            def prep_log(q):
                act.wait_ge(exp_small, q + 1)
                nc.scalar.activation(log1[:, :], small[:, :], ACT.Ln, bias=1.0).then_inc(log_done, 1)

            def prep_hi(q):
                act.wait_ge(bc_done, q + 1)
                act.wait_ge(rest_done, q)
                nc.scalar.activation(hi[:, :], ps_prep[0:96, :], ACT.Copy).then_inc(hi_done, 1)

            def prep_mid(q):
                act.wait_ge(rest_done, q + 1)
                act.wait_ge(bc_split, q)
                nc.scalar.activation(mid[:, :], rest[:, :], ACT.Copy).then_inc(mid_done, 1)

            def copy_b(n, m):
                act.wait_ge(b_done, m + 1)
                nc.scalar.activation(b_sb[:, n % RING, :], ps_b[:, :], ACT.Copy).then_inc(b_copied, 1)

            def decays(n, q):
                nc.scalar.activation(decay[:, n % RING, :], delta[:, ds(half(q), STEP)], ACT.Exp,
                                     scale=neg_a[:, ds(direction(q) * STATES + n, 1)]).then_inc(decayed, 1)

            prep_slot(0)
            prep_softplus(0)
            prep_log(0)
            prep_hi(0)
            prep_mid(0)
            for n in range(3):
                copy_b(n, n)
            act.wait_ge(dx_done, 1)
            for n in range(2):
                decays(n, 0)
            with act.Fori(0, ALL_CHUNKS) as j:
                m0 = j * STATES
                for n in range(STATES):
                    act.wait_ge(driven, m0 + n)
                    copy_b((n + 3) % STATES, m0 + n + 3)
                    nn = (n + 2) % STATES
                    if nn == 0:
                        act.wait_ge(dx_done, j + 2)
                    act.wait_ge(scanned, m0 + n)
                    decays(nn, j + (n + 2) // STATES)
                    if n == 0:
                        prep_slot(j + 1)
                    if n == 3:
                        prep_softplus(j + 1)
                    if n == 4:
                        prep_log(j + 1)
                    if n == 6:
                        prep_hi(j + 1)
                    if n == 8:
                        prep_mid(j + 1)

        @block.gpsimd
        def _(pool):
            def drives(n, m, q):
                b_copied_due = worked_out(pool, m + 1)
                pool.wait_ge(start, 1)
                pool.wait_ge(b_copied, b_copied_due)
                nc.gpsimd.tensor_tensor(drive[:, n % RING, :], b_sb[:, n % RING, :], dx[:, ds(half(q), STEP)],
                                        ALU.mult).then_inc(driven, 1)

            nc.gpsimd.memset(carry[:, :], 0.0).then_inc(start, 1)
            pool.wait_ge(start, 1)
            pool.wait_ge(dx_done, 1)
            for n in range(2):
                drives(n, n, 0)
            with pool.Fori(0, ALL_CHUNKS) as j:
                m0 = j * STATES
                for n in range(STATES):
                    nn = (n + 2) % STATES
                    scanned_due = worked_out(pool, m0 + n + 1)
                    pool.wait_ge(start, 1)
                    pool.wait_ge(scanned, scanned_due)
                    nc.gpsimd.tensor_copy(carry[:, STATES + n:STATES + n + 1], h[:, n % 2, STEP - 1:STEP]).then_inc(carried, 1)
                    if nn == 0:
                        pool.wait_ge(dx_done, j + 2)
                    drives(nn, m0 + n + 2, j + (n + 2) // STATES)

        @block.vector
        def _(dve):
            part_a, part_b = CONSTANTS.of(c, "part_a", 96), CONSTANTS.of(c, "part_b", 96)
            skip = WEIGHTS.of(w, "skip")

            def prep_one(q):
                dve.wait_ge(delta_done, q)
                dve.wait_ge(exp_small, q + 1)
                nc.vector.tensor_scalar(one[:, :], small[:, :], 1.0, -1.0, ALU.add, ALU.add).then_inc(dve_prep, 1)
                dve.wait_ge(dve_prep, q * PREP_DVE + 1)
                nc.vector.tensor_tensor(rest_e[:, :], small[:, :], one[:, :], ALU.subtract).then_inc(dve_prep, 1)

            def prep_delta(q, j=None):
                dve.wait_ge(log_done, q + 1)
                dve.wait_ge(dve_prep, q * PREP_DVE + 2)
                nc.vector.tensor_tensor(one[:, :], log1[:, :], pos[:, :], ALU.add).then_inc(dve_prep, 1)
                dve.wait_ge(dx_done, q)
                if j is not None:
                    dve.wait_ge(decayed, j * STATES)
                dve.wait_ge(dve_prep, q * PREP_DVE + 3)
                nc.vector.tensor_tensor(delta[:, ds(half(q), STEP)], one[:, :], rest_e[:, :], ALU.add).then_inc(delta_done, 1)

            def prep_dx(q, j=None):
                if j is not None:
                    dve.wait_ge(driven, j * STATES)
                dve.wait_ge(delta_done, q + 1)
                dve.wait_ge(x_loaded, q * 16 + 16)
                nc.vector.tensor_tensor(dx[:, ds(half(q), STEP)], delta[:, ds(half(q), STEP)], x_in[:, ds(half(q), STEP)],
                                        ALU.mult).then_inc(dx_done, 1)

            def prep_rest(q):
                dve.wait_ge(hi_done, q + 1)
                dve.wait_ge(bc_split, q)
                nc.vector.scalar_tensor_tensor(out=rest[:, :], in0=hi[:, :], scalar=part_a, in1=ps_prep[0:96, :],
                                               op0=ALU.mult, op1=ALU.add).then_inc(rest_done, 1)

            def prep_split(q, j=None):
                if j is not None:
                    dve.wait_ge(c_done, j * STATES)
                dve.wait_ge(mid_done, q + 1)
                nc.vector.scalar_tensor_tensor(out=bc[:, ds(half(q), STEP)], in0=mid[:, :], scalar=part_b, in1=rest[:, :],
                                               op0=ALU.mult, op1=ALU.add).then_inc(bc_split, 1)

            def scan(n, m, q):
                dve.wait_ge(decayed, m + 1)
                dve.wait_ge(driven, m + 1)
                nc.vector.tensor_tensor_scan(h[:, n % 2, :], decay[:, n % RING, :], drive[:, n % RING, :],
                                             initial=carry[:, ds(((q % SCAN_CHUNKS + SCAN_CHUNKS - 1) // SCAN_CHUNKS) * STATES + n, 1)],
                                             op0=ALU.mult, op1=ALU.add).then_inc(scanned, 1)

            prep_one(0)
            prep_delta(0)
            prep_dx(0)
            prep_rest(0)
            prep_split(0)
            dve.wait_ge(start, 1)
            scan(0, 0, 0)
            with dve.Fori(0, ALL_CHUNKS) as j:
                m0 = j * STATES
                for n in range(STATES):
                    dve.wait_ge(scanned, m0 + n + 1)
                    dve.wait_ge(c_done, m0 + n + 1)
                    dve.wait_ge(summed, m0 + max(n - 1, 0))
                    nc.vector.tensor_tensor(hc[:, n % 2, :], h[:, n % 2, :], ps_c[:, :], ALU.mult).then_inc(multiplied, 1)
                    dve.wait_ge(carried, m0 + n)
                    dve.wait_ge(multiplied, m0 + n)
                    scan((n + 1) % STATES, m0 + n + 1, j + (n + 1) // STATES)
                    if n == 4:
                        prep_one(j + 1)
                    if n == 5:
                        prep_delta(j + 1, j)
                    if n == 6:
                        prep_dx(j + 1, j)
                    if n == 7:
                        prep_rest(j + 1)
                    if n == 9:
                        prep_split(j + 1, j)
                dve.wait_ge(summed, m0 + STATES)
                dve.wait_ge(y_stored, j * 16)
                nc.vector.scalar_tensor_tensor(out=y_sb[:, :], in0=x_in[:, ds(half(j), STEP)], scalar=skip[:, ds(direction(j), 1)],
                                               in1=ps_y[:, :], op0=ALU.mult, op1=ALU.add).then_inc(y_done, 1)


LN_EPS_SCAN = 1e-5
LN_EPS = 1e-5
HEAD_SCALE = HEAD ** -0.5
GROUPS = 2
GROUP_HEADS = HEADS // GROUPS
SLOT = P // GROUP_HEADS
BLOCK_TILES = BANK // P


def conv_back(nc, x, w, c, d, scan_out, gate, left, tokens, q_parts, k_parts, values):
    with ExitStack() as ctx:
        sb = lambda name, shape, dt=F32: ctx.enter_context(nc.sbuf_tensor("cb_" + name, shape, dt))
        pb = lambda name: ctx.enter_context(nc.psum_tensor("cb_" + name, [P, BANK], F32))
        sem = lambda name: ctx.enter_context(nc.semaphore("cb_" + name))
        y = [sb(f"y{k}", [P, TOK]) for k in range(DIRS)]
        x_tok, t_tok = sb("x_tok", [P, TILES, CH]), sb("t_tok", [P, TILES, CH])
        centre, square, normed, scaled = (sb(n, [P, 2, BANK]) for n in ("centre", "square", "normed", "scaled"))
        log_var, rstd = sb("log_var", [P, BANK]), sb("rstd", [P, BANK])
        gate_in, both, o_ch = (sb(n, [P, 2, BANK]) for n in ("gate_in", "both", "o_ch"))
        stats, moments = sb("stats", [P, TILES, 6]), sb("moments", [P, TILES, 2])
        t_log, t_rstd = sb("t_log", [P, TILES]), sb("t_rstd", [P, TILES])
        xn_tok = sb("xn_tok", [P, 2, BANK])
        xn_ch = sb("xn_ch", [P, 2, BANK])
        hi, mid, lo = (sb(n, [P, 2, BANK], BF16) for n in ("hi", "mid", "lo"))
        rest = sb("rest", [P, 2, BANK])
        v_sb = sb("v_sb", [P, 2, GROUPS, BLOCK_TILES, GROUP_HEADS, SLOT])
        eps = sb("eps", [P, 1])
        ps_mean, ps_var, ps_xr, ps_out, ps_tok, ps_xn, ps_q, ps_k = (
            pb(n) for n in ("ps_mean", "ps_var", "ps_xr", "ps_out", "ps_tok", "ps_xn", "ps_q", "ps_k"))
        ps_qk, ps_v = (ps_q, ps_k), ps_mean

        names = ("y_loaded x_loaded ready added mean_done centred squared var_done log_done rstd_done norm_done scale_done "
                 "gated xr_done xr_silu out_done out_silu tok_done t_added stats_done moments_done t_log_done t_rstd_done "
                 "xn_done xn_turned xn_copied q_done k_done v_done hi_done rest_done mid_done lo_done v_copied t_stored").split()
        (y_loaded, x_loaded, ready, added, mean_done, centred, squared, var_done, log_done, rstd_done, norm_done, scale_done,
         gated, xr_done, xr_silu, out_done, out_silu, tok_done, t_added, stats_done, moments_done, t_log_done, t_rstd_done,
         xn_done, xn_turned, xn_copied, q_done, k_done, v_done, hi_done, rest_done, mid_done, lo_done, v_copied, t_stored) = map(sem, names)
        gate_loaded, left_loaded, v_stored, qk_stored = ([sem(f"{n}{i}") for i in range(2)] for n in ("gate_loaded", "left_loaded", "v_stored", "qk_stored"))
        block = ctx.enter_context(nc.Block())
        cols = lambda g: slice(g * BANK, (g + 1) * BANK)

        @block.sync
        def _(sp):
            def load_y(b, k):
                sp.dma_start(y[k][:, :].rearrange("p (c t) -> p c t", t=STEP), scan_out[b, k]).then_inc(y_loaded, 16)

            def load_x(b):
                for tiles, rows in X_PARTS:
                    sp.dma_start(x_tok[:, tiles, :], x[b, rows].rearrange("(t p) c -> p t c", p=P)).then_inc(x_loaded, 16)

            for k in range(DIRS):
                load_y(0, k)
            load_x(0)
            with sp.Fori(0, IMAGES) as b:
                first = b * CHUNKS
                for g in range(CHUNKS):
                    sp.wait_ge(gated, first + max(g - 1, 0))
                    sp.dma_start(gate_in[:, g % 2, :], gate[b, :, cols(g)]).then_inc(gate_loaded[g % 2], 16)
                for g in range(CHUNKS):
                    sp.wait_ge(out_done, first + max(g - 1, 0))
                    sp.dma_start(both[0:HALF, g % 2, :], left[b, :, cols(g)]).then_inc(left_loaded[g % 2], 16)
                sp.wait_ge(xr_done, first + CHUNKS)
                for k in range(DIRS):
                    load_y((b + 1) % IMAGES, k)
                sp.wait_ge(t_added, first + CHUNKS)
                load_x((b + 1) % IMAGES)
                sp.dma_start(tokens.rearrange("(b g) p t -> b p g t", g=CHUNKS)[b],
                             t_tok[:, :, :].rearrange("p (g t) c -> p g (t c)", g=CHUNKS)).then_inc(t_stored, 16)
                for g in range(CHUNKS):
                    i = g % 2
                    for s, dram in ((0, q_parts), (1, k_parts)):
                        sp.wait_ge(lo_done, 2 * (first + g) + s + 1)
                        for part, tile in enumerate((hi, mid, lo)):
                            sp.dma_start(dram[b, part, :, cols(g)], tile[:, s, :]).then_inc(qk_stored[s], 16)
                    sp.wait_ge(v_copied, first + g + 1)
                    for r in range(GROUPS):
                        sp.dma_start(values[b, r, :, g * BLOCK_TILES:(g + 1) * BLOCK_TILES, :],
                                     v_sb[:, i, r].rearrange("p t h v -> p t (h v)")).then_inc(v_stored[i], 16)
            sp.wait_ge(y_loaded, 16 * DIRS * (IMAGES + 1))
            sp.wait_ge(x_loaded, X_COUNT * (IMAGES + 1))
            sp.wait_ge(t_stored, 16 * IMAGES)
            for i in range(2):
                sp.wait_ge(qk_stored[i], 16 * PARTS * IMAGES * CHUNKS)
                sp.wait_ge(v_stored[i], 16 * GROUPS * IMAGES * CHUNKS // 2)

        @block.gpsimd
        def _(pool):
            nc.gpsimd.memset(v_sb[:, :, :, :, :, :], 0.0).then_inc(ready, 1)
            pool.wait_ge(ready, 1)
            nc.gpsimd.memset(v_sb[:, :, :, :, :, HEAD:HEAD + 1].rearrange("p a b t h v -> p (a b t h) v"), 1.0).then_inc(ready, 1)
            nc.gpsimd.memset(eps[:, :], LN_EPS_SCAN).then_inc(ready, 1)
            with pool.Fori(0, IMAGES) as b:
                first = b * CHUNKS
                for g in range(CHUNKS):
                    pool.wait_ge(scale_done, first + g + 1)
                    pool.wait_ge(gate_loaded[g % 2], (b * (CHUNKS // 2) + g // 2) * 16 + 16)
                    nc.gpsimd.tensor_tensor(y[2][:, cols(g)], scaled[:, g % 2, :], gate_in[:, g % 2, :], ALU.mult).then_inc(gated, 1)
                for g in range(CHUNKS):
                    for s in range(2):
                        n = 2 * (first + g) + s
                        pool.wait_ge(mid_done, n + 1)
                        pool.wait_ge(qk_stored[s], (first + g) * 16 * PARTS)
                        nc.gpsimd.tensor_tensor(lo[:, s, :], rest[:, s, :], mid[:, s, :], ALU.subtract).then_inc(lo_done, 1)

        @block.tensor
        def _(pe):
            ident, mean = CONSTANTS.of(c, "ident"), CONSTANTS.of(c, "mean")
            cv_out, cv3, qkv = DERIVED.of(d, "cv_out"), WEIGHTS.of(w, "cv3"), WEIGHTS.of(w, "qkv")
            with pe.Fori(0, IMAGES) as b:
                first = b * CHUNKS
                pe.wait_ge(added, (b + 1) * 3)
                pe.wait_ge(v_copied, first)
                for g in range(CHUNKS + 1):
                    if g < CHUNKS:
                        pe.wait_ge(centred, first + g)
                        nc.tensor.matmul(ps_mean[:, :], mean, y[0][:, cols(g)], start=True, stop=True).then_inc(mean_done, 1)
                    if g:
                        pe.wait_ge(squared, first + g)
                        pe.wait_ge(log_done, first + g - 1)
                        nc.tensor.matmul(ps_var[:, :], mean, square[:, (g - 1) % 2, :], start=True, stop=True).then_inc(var_done, 1)
                for g in range(CHUNKS + 2):
                    if g < CHUNKS:
                        pe.wait_ge(gated, first + g + 1)
                        pe.wait_ge(xr_silu, first + g)
                        nc.tensor.matmul(ps_xr[:, :], cv_out, y[2][:, cols(g)], start=True, stop=True).then_inc(xr_done, 1)
                    if 0 < g < CHUNKS + 1:
                        h = g - 1
                        pe.wait_ge(xr_silu, first + h + 1)
                        pe.wait_ge(left_loaded[h % 2], (b * (CHUNKS // 2) + h // 2) * 16 + 16)
                        pe.wait_ge(out_silu, first + h)
                        nc.tensor.matmul(ps_out[:, :], cv3, both[:, h % 2, :], start=True, stop=True).then_inc(out_done, 1)
                    if g > 1:
                        h = g - 2
                        pe.wait_ge(out_silu, first + h + 1)
                        pe.wait_ge(t_added, first + h)
                        for t in range(BLOCK_TILES):
                            last = nc.tensor.transpose(ps_tok[:, t * P:(t + 1) * P], o_ch[:, h % 2, t * P:(t + 1) * P], ident)
                        last.then_inc(tok_done, 1)
                for g in range(CHUNKS + 1):
                    if g < CHUNKS:
                        pe.wait_ge(xn_done, first + g + 1)
                        pe.wait_ge(xn_copied, first + g)
                        for t in range(BLOCK_TILES):
                            last = nc.tensor.transpose(ps_xn[:, t * P:(t + 1) * P], xn_tok[:, g % 2, t * P:(t + 1) * P], ident)
                        last.then_inc(xn_turned, 1)
                    if g:
                        h = g - 1
                        pe.wait_ge(xn_copied, first + h + 1)
                        for s, done in ((0, q_done), (1, k_done)):
                            pe.wait_ge(rest_done, 2 * (first + h) - 1 + s if h else 2 * first)
                            nc.tensor.matmul(ps_qk[s][:, :], qkv[:, s * P:(s + 1) * P], xn_ch[:, h % 2, :], start=True, stop=True).then_inc(done, 1)
                        pe.wait_ge(v_copied, first + h)
                        for t in range(BLOCK_TILES):
                            last = nc.tensor.matmul(ps_v[:, t * P:(t + 1) * P], xn_ch[:, h % 2, t * P:(t + 1) * P],
                                                    qkv[:, 2 * P:3 * P], start=True, stop=True)
                        last.then_inc(v_done, 1)

        @block.scalar
        def _(act):
            act.wait_ge(ready, 3)
            with act.Fori(0, IMAGES) as b:
                first = b * CHUNKS
                for g in range(CHUNKS + 1):
                    if g < CHUNKS:
                        act.wait_ge(centred, first + g + 1)
                        act.wait_ge(var_done, first + max(g - 1, 0))
                        nc.scalar.activation(square[:, g % 2, :], centre[:, g % 2, :], ACT.Square).then_inc(squared, 1)
                    if g:
                        h = g - 1
                        act.wait_ge(var_done, first + h + 1)
                        act.wait_ge(rstd_done, first + h)
                        nc.scalar.activation(log_var[:, :], ps_var[:, :], ACT.Ln, bias=eps[:, :]).then_inc(log_done, 1)
                        act.wait_ge(log_done, first + h + 1)
                        act.wait_ge(norm_done, first + h)
                        nc.scalar.activation(rstd[:, :], log_var[:, :], ACT.Exp, scale=-0.5).then_inc(rstd_done, 1)
                        act.wait_ge(norm_done, first + h + 1)
                        act.wait_ge(gated, first + max(h - 1, 0))
                        nc.scalar.activation(scaled[:, h % 2, :], normed[:, h % 2, :], ACT.Identity, bias=WEIGHTS.of(w, "ln_b"),
                                             scale=WEIGHTS.of(w, "ln_g")).then_inc(scale_done, 1)
                for g in range(CHUNKS + 1):
                    if g < CHUNKS:
                        act.wait_ge(xr_done, first + g + 1)
                        act.wait_ge(out_done, first + max(g - 1, 0))
                        nc.scalar.activation(both[HALF:P, g % 2, :], ps_xr[HALF:P, :], ACT.Silu, bias=WEIGHTS.of(w, "cv_b", start=HALF),
                                             scale=WEIGHTS.of(w, "cv_g", start=HALF)).then_inc(xr_silu, 1)
                    if g:
                        h = g - 1
                        act.wait_ge(out_done, first + h + 1)
                        act.wait_ge(tok_done, first + max(h - 1, 0))
                        nc.scalar.activation(o_ch[:, h % 2, :], ps_out[:, :], ACT.Silu, bias=WEIGHTS.of(w, "cv3_b"),
                                             scale=WEIGHTS.of(w, "cv3_g")).then_inc(out_silu, 1)
                act.wait_ge(moments_done, (b + 1) * TILES)
                act.wait_ge(t_rstd_done, b)
                nc.scalar.activation(t_log[:, :], moments[:, :, 1], ACT.Ln, bias=eps[:, :]).then_inc(t_log_done, 1)
                act.wait_ge(t_log_done, b + 1)
                act.wait_ge(xn_done, first)
                nc.scalar.activation(t_rstd[:, :], t_log[:, :], ACT.Exp, scale=-0.5).then_inc(t_rstd_done, 1)
                for g in range(CHUNKS):
                    act.wait_ge(xn_turned, first + g + 1)
                    act.wait_ge(v_done, first + max(g - 1, 0))
                    nc.scalar.activation(xn_ch[:, g % 2, :], ps_xn[:, :], ACT.Copy).then_inc(xn_copied, 1)
                    for s, done in ((0, q_done), (1, k_done)):
                        n = 2 * (first + g) + s
                        act.wait_ge(done, first + g + 1)
                        act.wait_ge(qk_stored[s], (first + g) * 16 * PARTS)
                        nc.scalar.activation(hi[:, s, :], ps_qk[s][:, :], ACT.Copy, scale=HEAD_SCALE if s == 0 else 1.0).then_inc(hi_done, 1)
                    for s in range(2):
                        n = 2 * (first + g) + s
                        act.wait_ge(rest_done, n + 1)
                        nc.scalar.activation(mid[:, s, :], rest[:, s, :], ACT.Copy).then_inc(mid_done, 1)
                    act.wait_ge(v_done, first + g + 1)
                    act.wait_ge(v_stored[g % 2], (b * (CHUNKS // 2) + g // 2) * 16 * GROUPS)
                    for r in range(GROUPS):
                        last = nc.scalar.activation(
                            v_sb[:, g % 2, r, :, :, 0:HEAD],
                            ps_v[:, :].rearrange("p (t r h v) -> p r t h v", r=GROUPS, h=GROUP_HEADS, v=HEAD)[:, r], ACT.Copy)
                    last.then_inc(v_copied, 1)

        @block.vector
        def _(dve):
            dve.wait_ge(ready, 3)
            with dve.Fori(0, IMAGES) as b:
                first = b * CHUNKS
                dve.wait_ge(y_loaded, b * 16 * DIRS + 16 * DIRS)
                nc.vector.tensor_tensor(y[0][:, :], y[0][:, :], y[2][:, ::-1], ALU.add).then_inc(added, 1)
                nc.vector.tensor_tensor(y[1][:, :], y[1][:, :], y[3][:, ::-1], ALU.add).then_inc(added, 1)
                dve.wait_ge(added, b * 3 + 2)
                rows = y[0][:, :].rearrange("p (r s) -> p r s", s=SIDE)
                nc.vector.tensor_tensor(rows, rows, y[1][:, :].rearrange("p (s r) -> p r s", r=SIDE), ALU.add).then_inc(added, 1)
                for g in range(CHUNKS + 1):
                    if g < CHUNKS:
                        dve.wait_ge(mean_done, first + g + 1)
                        dve.wait_ge(squared, first + max(g - 1, 0))
                        dve.wait_ge(norm_done, first + max(g - 1, 0))
                        nc.vector.tensor_tensor(centre[:, g % 2, :], y[0][:, cols(g)], ps_mean[:, :], ALU.subtract).then_inc(centred, 1)
                    if g:
                        h = g - 1
                        dve.wait_ge(rstd_done, first + h + 1)
                        dve.wait_ge(scale_done, first + max(h - 1, 0))
                        nc.vector.tensor_tensor(normed[:, h % 2, :], centre[:, h % 2, :], rstd[:, :], ALU.mult).then_inc(norm_done, 1)
                dve.wait_ge(x_loaded, b * X_COUNT + X_COUNT)
                dve.wait_ge(t_stored, b * 16)
                dve.wait_ge(xn_done, first)
                for g in range(CHUNKS):
                    tiles = slice(g * BLOCK_TILES, (g + 1) * BLOCK_TILES)
                    dve.wait_ge(tok_done, first + g + 1)
                    nc.vector.tensor_tensor(t_tok[:, tiles, :], x_tok[:, tiles, :], ps_tok[:, :].rearrange("p (t c) -> p t c", c=CH),
                                            ALU.add).then_inc(t_added, 1)
                    dve.wait_ge(t_added, first + g + 1)
                    dve.wait_ge(t_log_done, b)
                    for t in range(g * BLOCK_TILES, (g + 1) * BLOCK_TILES):
                        nc.vector.bn_stats(stats[:, t, :], t_tok[:, t, :]).then_inc(stats_done, 1)
                    stats_done_due = worked_out(dve, b * TILES + (g + 1) * BLOCK_TILES)
                    dve.wait_ge(ready, 3)
                    dve.wait_ge(stats_done, stats_done_due)
                    for t in range(g * BLOCK_TILES, (g + 1) * BLOCK_TILES):
                        nc.vector.bn_aggr(moments[:, t, :], stats[:, t, :]).then_inc(moments_done, 1)
                dve.wait_ge(moments_done, (b + 1) * TILES)
                dve.wait_ge(t_rstd_done, b + 1)
                for g in range(CHUNKS + 1):
                    if g < CHUNKS:
                        dve.wait_ge(xn_turned, first + max(g - 1, 0))
                        for t in range(BLOCK_TILES):
                            n = g * BLOCK_TILES + t
                            last = nc.vector.tensor_scalar(xn_tok[:, g % 2, t * P:(t + 1) * P], t_tok[:, n, :], moments[:, n, 0:1],
                                                           t_rstd[:, n:n + 1], ALU.subtract, ALU.mult)
                        last.then_inc(xn_done, 1)
                    if g:
                        h = g - 1
                        for s in range(2):
                            n = 2 * (first + h) + s
                            dve.wait_ge(hi_done, n + 1)
                            dve.wait_ge(lo_done, n - 1 if h or s else 2 * first)
                            nc.vector.scalar_tensor_tensor(out=rest[:, s, :], in0=ps_qk[s][:, :], scalar=HEAD_SCALE if s == 0 else 1.0,
                                                           in1=hi[:, s, :], op0=ALU.mult, op1=ALU.subtract).then_inc(rest_done, 1)


Q_PARTS, K_PARTS = (0, 0, 1, 0, 1, 2), (0, 1, 0, 2, 1, 0)
SCORE_ROWS = HEAD * len(Q_PARTS)
ROWS_MAX = SCORE_ROWS + PARTS
UNITS = IMAGES * GROUPS
QBLOCKS = TOK // BANK
STEPS = [BLOCK_TILES * i * (i + 1) // 2 for i in range(QBLOCKS + 1)]
TOP = GROUP_HEADS * BLOCK_TILES
Q_SLOTS = 4


def attention(nc, c, c16, q_parts, k_parts, values, maxima, attended):
    with ExitStack() as ctx:
        sb = lambda name, shape, dt=F32: ctx.enter_context(nc.sbuf_tensor("at_" + name, shape, dt))
        pb = lambda name, n=BANK: ctx.enter_context(nc.psum_tensor("at_" + name, [P, n], F32))
        sem = lambda name: ctx.enter_context(nc.semaphore("at_" + name))
        k_sb = sb("k_sb", [ROWS_MAX, 2 * GROUP_HEADS * TOK], BF16)
        q_sb = sb("q_sb", [ROWS_MAX, Q_SLOTS, GROUP_HEADS, BANK], BF16)
        v_sb = sb("v_sb", [P, 2 * TILES * P])
        v_now = sb("v_now", [P, BLOCK_TILES, P])
        weights = sb("weights", [P, 2, 2, 2, BANK])
        top, neg = sb("top", [P, TOP, QBLOCKS]), sb("neg", [P, TOP])
        m_rest, m_row = sb("m_rest", [TOP, P]), sb("m_row", [TOP, PARTS, P], BF16)
        o_sb, inverse, o_out = sb("o_sb", [P, BANK]), sb("inverse", [P, BANK]), sb("o_out", [P, BANK])
        ps_s = [pb(f"ps_s{i}", 2 * BANK) for i in range(2)]
        ps_m = [pb(f"ps_m{i}") for i in range(2)]
        ps_o, ps_x = pb("ps_o"), pb("ps_x")
        names = ("ones k_loaded q_loaded v_loaded v_copied scored weighed summed max_scored maxed negated turned "
                 "m_hi_done m_rest_done m_mid_done m_lo_done m_stored m_loaded o_copied sums_done inverted scaled o_stored").split()
        (ones, k_loaded, q_loaded, v_loaded, v_copied, scored, weighed, summed, max_scored, maxed, negated, turned,
         m_hi_done, m_rest_done, m_mid_done, m_lo_done, m_stored, m_loaded, o_copied, sums_done, inverted, scaled, o_stored) = map(sem, names)
        block = ctx.enter_context(nc.Block())

        def step(u, i, kk, t):
            return u * STEPS[-1] + (STEPS[i] + t) + kk * BLOCK_TILES

        def chunk(u, i, kk, n):
            return u * (TOP * QBLOCKS * (QBLOCKS + 1) // 2) + (TOP * i * (i + 1) // 2 + n) + kk * TOP

        def at_least(engine, semaphore, value):
            if not isinstance(value, int) or value > 0:
                engine.wait_ge(semaphore, value)

        def block_of(u, i):
            return u * QBLOCKS + i

        def following(u, i):
            return (u, i + 1) if i + 1 < QBLOCKS else (u + 1, 0)

        def first_pass(i):
            reg, diag = [(i, n) for n in range(TOP)] if i + 1 < QBLOCKS else [], [(None, n) for n in range(TOP)]
            todo = reg + diag
            shares = [len(todo) * f // 16 for f in (7, 13, 16, 16)]
            return [todo[a:b] for a, b in zip([0] + shares, shares)]

        EVEN = [[(None, n) for n in range(TOP * t // BLOCK_TILES, TOP * (t + 1) // BLOCK_TILES)] for t in range(BLOCK_TILES)]

        @block.sync
        def _(sp):
            def load_k(u, v):
                half = (v % 2) * (GROUP_HEADS * TOK)
                source = k_parts.rearrange("b s (r h d) t -> b r s d h t", r=GROUPS, h=GROUP_HEADS)[u // GROUPS, u % GROUPS]
                for g, part in enumerate(K_PARTS):
                    sp.dma_start(k_sb[g * HEAD:(g + 1) * HEAD, ds(half, GROUP_HEADS * TOK)].rearrange("d (h t) -> d h t", t=TOK),
                                 source[part]).then_inc(k_loaded, 16)
                sp.dma_start(v_sb[:, ds((v % 2) * (TILES * P), TILES * P)],
                             values.rearrange("b r p t v -> b r p (t v)")[u // GROUPS, u % GROUPS]).then_inc(v_loaded, 16)

            def load_q(u, i):
                source = q_parts.rearrange("b s (r h d) t -> b r s d h t", r=GROUPS, h=GROUP_HEADS)[u // GROUPS, u % GROUPS]
                for g, part in enumerate(Q_PARTS):
                    sp.dma_start(q_sb[g * HEAD:(g + 1) * HEAD, i % Q_SLOTS], source[part, :, :, i * BANK:(i + 1) * BANK]).then_inc(q_loaded, 16)

            def move_maxima(u, i):
                sp.wait_ge(m_lo_done, block_of(u, i) + 1)
                sp.dma_start(maxima, m_row[:, :, :]).then_inc(m_stored, 16)
                sp.wait_ge(m_stored, block_of(u, i) * 16 + 16)
                sp.dma_start(q_sb[SCORE_ROWS:ROWS_MAX, i % Q_SLOTS].rearrange("s h (t q) -> s (h t) q", q=P),
                             maxima.rearrange("n s q -> s n q")).then_inc(m_loaded, 16)

            load_q(0, 0)
            load_k(0, 0)
            sp.wait_ge(q_loaded, 16 * len(Q_PARTS))
            load_q(0, 1)
            move_maxima(0, 0)
            with sp.Fori(0, UNITS) as u:
                for i in range(QBLOCKS):
                    n = block_of(u, i)
                    q_loaded_due, summed_due = worked_out(sp, (n + 2) * (16 * len(Q_PARTS))), worked_out(sp, step(u, i, 0, 0))
                    sp.wait_ge(v_loaded, 16)
                    sp.wait_ge(q_loaded, q_loaded_due)
                    at_least(sp, summed, summed_due)
                    ahead = (u, i + 2) if i + 2 < QBLOCKS else ((u + 1) % UNITS, i + 2 - QBLOCKS)
                    load_q(*ahead)
                    if i == 1:
                        sp.wait_ge(k_loaded, (u + 1) * (16 * len(K_PARTS)))
                        sp.wait_ge(v_loaded, u * 16 + 16)
                        load_k((u + 1) % UNITS, u + 1)
                    v, j = following(u, i)
                    move_maxima(v, j)
                    sp.wait_ge(scaled, n + 1)
                    sp.dma_start(attended[u % GROUPS, (u // GROUPS) * QBLOCKS + i], o_out[:, :]).then_inc(o_stored, 16)
            sp.wait_ge(o_stored, 16 * UNITS * QBLOCKS)
            sp.wait_ge(m_loaded, 16 * (UNITS * QBLOCKS + 1))
            sp.wait_ge(q_loaded, 16 * len(Q_PARTS) * (UNITS * QBLOCKS + 2))
            sp.wait_ge(k_loaded, 16 * len(K_PARTS) * (UNITS + 1))
            sp.wait_ge(v_loaded, 16 * (UNITS + 1))

        @block.tensor
        def _(pe):
            ident, head_sum = CONSTANTS.of(c, "ident"), CONSTANTS.of(c, "head_sum")
            ident16, above, below = (CONSTANTS16.of(c16, n) for n in ("ident", "above", "below"))

            def max_scores(u, i, kk, n):
                h, t = n // BLOCK_TILES, n % BLOCK_TILES
                diag = kk is None
                kk = i if diag else kk
                m = chunk(u, i, kk, n)
                width = (t + 1) * P if diag else BANK
                at_least(pe, maxed, m - 1)
                out = ps_m[n % 2]
                last = nc.tensor.matmul(out[:, 0:width], q_sb[0:SCORE_ROWS, i % Q_SLOTS, h, t * P:(t + 1) * P],
                                        k_sb[0:SCORE_ROWS, ds((u % 2) * (GROUP_HEADS * TOK) + h * TOK + kk * BANK, width)],
                                        start=True, stop=not diag)
                if diag:
                    last = nc.tensor.matmul(out[:, width - P:width], ident16, below, start=False, stop=True)
                last.then_inc(max_scored, 1)

            def scores(u, i, kk, t, diag):
                s = step(u, i, kk, t)
                off = t * P if diag else 0
                for p in range(2):
                    if isinstance(kk, int) and kk == 0 and t == 0:
                        at_least(pe, weighed, s * 2)
                    else:
                        pe.wait_ge(weighed, s * 2 - 1 + p)
                    for h in (2 * p, 2 * p + 1):
                        out = ps_s[p][:, (h % 2) * BANK + off:(h % 2 + 1) * BANK]
                        last = nc.tensor.matmul(out, k_sb[:, ds((u % 2) * (GROUP_HEADS * TOK) + h * TOK + kk * BANK + t * P, P)],
                                                q_sb[:, i % Q_SLOTS, h, off:BANK], start=True, stop=not diag)
                        if diag:
                            last = nc.tensor.matmul(out[:, 0:P], ident16, above, start=False, stop=True)
                    last.then_inc(scored, 1)

            def weighted_sum(u, i, kk, t, diag):
                s = step(u, i, kk, t)
                off = t * P if diag else 0
                pe.wait_ge(weighed, s * 2 + 2)
                pe.wait_ge(v_copied, s + 1)
                begin = isinstance(kk, int) and kk == 0 and t == 0
                if begin:
                    at_least(pe, o_copied, block_of(u, i))
                for h in range(GROUP_HEADS):
                    last = nc.tensor.matmul(ps_o[h * SLOT:(h + 1) * SLOT, off:BANK], v_now[:, t, h * SLOT:(h + 1) * SLOT],
                                            weights[:, t % 2, h // 2, h % 2, off:BANK], start=begin, stop=(diag and t == BLOCK_TILES - 1),
                                            skip_group_check=True)
                last.then_inc(summed, 1)

            def turn_maxima(u, i):
                n = block_of(u, i)
                pe.wait_ge(negated, n + 1)
                if not (isinstance(n, int) and n == 0):
                    pe.wait_ge(inverted, n - 1)
                nc.tensor.transpose(ps_x[0:TOP, 0:P], neg[:, :], ident).then_inc(turned, 1)

            def head_sums(u, i):
                n = block_of(u, i)
                pe.wait_ge(o_copied, n + 1)
                pe.wait_ge(m_rest_done, n + 2)
                nc.tensor.matmul(ps_x[:, :], head_sum, o_sb[:, :], start=True, stop=True).then_inc(sums_done, 1)

            pe.wait_ge(q_loaded, 16 * len(Q_PARTS))
            pe.wait_ge(k_loaded, 16 * len(K_PARTS))
            pe.wait_ge(ones, 2)
            for n in range(TOP):
                max_scores(0, 0, None, n)
            turn_maxima(0, 0)
            with pe.Fori(0, UNITS) as u:
                for i in range(QBLOCKS):
                    v, j = following(u, i)
                    nc.cur_bb.disable_value_cache()
                    pe.wait_ge(m_loaded, block_of(u, i) * 16 + 16)
                    pe.wait_ge(q_loaded, (block_of(v, j) + 1) * (16 * len(Q_PARTS)))
                    pe.wait_ge(v_loaded, u * 16 + 16)
                    if j == 0:
                        pe.wait_ge(k_loaded, (u + 2) * (16 * len(K_PARTS)))

                    def group(kk, then):
                        for t in range(BLOCK_TILES):
                            share = EVEN[t] if j else []
                            for _, n in share[0:2]:
                                max_scores(v, j, kk, n)
                            if t + 1 < BLOCK_TILES:
                                scores(u, i, kk, t + 1, False)
                            else:
                                scores(u, i, kk + 1, 0, then)
                            for _, n in share[2:3]:
                                max_scores(v, j, kk, n)
                            weighted_sum(u, i, kk, t, False)
                            for _, n in share[3:4]:
                                max_scores(v, j, kk, n)

                    scores(u, i, 0, 0, i == 0)
                    if i > 1:
                        group(0, False)
                        if i > 2:
                            with pe.Fori(1, i - 1) as kk:
                                nc.cur_bb.disable_value_cache()
                                group(kk, False)
                            nc.cur_bb.disable_value_cache()
                    if i:
                        group(i - 1, True)
                    for t, share in enumerate(first_pass(i)):
                        half = len(share) // 2
                        for kk, n in share[:half]:
                            max_scores(v, j, kk, n)
                        if t + 1 < BLOCK_TILES:
                            scores(u, i, i, t + 1, True)
                        for kk, n in share[half:]:
                            max_scores(v, j, kk, n)
                        if t + 1 == BLOCK_TILES:
                            turn_maxima(v, j)
                        weighted_sum(u, i, i, t, True)
                    head_sums(u, i)

        @block.scalar
        def _(act):
            def weigh(u, i, kk, t, diag):
                s = step(u, i, kk, t)
                off = t * P if diag else 0
                if i == 0:
                    at_least(act, summed, step(u, i, 0, 0) if t == 0 else s - 1)
                else:
                    act.wait_ge(summed, s - 1)
                for p in range(2):
                    act.wait_ge(scored, s * 2 + p + 1)
                    nc.scalar.activation(weights[:, t % 2, p, :, off:BANK], ps_s[p][:, :].rearrange("p (h q) -> p h q", q=BANK)[:, :, off:BANK],
                                         ACT.Exp).then_inc(weighed, 1)

            def split_maxima(u, i):
                n = block_of(u, i)
                act.wait_ge(turned, n + 1)
                at_least(act, m_stored, n * 16)
                nc.scalar.activation(m_row[:, 0, :], ps_x[0:TOP, 0:P], ACT.Copy).then_inc(m_hi_done, 1)
                act.wait_ge(m_rest_done, n + 1)
                nc.scalar.activation(m_row[:, 1, :], m_rest[:, :], ACT.Copy).then_inc(m_mid_done, 1)

            split_maxima(0, 0)
            with act.Fori(0, UNITS) as u:
                for i in range(QBLOCKS):
                    if i > 2:
                        with act.Fori(0, i) as kk:
                            for t in range(BLOCK_TILES):
                                weigh(u, i, kk, t, False)
                    else:
                        for kk in range(i):
                            for t in range(BLOCK_TILES):
                                weigh(u, i, kk, t, False)
                    for t in range(BLOCK_TILES):
                        weigh(u, i, i, t, True)
                    split_maxima(*following(u, i))
                    act.wait_ge(summed, step(u, i, i, BLOCK_TILES))
                    at_least(act, scaled, block_of(u, i))
                    act.wait_ge(sums_done, block_of(u, i))
                    nc.scalar.activation(o_sb[:, :], ps_o[:, :], ACT.Copy).then_inc(o_copied, 1)

        @block.gpsimd
        def _(pool):
            half = GROUP_HEADS * TOK
            nc.gpsimd.memset(k_sb[SCORE_ROWS:ROWS_MAX, 0:half], 1.0).then_inc(ones, 1)
            pool.wait_ge(ones, 1)
            nc.gpsimd.memset(k_sb[SCORE_ROWS:ROWS_MAX, half:2 * half], 1.0).then_inc(ones, 1)
            pool.wait_ge(ones, 2)

            def copy_v(u, i, kk, t):
                s = step(u, i, kk, t)
                summed_due = worked_out(pool, step(u, i, 0, 0) if i == 0 else s - 3)
                pool.wait_ge(ones, 2)
                at_least(pool, summed, summed_due)
                nc.gpsimd.tensor_copy(v_now[:, t, :], v_sb[:, ds((u % 2) * (TILES * P) + (kk * BLOCK_TILES + t) * P, P)]).then_inc(v_copied, 1)

            with pool.Fori(0, UNITS) as u:
                pool.wait_ge(v_loaded, u * 16 + 16)
                for i in range(QBLOCKS):
                    if i > 2:
                        with pool.Fori(0, i + 1) as kk:
                            for t in range(BLOCK_TILES):
                                copy_v(u, i, kk, t)
                    else:
                        for kk in range(i + 1):
                            for t in range(BLOCK_TILES):
                                copy_v(u, i, kk, t)
                    pool.wait_ge(inverted, block_of(u, i) + 1)
                    at_least(pool, o_stored, block_of(u, i) * 16)
                    nc.gpsimd.tensor_tensor(o_out[:, :], o_sb[:, :], inverse[:, :], ALU.mult).then_inc(scaled, 1)

        @block.vector
        def _(dve):
            def maximum(u, i, kk, n):
                t = n % BLOCK_TILES
                width = (t + 1) * P if kk is None else BANK
                kk = i if kk is None else kk
                dve.wait_ge(max_scored, chunk(u, i, kk, n) + 1)
                nc.vector.reduce_max(top[:, n, ds(kk, 1)], ps_m[n % 2][:, 0:width], AX.X).then_inc(maxed, 1)

            def negate_maxima(u, i):
                n = block_of(u, i)
                dve.wait_ge(maxed, chunk(u, i, i, TOP))
                at_least(dve, turned, n)
                nc.vector.tensor_reduce(neg[:, :], top[:, :, 0:i + 1], AX.X, ALU.max, negate=True).then_inc(negated, 1)

            def split_maxima(u, i):
                n = block_of(u, i)
                dve.wait_ge(m_hi_done, n + 1)
                at_least(dve, m_lo_done, n)
                nc.vector.tensor_tensor(m_rest[:, :], ps_x[0:TOP, 0:P], m_row[:, 0, :], ALU.subtract).then_inc(m_rest_done, 1)
                dve.wait_ge(m_mid_done, n + 1)
                nc.vector.tensor_tensor(m_row[:, 2, :], m_rest[:, :], m_row[:, 1, :], ALU.subtract).then_inc(m_lo_done, 1)

            for n in range(TOP):
                maximum(0, 0, None, n)
            negate_maxima(0, 0)
            split_maxima(0, 0)
            with dve.Fori(0, UNITS) as u:
                for i in range(QBLOCKS):
                    v, j = following(u, i)
                    dve.wait_ge(m_hi_done, 1)
                    dve.wait_ge(negated, block_of(v, j))
                    if j:
                        if i > 1:
                            with dve.Fori(0, i) as kk:
                                for n in range(TOP):
                                    maximum(v, j, kk, n)
                        else:
                            for kk in range(i):
                                for n in range(TOP):
                                    maximum(v, j, kk, n)
                        for n in range(TOP):
                            maximum(v, j, i, n)
                    for n in range(TOP):
                        maximum(v, j, None, n)
                    negate_maxima(v, j)
                    split_maxima(v, j)
                    dve.wait_ge(sums_done, block_of(u, i) + 1)
                    at_least(dve, scaled, block_of(u, i))
                    nc.vector.reciprocal(inverse[:, :], ps_x[:, :]).then_inc(inverted, 1)


ALL_BLOCKS = IMAGES * CHUNKS


def experts(nc, w, c, c16, bias16, attended, tokens, out):
    with ExitStack() as ctx:
        sb = lambda name, shape, dt=F32: ctx.enter_context(nc.sbuf_tensor("ex_" + name, shape, dt))
        pb = lambda name, n=BANK: ctx.enter_context(nc.psum_tensor("ex_" + name, [P, n], F32))
        sem = lambda name: ctx.enter_context(nc.semaphore("ex_" + name))
        att, tok = sb("att", [P, 2, GROUPS, BANK]), sb("tok", [P, 2, BANK])
        t_sb, xn_tok, xn_ch = sb("t_sb", [P, 2, BANK]), sb("xn_tok", [P, BANK]), sb("xn_ch", [P, 2, BANK])
        stats, moments = sb("stats", [P, BLOCK_TILES, 6]), sb("moments", [P, BLOCK_TILES, 2])
        log_var, rstd, eps = sb("log_var", [P, BLOCK_TILES]), sb("rstd", [P, BLOCK_TILES]), sb("eps", [P, 1])
        tile_by = lambda name, n, dt=F32: sb(name, [P, BLOCK_TILES, n], dt)
        logits, best, index = tile_by("logits", EXPERTS), tile_by("best", 8), tile_by("index", 8, mybir.dt.uint32)
        index_f, order = tile_by("index_f", 8), sb("order", [P, EXPERTS])
        order_i = sb("order_i", [P, EXPERTS], mybir.dt.int32)
        is_first, is_second, first_w, second_w = (tile_by(n, EXPERTS) for n in ("is_first", "is_second", "first_w", "second_w"))
        gap, ratio, total, share1, share2 = (sb(n, [P, BLOCK_TILES]) for n in ("gap", "ratio", "total", "share1", "share2"))
        mix = sb("mix", [P, 2, BLOCK_TILES, EXPERTS])
        product = sb("product", [P, 2, EXPERTS * CH])
        half, quarter = sb("half", [P, 2, EXPERTS * CH // 2]), sb("quarter", [P, 2, EXPERTS * CH // 4])
        mixed, out_sb = sb("mixed", [P, 2, BANK]), sb("out_sb", [P, 2, BANK])
        ps_proj, ps_xn, ps_router = pb("ps_proj"), pb("ps_xn"), pb("ps_router")
        ps_e = [pb(f"ps_e{i}", 2 * BANK) for i in range(2)]
        names = ("ready att_loaded tok_loaded projected added stats_done moments_done log_done rstd_done xn_done xn_turned xn_copied "
                 "routed logits_done best_done index_done small second_done gap_done ratio_done mix_done expert_done product_done halved quartered "
                 "tile_mixed out_done").split()
        (ready, att_loaded, tok_loaded, projected, added, stats_done, moments_done, log_done, rstd_done, xn_done, xn_turned, xn_copied,
         routed, logits_done, best_done, index_done, small, second_done, gap_done, ratio_done, mix_done, expert_done, product_done, halved, quartered,
         tile_mixed, out_done) = map(sem, names)
        stored = [sem(f"stored{i}") for i in range(2)]
        block = ctx.enter_context(nc.Block())
        SMALL = 7
        tile_cols = lambda t: slice(t * P, (t + 1) * P)

        @block.sync
        def _(sp):
            def load(n, source, i):
                for r in range(GROUPS):
                    sp.dma_start(att[:, i, r, :], attended[r, source]).then_inc(att_loaded, 16)
                sp.dma_start(tok[:, i, :], tokens[source]).then_inc(tok_loaded, 16)

            load(0, 0, 0)
            with sp.Fori(0, ALL_BLOCKS // 2) as k:
                for i in range(2):
                    n = k * 2 + i
                    sp.wait_ge(att_loaded, n * (16 * GROUPS) + 16 * GROUPS)
                    sp.wait_ge(tok_loaded, n * 16 + 16)
                    sp.wait_ge(added, n)
                    load(n + 1, (n + 1) % ALL_BLOCKS, 1 - i)
                    sp.wait_ge(out_done, n + 1)
                    sp.dma_start(out[n], out_sb[:, i, :].rearrange("p (t c) -> p t c", c=CH)).then_inc(stored[i], 16)
            for i in range(2):
                sp.wait_ge(stored[i], 16 * ALL_BLOCKS // 2)
            sp.wait_ge(att_loaded, 16 * GROUPS * (ALL_BLOCKS + 1))
            sp.wait_ge(tok_loaded, 16 * (ALL_BLOCKS + 1))

        @block.tensor
        def _(pe):
            ident, w_proj = CONSTANTS.of(c, "ident"), WEIGHTS.of(w, "w_proj")
            router, expert_w, ones16 = WEIGHTS.of(w, "router"), WEIGHTS.of(w, "experts"), CONSTANTS16.of(c16, "ones")

            def project(n, i):
                pe.wait_ge(att_loaded, n * (16 * GROUPS) + 16 * GROUPS)
                pe.wait_ge(added, n)
                for t in range(BLOCK_TILES):
                    for r in range(GROUPS):
                        last = nc.tensor.matmul(ps_proj[:, tile_cols(t)], att[:, i, r, tile_cols(t)], w_proj[:, r * P:(r + 1) * P],
                                                start=(r == 0), stop=(r == GROUPS - 1))
                last.then_inc(projected, 1)

            def turn(n, i):
                pe.wait_ge(xn_done, n + 1)
                pe.wait_ge(xn_copied, n)
                for t in range(BLOCK_TILES):
                    last = nc.tensor.transpose(ps_xn[:, tile_cols(t)], xn_tok[:, tile_cols(t)], ident)
                last.then_inc(xn_turned, 1)

            def route(n, i):
                pe.wait_ge(xn_copied, n + 1)
                pe.wait_ge(logits_done, n)
                for t in range(BLOCK_TILES):
                    last = nc.tensor.matmul(ps_router[:, t * EXPERTS:(t + 1) * EXPERTS], xn_ch[:, i, tile_cols(t)], router,
                                            start=True, stop=True)
                last.then_inc(routed, 1)

            def expert_products(n, i, t):
                pe.wait_ge(product_done, n * BLOCK_TILES + max(t - 1, 0))
                for e in range(2):
                    columns = slice(e * BANK, (e + 1) * BANK)
                    nc.tensor.matmul(ps_e[t % 2][:, columns], xn_ch[:, i, tile_cols(t)], expert_w[:, columns], start=True, stop=False)
                    last = nc.tensor.matmul(ps_e[t % 2][:, columns], ones16, bias16[:, columns], start=False, stop=True)
                last.then_inc(expert_done, 1)

            pe.wait_ge(ready, 2)
            project(0, 0)
            turn(0, 0)
            route(0, 0)
            with pe.Fori(0, ALL_BLOCKS // 2) as k:
                for i in range(2):
                    n = k * 2 + i
                    project(n + 1, 1 - i)
                    expert_products(n, i, 0)
                    expert_products(n, i, 1)
                    turn(n + 1, 1 - i)
                    expert_products(n, i, 2)
                    route(n + 1, 1 - i)
                    expert_products(n, i, 3)

        @block.scalar
        def _(act):
            def front(n, i):
                act.wait_ge(moments_done, n * BLOCK_TILES + BLOCK_TILES)
                act.wait_ge(rstd_done, n)
                nc.scalar.activation(log_var[:, :], moments[:, :, 1], ACT.Ln, bias=eps[:, :]).then_inc(log_done, 1)
                act.wait_ge(log_done, n + 1)
                act.wait_ge(xn_done, n)
                nc.scalar.activation(rstd[:, :], log_var[:, :], ACT.Exp, scale=-0.5).then_inc(rstd_done, 1)
                act.wait_ge(xn_turned, n + 1)
                if not (isinstance(n, int) and n == 0):
                    act.wait_ge(expert_done, (n - 1) * BLOCK_TILES)
                nc.scalar.activation(xn_ch[:, i, :], ps_xn[:, :], ACT.Copy).then_inc(xn_copied, 1)
                act.wait_ge(gap_done, n + 1)
                nc.scalar.activation(ratio[:, :], gap[:, :], ACT.Exp).then_inc(ratio_done, 1)

            act.wait_ge(ready, 2)
            front(0, 0)
            with act.Fori(0, ALL_BLOCKS // 2) as k:
                for i in range(2):
                    front(k * 2 + i + 1, 1 - i)

        @block.gpsimd
        def _(pool):
            nc.gpsimd.memset(eps[:, :], LN_EPS).then_inc(ready, 1)
            nc.gpsimd.iota(order_i[:, :], pattern=[[1, EXPERTS]], base=0, channel_multiplier=0).then_inc(ready, 1)
            with pool.Fori(0, ALL_BLOCKS // 2) as k:
                for i in range(2):
                    n = k * 2 + i
                    for t in range(BLOCK_TILES):
                        s, m = t % 2, n * BLOCK_TILES + t
                        w2, w4 = EXPERTS * CH // 2, EXPERTS * CH // 4
                        pool.wait_ge(product_done, m + 1)
                        pool.wait_ge(quartered, n * BLOCK_TILES + max(t - 1, 0))
                        nc.gpsimd.tensor_tensor(half[:, s, :], product[:, s, 0:w2], product[:, s, w2:2 * w2], ALU.add).then_inc(halved, 1)
                        pool.wait_ge(halved, m + 1)
                        pool.wait_ge(tile_mixed, n * BLOCK_TILES + max(t - 1, 0))
                        nc.gpsimd.tensor_tensor(quarter[:, s, :], half[:, s, 0:w4], half[:, s, w4:2 * w4], ALU.add).then_inc(quartered, 1)
                        pool.wait_ge(quartered, m + 1)
                        pool.wait_ge(out_done, n)
                        nc.gpsimd.tensor_tensor(mixed[:, i, tile_cols(t)], quarter[:, s, 0:CH], quarter[:, s, CH:2 * CH], ALU.add).then_inc(tile_mixed, 1)

        @block.vector
        def _(dve):
            spread = lambda v: v.unsqueeze(2).to_broadcast([P, BLOCK_TILES, EXPERTS])

            def norm(n, i):
                dve.wait_ge(projected, n + 1)
                dve.wait_ge(tok_loaded, n * 16 + 16)
                if not (isinstance(n, int) and n == 0):
                    dve.wait_ge(out_done, n - 1)
                nc.vector.tensor_tensor(t_sb[:, i, :], tok[:, i, :], ps_proj[:, :], ALU.add).then_inc(added, 1)
                dve.wait_ge(added, n + 1)
                dve.wait_ge(moments_done, n * BLOCK_TILES)
                for t in range(BLOCK_TILES):
                    nc.vector.bn_stats(stats[:, t, :], t_sb[:, i, tile_cols(t)]).then_inc(stats_done, 1)
                stats_done_due = worked_out(dve, n * BLOCK_TILES + BLOCK_TILES)
                xn_done_due = worked_out(dve, n)
                dve.wait_ge(ready, 3)
                dve.wait_ge(stats_done, stats_done_due)
                dve.wait_ge(xn_done, xn_done_due)
                for t in range(BLOCK_TILES):
                    nc.vector.bn_aggr(moments[:, t, :], stats[:, t, :]).then_inc(moments_done, 1)

            def normalise(n, i):
                dve.wait_ge(rstd_done, n + 1)
                dve.wait_ge(moments_done, n * BLOCK_TILES + BLOCK_TILES)
                dve.wait_ge(xn_turned, n)
                for t in range(BLOCK_TILES):
                    last = nc.vector.tensor_scalar(xn_tok[:, tile_cols(t)], t_sb[:, i, tile_cols(t)], moments[:, t, 0:1], rstd[:, t:t + 1],
                                                   ALU.subtract, ALU.mult)
                last.then_inc(xn_done, 1)

            def choose(n, i):
                dve.wait_ge(routed, n + 1)
                dve.wait_ge(index_done, n * BLOCK_TILES)
                nc.vector.tensor_tensor(logits[:, :, :], ps_router[:, 0:BLOCK_TILES * EXPERTS].rearrange("p (t e) -> p t e", e=EXPERTS),
                                        WEIGHTS.of(w, "router_b").unsqueeze(1).to_broadcast([P, BLOCK_TILES, EXPERTS]), ALU.add).then_inc(logits_done, 1)
                logits_done_due = worked_out(dve, n + 1)
                gap_done_due = worked_out(dve, n)
                dve.wait_ge(ready, 3)
                dve.wait_ge(logits_done, logits_done_due)
                dve.wait_ge(gap_done, gap_done_due)
                for t in range(BLOCK_TILES):
                    nc.vector.max(best[:, t, :], logits[:, t, :]).then_inc(best_done, 1)
                best_done_due = worked_out(dve, n * BLOCK_TILES + BLOCK_TILES)
                small_due = worked_out(dve, n * SMALL)
                dve.wait_ge(ready, 3)
                dve.wait_ge(best_done, best_done_due)
                dve.wait_ge(small, small_due)
                for t in range(BLOCK_TILES):
                    nc.vector.max_index(index[:, t, :], best[:, t, :], logits[:, t, :]).then_inc(index_done, 1)
                dve.wait_ge(ratio_done, n)
                nc.vector.tensor_tensor(gap[:, :], best[:, :, 1], best[:, :, 0], ALU.subtract).then_inc(gap_done, 1)
                dve.wait_ge(index_done, n * BLOCK_TILES + BLOCK_TILES)
                nc.vector.tensor_copy(index_f[:, :, :], index[:, :, :]).then_inc(small, 1)
                dve.wait_ge(small, n * SMALL + 1)
                dve.wait_ge(mix_done, n)
                expert = order[:, :].unsqueeze(1).to_broadcast([P, BLOCK_TILES, EXPERTS])
                nc.vector.tensor_tensor(is_first[:, :, :], expert, spread(index_f[:, :, 0]), ALU.is_equal).then_inc(small, 1)
                nc.vector.tensor_tensor(is_second[:, :, :], expert, spread(index_f[:, :, 1]), ALU.is_equal).then_inc(small, 1)

            def shares(n, i):
                dve.wait_ge(ratio_done, n + 1)
                nc.vector.tensor_scalar(total[:, :], ratio[:, :], 1.0, None, ALU.add).then_inc(small, 1)
                dve.wait_ge(small, n * SMALL + 4)
                nc.vector.reciprocal(share1[:, :], total[:, :]).then_inc(small, 1)
                dve.wait_ge(small, n * SMALL + 5)
                nc.vector.tensor_tensor(share2[:, :], ratio[:, :], share1[:, :], ALU.mult).then_inc(small, 1)
                nc.vector.tensor_tensor(first_w[:, :, :], is_first[:, :, :], spread(share1[:, :]), ALU.mult).then_inc(small, 1)
                dve.wait_ge(small, n * SMALL + SMALL)
                nc.vector.tensor_tensor(second_w[:, :, :], is_second[:, :, :], spread(share2[:, :]), ALU.mult).then_inc(second_done, 1)
                dve.wait_ge(second_done, n + 1)
                if not (isinstance(n, int) and n == 0):
                    dve.wait_ge(product_done, (n - 1) * BLOCK_TILES)
                nc.vector.tensor_tensor(mix[:, i], first_w[:, :, :], second_w[:, :, :], ALU.add).then_inc(mix_done, 1)

            def weigh(n, i, t):
                m = n * BLOCK_TILES + t
                dve.wait_ge(expert_done, m + 1)
                dve.wait_ge(mix_done, n + 1)
                dve.wait_ge(halved, n * BLOCK_TILES + max(t - 1, 0))
                nc.vector.tensor_tensor(product[:, t % 2, :].rearrange("p (e c) -> p e c", c=CH),
                                        ps_e[t % 2][:, :].rearrange("p (e c) -> p e c", c=CH),
                                        mix[:, i, t, :].unsqueeze(2).to_broadcast([P, EXPERTS, CH]), ALU.mult).then_inc(product_done, 1)

            dve.wait_ge(ready, 2)
            nc.vector.tensor_copy(order[:, :], order_i[:, :]).then_inc(ready, 1)
            dve.wait_ge(ready, 3)
            norm(0, 0)
            normalise(0, 0)
            choose(0, 0)
            shares(0, 0)
            with dve.Fori(0, ALL_BLOCKS // 2) as k:
                for i in range(2):
                    n = k * 2 + i
                    norm(n + 1, 1 - i)
                    weigh(n, i, 0)
                    normalise(n + 1, 1 - i)
                    weigh(n, i, 1)
                    weigh(n, i, 2)
                    choose(n + 1, 1 - i)
                    weigh(n, i, 3)
                    shares(n + 1, 1 - i)
                    dve.wait_ge(tile_mixed, n * BLOCK_TILES + BLOCK_TILES)
                    dve.wait_ge(stored[i], k * 16)
                    nc.vector.tensor_tensor(out_sb[:, i, :], t_sb[:, i, :], mixed[:, i, :], ALU.add).then_inc(out_done, 1)


def build(nc, x, weights, constants, constants16, out):
    dram = lambda name, shape, dt=F32: nc.dram_tensor(name, shape, dt).ap()
    scan_in = dram("scan_in", (ALL_CHUNKS, P, STEP))
    scan_out = dram("scan_out", (ALL_CHUNKS, P, STEP))
    gate = dram("gate_dram", (IMAGES, P, TOK))
    left = dram("left_dram", (IMAGES, HALF, TOK))
    tokens = dram("tokens", (ALL_BLOCKS, P, BANK))
    q_parts, k_parts = (dram(n, (IMAGES, PARTS, P, TOK), BF16) for n in ("q_parts", "k_parts"))
    values = dram("values", (IMAGES, GROUPS, P, TILES, P))
    maxima = dram("maxima", (TOP, PARTS, P), BF16)
    attended = dram("attended", (GROUPS, ALL_BLOCKS, P, BANK))
    by_direction = lambda t: t.rearrange("(b k c) p t -> b k p c t", k=DIRS, c=SCAN_CHUNKS)
    x_images = x.rearrange("b h w c -> b (h w) c")
    with ExitStack() as ctx:
        sb = lambda name, shape, dt=F32: ctx.enter_context(nc.sbuf_tensor(name, shape, dt))
        w, c, c16 = sb("w", [P, WEIGHTS.n]), sb("c", [P, CONSTANTS.n]), sb("c16", [P, CONSTANTS16.n], BF16)
        d, bias16 = sb("d", [P, DERIVED.n]), sb("bias16", [P, EXPERTS * P], BF16)
        prepare(nc, weights, constants, constants16, w, c, c16, d, bias16)
        conv_front(nc, x_images, w, c, d, by_direction(scan_in), gate, left)
        state_scan(nc, w, c, c16, d, scan_in, scan_out)
        conv_back(nc, x_images, w, c, d, by_direction(scan_out), gate, left, tokens, q_parts, k_parts, values)
        attention(nc, c, c16, q_parts, k_parts, values, maxima, attended)
        experts(nc, w, c, c16, bias16, attended, tokens, out.rearrange("b h w c -> (b h w) c").rearrange("(n t p) c -> n p t c", p=P, t=BLOCK_TILES))


def lay_out_weights(i):
    w = np.zeros((P, WEIGHTS.n), np.float32)
    col = lambda name: WEIGHTS.of(w, name)
    L, R = slice(0, HALF), slice(HALF, P)
    g = lambda name: np.asarray(i["L0_conv_" + name])
    col("in1x1")[L, L], col("in1x1")[R, R] = g("cv2_w").T, g("cv1_w").T
    col("in_scale")[:, 0] = np.concatenate([g("cv2_g"), g("cv1_g")])
    col("in_bias")[:, 0] = np.concatenate([g("cv2_b"), g("cv1_b")])
    col("bn0_scale")[:, 0] = np.concatenate([g("bn0_g"), np.ones(HALF, np.float32)])
    col("bn0_bias")[L, 0] = g("bn0_b")
    col("xh")[R], col("gate")[R] = g("in_proj_w")[:P].T, g("in_proj_w")[P:].T
    col("dw")[:] = np.broadcast_to(g("dw_w").reshape(1, TAPS * P), (P, TAPS * P))
    col("dw_b")[:, 0] = g("dw_b")
    for n in ("1", "2"):
        col("c" + n)[L] = g(f"c{n}_w").reshape(TAPS, HALF, HALF).transpose(1, 0, 2).reshape(HALF, TAPS * HALF)
        for v in (f"c{n}_b", f"bn{n}_g", f"bn{n}_b"):
            col(v)[L, 0] = g(v)
    col("c3")[L], col("c3_b")[L, 0] = g("c3_w").T, g("c3_b")
    xp = g("x_proj_w")
    bc = xp[:, DT_RANK:].transpose(2, 0, 1)
    col("bc")[:] = np.concatenate([bc] * PARTS, axis=2).reshape(P, DIRS * 96)
    col("xp_dt")[:DT_RANK] = xp[:, :DT_RANK].transpose(1, 0, 2).reshape(DT_RANK, DIRS * P)
    col("dt_w")[:DT_RANK] = g("dt_w").transpose(2, 0, 1).reshape(DT_RANK, DIRS * P)
    col("dt_b")[:] = g("dt_b").T
    col("a_logs")[:] = g("A_logs").reshape(DIRS, P, STATES).transpose(1, 0, 2).reshape(P, DIRS * STATES)
    col("skip")[:] = g("Ds").reshape(DIRS, P).T
    col("ln_g")[:, 0], col("ln_b")[:, 0] = g("ln_g"), g("ln_b")
    col("out_proj")[L] = g("out_proj_w")
    col("cv")[L, HALF:] = g("cv_w").T
    col("cv_g")[R, 0], col("cv_b")[R, 0] = g("cv_g"), g("cv_b")
    shuffle = np.arange(P).reshape(2, HALF).T.reshape(P)
    col("cv3")[:] = g("cv3_w")[shuffle].T
    col("cv3_g")[:, 0], col("cv3_b")[:, 0] = g("cv3_g")[shuffle], g("cv3_b")[shuffle]
    col("qkv")[:] = i["L1_attn_w_attn"]
    wp = np.zeros((2, HEADS // 2, 2 * HEAD, P), np.float32)
    wp[:, :, :HEAD] = np.asarray(i["L1_attn_w_proj"]).reshape(2, HEADS // 2, HEAD, P)
    col("w_proj")[:] = wp.reshape(2, P, P).transpose(1, 0, 2).reshape(P, 2 * P)
    col("router")[:] = i["L1_ffn_router_w"]
    col("router_b")[:] = np.broadcast_to(i["L1_ffn_router_b"], (P, EXPERTS))
    col("experts")[:] = np.asarray(i["L1_ffn_expert_w"]).transpose(1, 0, 2).reshape(P, EXPERTS * P)
    col("expert_b")[:PARTS] = np.broadcast_to(np.asarray(i["L1_ffn_expert_b"]).reshape(1, EXPERTS * P), (PARTS, EXPERTS * P))
    return w


def lay_out_constants():
    c, c16 = np.zeros((P, CONSTANTS.n), np.float32), np.zeros((P, CONSTANTS16.n), np.float32)
    CONSTANTS.of(c, "ident")[:] = np.eye(P)
    CONSTANTS.of(c, "mean")[:] = 1.0 / P
    CONSTANTS.of(c, "part_a")[32:96] = -1.0
    CONSTANTS.of(c, "part_b")[64:96] = -1.0
    CONSTANTS.of(c, "row_a")[1:3] = -1.0
    CONSTANTS.of(c, "row_b")[2:3] = -1.0
    for h in range(HEADS // 2):
        CONSTANTS.of(c, "head_sum")[32 * h + HEAD, 32 * h:32 * h + 32] = 1.0
    for n in range(2 * STATES):
        CONSTANTS16.of(c16, "select")[n:96:32, n * P:(n + 1) * P] = 1.0
    CONSTANTS16.of(c16, "ident")[:] = np.eye(P)
    CONSTANTS16.of(c16, "above")[:] = np.where(np.arange(P)[:, None] > np.arange(P)[None, :], MASKED, 0.0)
    CONSTANTS16.of(c16, "below")[:] = np.where(np.arange(P)[:, None] < np.arange(P)[None, :], MASKED, 0.0)
    CONSTANTS16.of(c16, "ones")[:PARTS] = 1.0
    return c, c16.astype(mybir.dt.np(BF16))


def kernel(**inputs):
    import concourse.bacc as bacc
    from concourse.bass_utils import run_bass_kernel_spmd

    nc = bacc.Bacc("TRN2", target_bir_lowering=False, num_devices=1)
    c, c16 = lay_out_constants()
    arrays = {"x_in": np.ascontiguousarray(inputs["x"]), "weights": lay_out_weights(inputs), "constants": c, "constants16": c16}
    args = [nc.dram_tensor(n, a.shape, mybir.dt.from_np(a.dtype), kind="ExternalInput").ap() for n, a in arrays.items()]
    out = nc.dram_tensor("out", (IMAGES, SIDE, SIDE, CH), F32, kind="ExternalOutput").ap()
    build(nc, *args, out)
    result = run_bass_kernel_spmd(nc, [arrays], core_ids=[0])
    return result.results[0]["out"]
```

```python
import numpy as np
from contextlib import ExitStack

import concourse.bass as bass
from concourse import mybir

F32 = mybir.dt.float32
BF16 = mybir.dt.bfloat16
ALU = mybir.AluOpType
ACT = mybir.ActivationFunctionType
AX = mybir.AxisListType
ds = bass.ds

P = 128
IMAGES, SIDE, CH = 4, 64, 128
HALF = CH // 2
TOK = SIDE * SIDE
BANK = 512
PAD = SIDE + 2
ROWS = BANK // SIDE
CHUNKS = TOK // BANK
TILES = TOK // P
TAPS = 9

DIRS, STATES, DT_RANK = 4, 16, 4
STEP = 1024
SCAN_CHUNKS = TOK // STEP
ALL_CHUNKS = IMAGES * DIRS * SCAN_CHUNKS
PARTS = 3

HEADS, HEAD = 8, 16
EXPERTS = 8


class Columns:

    def __init__(self, widths):
        self.at, self.n = {}, 0
        for name, width in widths:
            self.at[name] = (self.n, width)
            self.n += width

    def of(self, tensor, name, rows=P, start=0):
        at, width = self.at[name]
        return tensor[start:rows, at:at + width]


WEIGHTS = Columns([
    ("in1x1", P), ("in_scale", 1), ("in_bias", 1), ("bn0_scale", 1), ("bn0_bias", 1),
    ("xh", P), ("gate", P), ("dw", TAPS * P), ("dw_b", 1),
    ("c1", TAPS * HALF), ("c1_b", 1), ("bn1_g", 1), ("bn1_b", 1),
    ("c2", TAPS * HALF), ("c2_b", 1), ("bn2_g", 1), ("bn2_b", 1),
    ("c3", HALF), ("c3_b", 1),
    ("bc", DIRS * 96), ("xp_dt", DIRS * P), ("dt_w", DIRS * P), ("dt_b", DIRS),
    ("a_logs", DIRS * STATES), ("skip", DIRS),
    ("ln_g", 1), ("ln_b", 1), ("out_proj", P), ("cv", P), ("cv_g", 1), ("cv_b", 1),
    ("cv3", P), ("cv3_g", 1), ("cv3_b", 1),
    ("qkv", 3 * P), ("w_proj", 2 * P),
    ("router", EXPERTS), ("router_b", EXPERTS), ("experts", EXPERTS * P), ("expert_b", EXPERTS * P),
])
CONSTANTS = Columns([
    ("ident", P), ("mean", P), ("part_a", 1), ("part_b", 1), ("row_a", 1), ("row_b", 1),
    ("head_sum", P),
])
CONSTANTS16 = Columns([("select", 2 * STATES * P), ("ident", P), ("above", P), ("below", P), ("ones", P)])
MASKED = -1e30
DERIVED = Columns([
    ("taps", TAPS * P), ("dt", DIRS * P), ("neg_a", DIRS * STATES), ("cv_out", P),
    ("c1_bias", 1), ("c2_bias", 1),
])


def scan_slot(tensor):
    return tensor[:, 0:P], tensor[:, P:P + 96], tensor[:, P + 96:P + 97]


def prepare(nc, weights, constants, constants16, w, c, c16, d, bias16):
    with ExitStack() as ctx:
        sb = lambda name, shape, dt=F32: ctx.enter_context(nc.sbuf_tensor(name, shape, dt))
        sem = lambda name: ctx.enter_context(nc.semaphore(name))
        hi = sb("pre_hi", [P, EXPERTS * P], BF16)
        rest = sb("pre_rest", [P, EXPERTS * P])
        exp_a = sb("pre_exp_a", [P, DIRS * STATES])
        ps = ctx.enter_context(nc.psum_tensor("pre_ps", [P, (DIRS + 1) * BANK], F32))
        loaded, products, exp_done, chain = (sem(f"pre_{n}") for n in ("loaded", "products", "exp", "chain"))
        block = ctx.enter_context(nc.Block())

        @block.sync
        def _(sp):
            sp.dma_start(w[:, :], weights).then_inc(loaded, 16)
            sp.dma_start(c[:, :], constants).then_inc(loaded, 16)
            sp.dma_start(c16[:, :], constants16).then_inc(loaded, 16)
            sp.wait_ge(loaded, 48)

        @block.tensor
        def _(pe):
            pe.wait_ge(loaded, 48)
            xp, dt = WEIGHTS.of(w, "xp_dt"), WEIGHTS.of(w, "dt_w")
            for k in range(DIRS):
                nc.tensor.matmul(ps[:, k * BANK:k * BANK + P], xp[:, k * P:(k + 1) * P],
                                 dt[:, k * P:(k + 1) * P], start=True, stop=True)
            nc.tensor.matmul(ps[:, DIRS * BANK:DIRS * BANK + P], WEIGHTS.of(w, "out_proj"),
                             WEIGHTS.of(w, "cv"), start=True, stop=True).then_inc(products, 1)

        @block.scalar
        def _(act):
            act.wait_ge(loaded, 48)
            nc.scalar.activation(exp_a[:, :], WEIGHTS.of(w, "a_logs"), ACT.Exp).then_inc(exp_done, 1)
            nc.scalar.activation(hi[:, :], WEIGHTS.of(w, "expert_b"), ACT.Copy).then_inc(exp_done, 1)

        @block.vector
        def _(dve):
            dve.wait_ge(loaded, 48)
            for t in range(TAPS):
                nc.vector.tensor_tensor(DERIVED.of(d, "taps")[:, t * P:(t + 1) * P], WEIGHTS.of(w, "xh"),
                                        WEIGHTS.of(w, "dw")[:, t * P:(t + 1) * P], ALU.mult)
            for n in ("1", "2"):
                nc.vector.scalar_tensor_tensor(
                    out=DERIVED.of(d, f"c{n}_bias"), in0=WEIGHTS.of(w, f"c{n}_b"),
                    scalar=WEIGHTS.of(w, f"bn{n}_g"), in1=WEIGHTS.of(w, f"bn{n}_b"),
                    op0=ALU.mult, op1=ALU.add)
            dve.wait_ge(exp_done, 1)
            nc.vector.tensor_scalar(DERIVED.of(d, "neg_a"), exp_a[:, :], -1.0, None, ALU.mult)
            dve.wait_ge(exp_done, 2)
            part_a, part_b = CONSTANTS.of(c, "row_a"), CONSTANTS.of(c, "row_b")
            nc.vector.scalar_tensor_tensor(out=rest[:, :], in0=hi[:, :], scalar=part_a,
                                           in1=WEIGHTS.of(w, "expert_b"), op0=ALU.mult, op1=ALU.add).then_inc(chain, 1)
            dve.wait_ge(chain, 1)
            nc.vector.tensor_copy(hi[:, :], rest[:, :]).then_inc(chain, 1)
            dve.wait_ge(chain, 2)
            nc.vector.scalar_tensor_tensor(out=bias16[:, :], in0=hi[:, :], scalar=part_b, in1=rest[:, :],
                                           op0=ALU.mult, op1=ALU.add)
            dve.wait_ge(products, 1)
            nc.vector.tensor_copy(DERIVED.of(d, "dt").rearrange("p (k n) -> p k n", n=P),
                                  ps[:, 0:DIRS * BANK].rearrange("p (k n) -> p k n", n=BANK)[:, :, 0:P])
            nc.vector.tensor_copy(DERIVED.of(d, "cv_out"), ps[:, DIRS * BANK:DIRS * BANK + P])


X_PARTS = [(slice(t, t + 4), slice(t * P, (t + 4) * P)) for t in range(0, TILES, 4)]
X_COUNT = 16 * len(X_PARTS)


def worked_out(engine, value):
    return value if isinstance(value, int) else engine.to_reg(value)


def conv_front(nc, x, w, c, d, scan_in, gate, left):
    with ExitStack() as ctx:
        sb = lambda name, shape: ctx.enter_context(nc.sbuf_tensor("cf_" + name, shape, F32))
        pb = lambda name: ctx.enter_context(nc.psum_tensor("cf_" + name, [P, BANK], F32))
        sem = lambda name: ctx.enter_context(nc.semaphore("cf_" + name))
        x_tok = sb("x_tok", [P, TILES, CH])
        x_ch = sb("x_ch", [P, TOK])
        act_in = sb("act_in", [P, 2, BANK])
        pad1 = sb("pad1", [P, PAD, PAD])
        pad2 = sb("pad2", [P, PAD, PAD])
        conv2 = sb("conv2", [P, 2, BANK])
        left_sb = sb("left_sb", [P, 2, BANK])
        gate_sb = sb("gate_sb", [P, 2, BANK])
        dirs = [sb(f"dir{k}", [P, TOK]) for k in range(DIRS)]
        ps_tr = [pb(f"ps_tr{i}") for i in range(2)]
        ps_in, ps_xh, ps_gate, ps_c1, ps_c2, ps_c3 = (pb(n) for n in ("ps_in", "ps_xh", "ps_gate", "ps_c1", "ps_c2", "ps_c3"))

        x_loaded, cleared = sem("x_loaded"), sem("cleared")
        transposed, x_copied = sem("transposed"), sem("x_copied")
        in_done, in_silu, padded = sem("in_done"), sem("in_silu"), sem("padded")
        xh_done, xh_silu, gate_done, gate_silu = sem("xh_done"), sem("xh_silu"), sem("gate_done"), sem("gate_silu")
        c1_done, c1_relu, c2_done, c2_relu = sem("c1_done"), sem("c1_relu"), sem("c2_done"), sem("c2_relu")
        c3_done, c3_relu, turned = sem("c3_done"), sem("c3_relu"), sem("turned")
        gate_stored, left_stored = [sem(f"gate_stored{i}") for i in range(2)], [sem(f"left_stored{i}") for i in range(2)]
        dirs_stored = sem("dirs_stored")
        block = ctx.enter_context(nc.Block())

        def window(pad, g, dy, dx):
            return pad[:, g * ROWS + dy:g * ROWS + dy + ROWS, dx:dx + SIDE]

        def inner(pad, g, rows=P):
            return pad[0:rows, g * ROWS + 1:(g + 1) * ROWS + 1, 1:SIDE + 1]

        def rows_of(tile):
            return tile.rearrange("p (r s) -> p r s", s=SIDE)

        @block.sync
        def _(sp):
            def load_x(b):
                for tiles, rows in X_PARTS:
                    sp.dma_start(x_tok[:, tiles, :], x[b, rows].rearrange("(t p) c -> p t c", p=P)).then_inc(x_loaded, 16)

            load_x(0)
            with sp.Fori(0, IMAGES) as b:
                sp.wait_ge(transposed, b * CHUNKS + CHUNKS)
                load_x((b + 1) % IMAGES)
                for g in range(CHUNKS):
                    sp.wait_ge(gate_silu, b * CHUNKS + g + 1)
                    sp.dma_start(gate[b, :, g * BANK:(g + 1) * BANK], gate_sb[:, g % 2, :]).then_inc(gate_stored[g % 2], 16)
                sp.dma_start(scan_in[b, 0], dirs[0][:, :].rearrange("p (c t) -> p c t", t=STEP)).then_inc(dirs_stored, 16)
                for k in range(1, DIRS):
                    sp.wait_ge(turned, b * (DIRS - 1) + k)
                    sp.dma_start(scan_in[b, k], dirs[k][:, :].rearrange("p (c t) -> p c t", t=STEP)).then_inc(dirs_stored, 16)
                for g in range(CHUNKS):
                    sp.wait_ge(c3_relu, b * CHUNKS + g + 1)
                    sp.dma_start(left[b, :, g * BANK:(g + 1) * BANK], left_sb[0:HALF, g % 2, :]).then_inc(left_stored[g % 2], 16)
            sp.wait_ge(x_loaded, X_COUNT * (IMAGES + 1))
            sp.wait_ge(dirs_stored, 16 * IMAGES * DIRS)
            for i in range(2):
                sp.wait_ge(gate_stored[i], 16 * IMAGES * CHUNKS // 2)
                sp.wait_ge(left_stored[i], 16 * IMAGES * CHUNKS // 2)

        @block.gpsimd
        def _(pool):
            nc.gpsimd.memset(pad1[:, :, :], 0.0).then_inc(cleared, 1)
            nc.gpsimd.memset(pad2[:, :, :], 0.0).then_inc(cleared, 1)

        @block.tensor
        def _(pe):
            in1x1, gate_w, c3 = WEIGHTS.of(w, "in1x1"), WEIGHTS.of(w, "gate"), WEIGHTS.of(w, "c3")
            taps, c1, c2 = DERIVED.of(d, "taps"), WEIGHTS.of(w, "c1"), WEIGHTS.of(w, "c2")
            ident = CONSTANTS.of(c, "ident")

            def conv(out, pad, g, stationary, width):
                for t in range(TAPS):
                    last = nc.tensor.matmul(out, stationary[:, t * width:(t + 1) * width],
                                            window(pad, g, t // 3, t % 3), start=(t == 0), stop=(t == TAPS - 1))
                return last

            pe.wait_ge(cleared, 2)
            with pe.Fori(0, IMAGES) as b:
                first = b * CHUNKS
                pe.wait_ge(x_loaded, b * X_COUNT + X_COUNT)
                for g in range(CHUNKS):
                    pe.wait_ge(x_copied, first + max(g - 1, 0))
                    for t in range(BANK // P):
                        last = nc.tensor.transpose(ps_tr[g % 2][:, t * P:(t + 1) * P], x_tok[:, g * (BANK // P) + t, :], ident)
                    last.then_inc(transposed, 1)
                for g in range(CHUNKS):
                    pe.wait_ge(x_copied, first + g + 1)
                    pe.wait_ge(in_silu, first + g)
                    nc.tensor.matmul(ps_in[:, :], in1x1, x_ch[:, g * BANK:(g + 1) * BANK], start=True, stop=True).then_inc(in_done, 1)
                for g in range(CHUNKS):
                    pe.wait_ge(padded, first + min(g + 2, CHUNKS))
                    pe.wait_ge(xh_silu, first + g)
                    conv(ps_xh[:, :], pad1, g, taps, P).then_inc(xh_done, 1)
                    pe.wait_ge(gate_silu, first + g)
                    nc.tensor.matmul(ps_gate[:, :], gate_w, window(pad1, g, 1, 1), start=True, stop=True).then_inc(gate_done, 1)
                    pe.wait_ge(c1_relu, first + g)
                    conv(ps_c1[0:HALF, :], pad1, g, c1, HALF).then_inc(c1_done, 1)
                for g in range(CHUNKS + 1):
                    if g < CHUNKS:
                        pe.wait_ge(c1_relu, first + min(g + 2, CHUNKS))
                        pe.wait_ge(c2_relu, first + g)
                        conv(ps_c2[0:HALF, :], pad2, g, c2, HALF).then_inc(c2_done, 1)
                    if g:
                        pe.wait_ge(cleared, 2)
                        pe.wait_ge(c2_relu, first + g)
                        pe.wait_ge(c3_relu, first + g - 1)
                        nc.tensor.matmul(ps_c3[0:HALF, :], c3[0:HALF, :], conv2[0:HALF, (g - 1) % 2, :],
                                         start=True, stop=True).then_inc(c3_done, 1)

        @block.scalar
        def _(act):
            act.wait_ge(cleared, 2)
            with act.Fori(0, IMAGES) as b:
                first = b * CHUNKS
                for g in range(CHUNKS):
                    act.wait_ge(in_done, first + g + 1)
                    act.wait_ge(padded, first + max(g - 1, 0))
                    nc.scalar.activation(act_in[:, g % 2, :], ps_in[:, :], ACT.Silu, bias=WEIGHTS.of(w, "in_bias"),
                                         scale=WEIGHTS.of(w, "in_scale")).then_inc(in_silu, 1)
                act.wait_ge(dirs_stored, b * DIRS * 16)
                act.wait_ge(c2_done, first)
                for g in range(CHUNKS):
                    act.wait_ge(xh_done, first + g + 1)
                    nc.scalar.activation(dirs[0][:, g * BANK:(g + 1) * BANK], ps_xh[:, :], ACT.Silu,
                                         bias=WEIGHTS.of(w, "dw_b")).then_inc(xh_silu, 1)
                    act.wait_ge(gate_done, first + g + 1)
                    act.wait_ge(gate_stored[g % 2], (b * (CHUNKS // 2) + g // 2) * 16)
                    nc.scalar.activation(gate_sb[:, g % 2, :], ps_gate[:, :], ACT.Silu).then_inc(gate_silu, 1)
                    act.wait_ge(c1_done, first + g + 1)
                    nc.scalar.activation(inner(pad2, g, HALF), rows_of(ps_c1[0:HALF, :]), ACT.Relu,
                                         bias=DERIVED.of(d, "c1_bias", HALF), scale=WEIGHTS.of(w, "bn1_g", HALF)).then_inc(c1_relu, 1)
                for g in range(CHUNKS + 1):
                    if g < CHUNKS:
                        act.wait_ge(c2_done, first + g + 1)
                        act.wait_ge(c3_done, first + max(g - 1, 0))
                        nc.scalar.activation(conv2[0:HALF, g % 2, :], ps_c2[0:HALF, :], ACT.Relu,
                                             bias=DERIVED.of(d, "c2_bias", HALF), scale=WEIGHTS.of(w, "bn2_g", HALF)).then_inc(c2_relu, 1)
                    if g:
                        i = (g - 1) % 2
                        act.wait_ge(c3_done, first + g)
                        act.wait_ge(left_stored[i], (b * (CHUNKS // 2) + (g - 1) // 2) * 16)
                        nc.scalar.activation(left_sb[0:HALF, i, :], ps_c3[0:HALF, :], ACT.Relu,
                                             bias=WEIGHTS.of(w, "c3_b", HALF)).then_inc(c3_relu, 1)

        @block.vector
        def _(dve):
            dve.wait_ge(cleared, 2)
            with dve.Fori(0, IMAGES) as b:
                first = b * CHUNKS
                dve.wait_ge(in_done, first)
                for g in range(CHUNKS):
                    dve.wait_ge(transposed, first + g + 1)
                    nc.vector.tensor_copy(x_ch[:, g * BANK:(g + 1) * BANK], ps_tr[g % 2][:, :]).then_inc(x_copied, 1)
                dve.wait_ge(c1_done, first)
                for g in range(CHUNKS):
                    dve.wait_ge(in_silu, first + g + 1)
                    nc.vector.tensor_scalar(inner(pad1, g), rows_of(act_in[:, g % 2, :]), WEIGHTS.of(w, "bn0_scale"),
                                            WEIGHTS.of(w, "bn0_bias"), ALU.mult, ALU.add).then_inc(padded, 1)
                dve.wait_ge(xh_silu, first + CHUNKS)
                nc.vector.tensor_copy(dirs[1][:, :].rearrange("p (s r) -> p s r", r=SIDE),
                                      dirs[0][:, :].rearrange("p (r s) -> p s r", s=SIDE)).then_inc(turned, 1)
                nc.vector.tensor_copy(dirs[2][:, :], dirs[0][:, ::-1]).then_inc(turned, 1)
                dve.wait_ge(turned, b * (DIRS - 1) + 1)
                nc.vector.tensor_copy(dirs[3][:, :], dirs[1][:, ::-1]).then_inc(turned, 1)


RING = 4


def state_scan(nc, w, c, c16, d, scan_in, scan_out):
    with ExitStack() as ctx:
        sb = lambda name, shape, dt=F32: ctx.enter_context(nc.sbuf_tensor("ss_" + name, shape, dt))
        pb = lambda name: ctx.enter_context(nc.psum_tensor("ss_" + name, [P, STEP], F32))
        sem = lambda name: ctx.enter_context(nc.semaphore("ss_" + name))
        x_in = sb("x_in", [P, 2 * STEP])
        slot = sb("slot", [P, P + 96 + 1])
        mag, pos, small, log1 = (sb(n, [P, STEP]) for n in ("mag", "pos", "small", "log1"))
        one, rest_e = sb("one", [P, STEP]), sb("rest_e", [P, STEP])
        hi, mid, rest = sb("hi", [96, STEP], BF16), sb("mid", [96, STEP], BF16), sb("rest", [96, STEP])
        delta, dx = sb("delta", [P, 2 * STEP]), sb("dx", [P, 2 * STEP])
        bc = sb("bc", [96, 2 * STEP], BF16)
        b_sb, decay, drive = (sb(n, [P, RING, STEP]) for n in ("b_sb", "decay", "drive"))
        h, hc = sb("h", [P, 2, STEP]), sb("hc", [P, 2, STEP])
        carry = sb("carry", [P, 2 * STATES])
        y_sb = sb("y_sb", [P, STEP])
        ps_prep, ps_b, ps_c, ps_y = pb("ps_prep"), pb("ps_b"), pb("ps_c"), pb("ps_y")

        x_loaded, y_stored, start = sem("x_loaded"), sem("y_stored"), sem("start")
        slot_filled, dt_done, dt_read, exp_small, log_done = (sem(n) for n in ("slot_filled", "dt_done", "dt_read", "exp_small", "log_done"))
        bc_done, hi_done, rest_done, mid_done, bc_split = (sem(n) for n in ("bc_done", "hi_done", "rest_done", "mid_done", "bc_split"))
        dve_prep, delta_done, dx_done = sem("dve_prep"), sem("delta_done"), sem("dx_done")
        b_done, b_copied, decayed, driven = (sem(n) for n in ("b_done", "b_copied", "decayed", "driven"))
        scanned, carried, c_done, multiplied, summed, y_done = (sem(n) for n in ("scanned", "carried", "c_done", "multiplied", "summed", "y_done"))
        act_prep = sem("act_prep")
        block = ctx.enter_context(nc.Block())

        slot_dt, slot_bc, slot_bias = scan_slot(slot)
        PREP_DVE = 3

        def direction(q):
            return (q // SCAN_CHUNKS) % DIRS

        def half(q):
            return (q % 2) * STEP

        @block.sync
        def _(sp):
            sp.dma_start(x_in[:, 0:STEP], scan_in[0]).then_inc(x_loaded, 16)
            with sp.Fori(0, ALL_CHUNKS) as j:
                q = j + 1
                sp.wait_ge(x_loaded, j * 16 + 16)
                sp.wait_ge(y_done, j)
                sp.dma_start(x_in[:, ds(half(q), STEP)], scan_in[q % ALL_CHUNKS]).then_inc(x_loaded, 16)
                sp.wait_ge(y_done, j + 1)
                sp.dma_start(scan_out[j], y_sb[:, :]).then_inc(y_stored, 16)
            sp.wait_ge(y_stored, 16 * ALL_CHUNKS)
            sp.wait_ge(x_loaded, 16 * (ALL_CHUNKS + 1))

        @block.tensor
        def _(pe):
            ident = CONSTANTS.of(c, "ident")
            select = CONSTANTS16.of(c16, "select", 96)

            def prep_dt(q):
                pe.wait_ge(slot_filled, q + 1)
                pe.wait_ge(x_loaded, q * 16 + 16)
                pe.wait_ge(rest_done, q)
                for i in range(STEP // BANK):
                    last = nc.tensor.matmul(ps_prep[:, i * BANK:(i + 1) * BANK], slot_dt,
                                            x_in[:, ds(half(q) + i * BANK, BANK)], start=True, stop=True)
                last.then_inc(dt_done, 1)

            def prep_bc(q):
                pe.wait_ge(dt_read, q + 1)
                for i in range(STEP // BANK):
                    last = nc.tensor.matmul(ps_prep[0:96, i * BANK:(i + 1) * BANK], slot_bc,
                                            x_in[:, ds(half(q) + i * BANK, BANK)], start=True, stop=True)
                last.then_inc(bc_done, 1)

            def spread(out, n, q):
                for i in range(STEP // BANK):
                    last = nc.tensor.matmul(out[:, i * BANK:(i + 1) * BANK], select[:, n * P:(n + 1) * P],
                                            bc[:, ds(half(q) + i * BANK, BANK)], start=True, stop=True)
                return last

            prep_dt(0)
            prep_bc(0)
            pe.wait_ge(bc_split, 1)
            for n in range(4):
                if n:
                    pe.wait_ge(b_copied, n)
                spread(ps_b, n, 0).then_inc(b_done, 1)
            spread(ps_c, STATES, 0).then_inc(c_done, 1)
            with pe.Fori(0, ALL_CHUNKS) as j:
                m0 = j * STATES
                for n in range(STATES):
                    pe.wait_ge(multiplied, m0 + n + 1)
                    nn, q = (n + 1) % STATES, j + (n + 1) // STATES
                    spread(ps_c, STATES + nn, q).then_inc(c_done, 1)
                    if n == 0:
                        pe.wait_ge(y_done, j)
                    for i in range(STEP // BANK):
                        last = nc.tensor.matmul(ps_y[:, i * BANK:(i + 1) * BANK], ident,
                                                hc[:, n % 2, i * BANK:(i + 1) * BANK],
                                                start=(n == 0), stop=(n == STATES - 1))
                    last.then_inc(summed, 1)
                    if n == 2:
                        prep_dt(j + 1)
                    if n == 4:
                        prep_bc(j + 1)
                    nn, q = (n + 4) % STATES, j + (n + 4) // STATES
                    if nn == 0:
                        pe.wait_ge(bc_split, j + 2)
                    pe.wait_ge(b_copied, m0 + n + 4)
                    spread(ps_b, nn, q).then_inc(b_done, 1)

        @block.scalar
        def _(act):
            neg_a, dt, bc_w, dt_b = DERIVED.of(d, "neg_a"), DERIVED.of(d, "dt"), WEIGHTS.of(w, "bc"), WEIGHTS.of(w, "dt_b")

            def prep_slot(q):
                k = direction(q)
                act.wait_ge(bc_done, q)
                act.wait_ge(dt_read, q)
                nc.scalar.activation(slot_dt, dt[:, ds(k * P, P)], ACT.Copy)
                nc.scalar.activation(slot_bc, bc_w[:, ds(k * 96, 96)], ACT.Copy)
                nc.scalar.activation(slot_bias, dt_b[:, ds(k, 1)], ACT.Copy).then_inc(slot_filled, 1)

            def prep_softplus(q):
                act.wait_ge(slot_filled, q + 1)
                act.wait_ge(dt_done, q + 1)
                act.wait_ge(dve_prep, q * PREP_DVE)
                act.wait_ge(exp_small, q)
                nc.scalar.activation(mag[:, :], ps_prep[:, :], ACT.Abs, bias=slot_bias).then_inc(act_prep, 1)
                nc.scalar.activation(pos[:, :], ps_prep[:, :], ACT.Relu, bias=slot_bias).then_inc(dt_read, 1)
                act.wait_ge(act_prep, q + 1)
                act.wait_ge(log_done, q)
                nc.scalar.activation(small[:, :], mag[:, :], ACT.Exp, scale=-1.0).then_inc(exp_small, 1)

            def prep_log(q):
                act.wait_ge(exp_small, q + 1)
                nc.scalar.activation(log1[:, :], small[:, :], ACT.Ln, bias=1.0).then_inc(log_done, 1)

            def prep_hi(q):
                act.wait_ge(bc_done, q + 1)
                act.wait_ge(rest_done, q)
                nc.scalar.activation(hi[:, :], ps_prep[0:96, :], ACT.Copy).then_inc(hi_done, 1)

            def prep_mid(q):
                act.wait_ge(rest_done, q + 1)
                act.wait_ge(bc_split, q)
                nc.scalar.activation(mid[:, :], rest[:, :], ACT.Copy).then_inc(mid_done, 1)

            def copy_b(n, m):
                act.wait_ge(b_done, m + 1)
                nc.scalar.activation(b_sb[:, n % RING, :], ps_b[:, :], ACT.Copy).then_inc(b_copied, 1)

            def decays(n, q):
                nc.scalar.activation(decay[:, n % RING, :], delta[:, ds(half(q), STEP)], ACT.Exp,
                                     scale=neg_a[:, ds(direction(q) * STATES + n, 1)]).then_inc(decayed, 1)

            prep_slot(0)
            prep_softplus(0)
            prep_log(0)
            prep_hi(0)
            prep_mid(0)
            for n in range(3):
                copy_b(n, n)
            act.wait_ge(dx_done, 1)
            for n in range(2):
                decays(n, 0)
            with act.Fori(0, ALL_CHUNKS) as j:
                m0 = j * STATES
                for n in range(STATES):
                    act.wait_ge(driven, m0 + n)
                    copy_b((n + 3) % STATES, m0 + n + 3)
                    nn = (n + 2) % STATES
                    if nn == 0:
                        act.wait_ge(dx_done, j + 2)
                    act.wait_ge(scanned, m0 + n)
                    decays(nn, j + (n + 2) // STATES)
                    if n == 0:
                        prep_slot(j + 1)
                    if n == 3:
                        prep_softplus(j + 1)
                    if n == 4:
                        prep_log(j + 1)
                    if n == 6:
                        prep_hi(j + 1)
                    if n == 8:
                        prep_mid(j + 1)

        @block.gpsimd
        def _(pool):
            def drives(n, m, q):
                b_copied_due = worked_out(pool, m + 1)
                pool.wait_ge(start, 1)
                pool.wait_ge(b_copied, b_copied_due)
                nc.gpsimd.tensor_tensor(drive[:, n % RING, :], b_sb[:, n % RING, :], dx[:, ds(half(q), STEP)],
                                        ALU.mult).then_inc(driven, 1)

            nc.gpsimd.memset(carry[:, :], 0.0).then_inc(start, 1)
            pool.wait_ge(start, 1)
            pool.wait_ge(dx_done, 1)
            for n in range(2):
                drives(n, n, 0)
            with pool.Fori(0, ALL_CHUNKS) as j:
                m0 = j * STATES
                for n in range(STATES):
                    nn = (n + 2) % STATES
                    scanned_due = worked_out(pool, m0 + n + 1)
                    pool.wait_ge(start, 1)
                    pool.wait_ge(scanned, scanned_due)
                    nc.gpsimd.tensor_copy(carry[:, STATES + n:STATES + n + 1], h[:, n % 2, STEP - 1:STEP]).then_inc(carried, 1)
                    if nn == 0:
                        pool.wait_ge(dx_done, j + 2)
                    drives(nn, m0 + n + 2, j + (n + 2) // STATES)

        @block.vector
        def _(dve):
            part_a, part_b = CONSTANTS.of(c, "part_a", 96), CONSTANTS.of(c, "part_b", 96)
            skip = WEIGHTS.of(w, "skip")

            def prep_one(q):
                dve.wait_ge(delta_done, q)
                dve.wait_ge(exp_small, q + 1)
                nc.vector.tensor_scalar(one[:, :], small[:, :], 1.0, -1.0, ALU.add, ALU.add).then_inc(dve_prep, 1)
                dve.wait_ge(dve_prep, q * PREP_DVE + 1)
                nc.vector.tensor_tensor(rest_e[:, :], small[:, :], one[:, :], ALU.subtract).then_inc(dve_prep, 1)

            def prep_delta(q, j=None):
                dve.wait_ge(log_done, q + 1)
                dve.wait_ge(dve_prep, q * PREP_DVE + 2)
                nc.vector.tensor_tensor(one[:, :], log1[:, :], pos[:, :], ALU.add).then_inc(dve_prep, 1)
                dve.wait_ge(dx_done, q)
                if j is not None:
                    dve.wait_ge(decayed, j * STATES)
                dve.wait_ge(dve_prep, q * PREP_DVE + 3)
                nc.vector.tensor_tensor(delta[:, ds(half(q), STEP)], one[:, :], rest_e[:, :], ALU.add).then_inc(delta_done, 1)

            def prep_dx(q, j=None):
                if j is not None:
                    dve.wait_ge(driven, j * STATES)
                dve.wait_ge(delta_done, q + 1)
                dve.wait_ge(x_loaded, q * 16 + 16)
                nc.vector.tensor_tensor(dx[:, ds(half(q), STEP)], delta[:, ds(half(q), STEP)], x_in[:, ds(half(q), STEP)],
                                        ALU.mult).then_inc(dx_done, 1)

            def prep_rest(q):
                dve.wait_ge(hi_done, q + 1)
                dve.wait_ge(bc_split, q)
                nc.vector.scalar_tensor_tensor(out=rest[:, :], in0=hi[:, :], scalar=part_a, in1=ps_prep[0:96, :],
                                               op0=ALU.mult, op1=ALU.add).then_inc(rest_done, 1)

            def prep_split(q, j=None):
                if j is not None:
                    dve.wait_ge(c_done, j * STATES)
                dve.wait_ge(mid_done, q + 1)
                nc.vector.scalar_tensor_tensor(out=bc[:, ds(half(q), STEP)], in0=mid[:, :], scalar=part_b, in1=rest[:, :],
                                               op0=ALU.mult, op1=ALU.add).then_inc(bc_split, 1)

            def scan(n, m, q):
                dve.wait_ge(decayed, m + 1)
                dve.wait_ge(driven, m + 1)
                nc.vector.tensor_tensor_scan(h[:, n % 2, :], decay[:, n % RING, :], drive[:, n % RING, :],
                                             initial=carry[:, ds(((q % SCAN_CHUNKS + SCAN_CHUNKS - 1) // SCAN_CHUNKS) * STATES + n, 1)],
                                             op0=ALU.mult, op1=ALU.add).then_inc(scanned, 1)

            prep_one(0)
            prep_delta(0)
            prep_dx(0)
            prep_rest(0)
            prep_split(0)
            dve.wait_ge(start, 1)
            scan(0, 0, 0)
            with dve.Fori(0, ALL_CHUNKS) as j:
                m0 = j * STATES
                for n in range(STATES):
                    dve.wait_ge(scanned, m0 + n + 1)
                    dve.wait_ge(c_done, m0 + n + 1)
                    dve.wait_ge(summed, m0 + max(n - 1, 0))
                    nc.vector.tensor_tensor(hc[:, n % 2, :], h[:, n % 2, :], ps_c[:, :], ALU.mult).then_inc(multiplied, 1)
                    dve.wait_ge(carried, m0 + n)
                    dve.wait_ge(multiplied, m0 + n)
                    scan((n + 1) % STATES, m0 + n + 1, j + (n + 1) // STATES)
                    if n == 4:
                        prep_one(j + 1)
                    if n == 5:
                        prep_delta(j + 1, j)
                    if n == 6:
                        prep_dx(j + 1, j)
                    if n == 7:
                        prep_rest(j + 1)
                    if n == 9:
                        prep_split(j + 1, j)
                dve.wait_ge(summed, m0 + STATES)
                dve.wait_ge(y_stored, j * 16)
                nc.vector.scalar_tensor_tensor(out=y_sb[:, :], in0=x_in[:, ds(half(j), STEP)], scalar=skip[:, ds(direction(j), 1)],
                                               in1=ps_y[:, :], op0=ALU.mult, op1=ALU.add).then_inc(y_done, 1)


LN_EPS_SCAN = 1e-5
LN_EPS = 1e-5
HEAD_SCALE = HEAD ** -0.5
GROUPS = 2
GROUP_HEADS = HEADS // GROUPS
SLOT = P // GROUP_HEADS
BLOCK_TILES = BANK // P


def conv_back(nc, x, w, c, d, scan_out, gate, left, tokens, q_parts, k_parts, values):
    with ExitStack() as ctx:
        sb = lambda name, shape, dt=F32: ctx.enter_context(nc.sbuf_tensor("cb_" + name, shape, dt))
        pb = lambda name: ctx.enter_context(nc.psum_tensor("cb_" + name, [P, BANK], F32))
        sem = lambda name: ctx.enter_context(nc.semaphore("cb_" + name))
        y = [sb(f"y{k}", [P, TOK]) for k in range(DIRS)]
        x_tok, t_tok = sb("x_tok", [P, TILES, CH]), sb("t_tok", [P, TILES, CH])
        centre, square, normed, scaled = (sb(n, [P, 2, BANK]) for n in ("centre", "square", "normed", "scaled"))
        log_var, rstd = sb("log_var", [P, BANK]), sb("rstd", [P, BANK])
        gate_in, both, o_ch = (sb(n, [P, 2, BANK]) for n in ("gate_in", "both", "o_ch"))
        stats, moments = sb("stats", [P, TILES, 6]), sb("moments", [P, TILES, 2])
        t_log, t_rstd = sb("t_log", [P, TILES]), sb("t_rstd", [P, TILES])
        xn_tok = sb("xn_tok", [P, 2, BANK])
        xn_ch = sb("xn_ch", [P, 2, BANK])
        hi, mid, lo = (sb(n, [P, 2, BANK], BF16) for n in ("hi", "mid", "lo"))
        rest = sb("rest", [P, 2, BANK])
        v_sb = sb("v_sb", [P, 2, GROUPS, BLOCK_TILES, GROUP_HEADS, SLOT])
        eps = sb("eps", [P, 1])
        ps_mean, ps_var, ps_xr, ps_out, ps_tok, ps_xn, ps_q, ps_k = (
            pb(n) for n in ("ps_mean", "ps_var", "ps_xr", "ps_out", "ps_tok", "ps_xn", "ps_q", "ps_k"))
        ps_qk, ps_v = (ps_q, ps_k), ps_mean

        names = ("y_loaded x_loaded ready added mean_done centred squared var_done log_done rstd_done norm_done scale_done "
                 "gated xr_done xr_silu out_done out_silu tok_done t_added stats_done moments_done t_log_done t_rstd_done "
                 "xn_done xn_turned xn_copied q_done k_done v_done hi_done rest_done mid_done lo_done v_copied t_stored").split()
        (y_loaded, x_loaded, ready, added, mean_done, centred, squared, var_done, log_done, rstd_done, norm_done, scale_done,
         gated, xr_done, xr_silu, out_done, out_silu, tok_done, t_added, stats_done, moments_done, t_log_done, t_rstd_done,
         xn_done, xn_turned, xn_copied, q_done, k_done, v_done, hi_done, rest_done, mid_done, lo_done, v_copied, t_stored) = map(sem, names)
        gate_loaded, left_loaded, v_stored, qk_stored = ([sem(f"{n}{i}") for i in range(2)] for n in ("gate_loaded", "left_loaded", "v_stored", "qk_stored"))
        block = ctx.enter_context(nc.Block())
        cols = lambda g: slice(g * BANK, (g + 1) * BANK)

        @block.sync
        def _(sp):
            def load_y(b, k):
                sp.dma_start(y[k][:, :].rearrange("p (c t) -> p c t", t=STEP), scan_out[b, k]).then_inc(y_loaded, 16)

            def load_x(b):
                for tiles, rows in X_PARTS:
                    sp.dma_start(x_tok[:, tiles, :], x[b, rows].rearrange("(t p) c -> p t c", p=P)).then_inc(x_loaded, 16)

            for k in range(DIRS):
                load_y(0, k)
            load_x(0)
            with sp.Fori(0, IMAGES) as b:
                first = b * CHUNKS
                for g in range(CHUNKS):
                    sp.wait_ge(gated, first + max(g - 1, 0))
                    sp.dma_start(gate_in[:, g % 2, :], gate[b, :, cols(g)]).then_inc(gate_loaded[g % 2], 16)
                for g in range(CHUNKS):
                    sp.wait_ge(out_done, first + max(g - 1, 0))
                    sp.dma_start(both[0:HALF, g % 2, :], left[b, :, cols(g)]).then_inc(left_loaded[g % 2], 16)
                sp.wait_ge(xr_done, first + CHUNKS)
                for k in range(DIRS):
                    load_y((b + 1) % IMAGES, k)
                sp.wait_ge(t_added, first + CHUNKS)
                load_x((b + 1) % IMAGES)
                sp.dma_start(tokens.rearrange("(b g) p t -> b p g t", g=CHUNKS)[b],
                             t_tok[:, :, :].rearrange("p (g t) c -> p g (t c)", g=CHUNKS)).then_inc(t_stored, 16)
                for g in range(CHUNKS):
                    i = g % 2
                    for s, dram in ((0, q_parts), (1, k_parts)):
                        sp.wait_ge(lo_done, 2 * (first + g) + s + 1)
                        for part, tile in enumerate((hi, mid, lo)):
                            sp.dma_start(dram[b, part, :, cols(g)], tile[:, s, :]).then_inc(qk_stored[s], 16)
                    sp.wait_ge(v_copied, first + g + 1)
                    for r in range(GROUPS):
                        sp.dma_start(values[b, r, :, g * BLOCK_TILES:(g + 1) * BLOCK_TILES, :],
                                     v_sb[:, i, r].rearrange("p t h v -> p t (h v)")).then_inc(v_stored[i], 16)
            sp.wait_ge(y_loaded, 16 * DIRS * (IMAGES + 1))
            sp.wait_ge(x_loaded, X_COUNT * (IMAGES + 1))
            sp.wait_ge(t_stored, 16 * IMAGES)
            for i in range(2):
                sp.wait_ge(qk_stored[i], 16 * PARTS * IMAGES * CHUNKS)
                sp.wait_ge(v_stored[i], 16 * GROUPS * IMAGES * CHUNKS // 2)

        @block.gpsimd
        def _(pool):
            nc.gpsimd.memset(v_sb[:, :, :, :, :, :], 0.0).then_inc(ready, 1)
            pool.wait_ge(ready, 1)
            nc.gpsimd.memset(v_sb[:, :, :, :, :, HEAD:HEAD + 1].rearrange("p a b t h v -> p (a b t h) v"), 1.0).then_inc(ready, 1)
            nc.gpsimd.memset(eps[:, :], LN_EPS_SCAN).then_inc(ready, 1)
            with pool.Fori(0, IMAGES) as b:
                first = b * CHUNKS
                for g in range(CHUNKS):
                    pool.wait_ge(scale_done, first + g + 1)
                    pool.wait_ge(gate_loaded[g % 2], (b * (CHUNKS // 2) + g // 2) * 16 + 16)
                    nc.gpsimd.tensor_tensor(y[2][:, cols(g)], scaled[:, g % 2, :], gate_in[:, g % 2, :], ALU.mult).then_inc(gated, 1)
                for g in range(CHUNKS):
                    for s in range(2):
                        n = 2 * (first + g) + s
                        pool.wait_ge(mid_done, n + 1)
                        pool.wait_ge(qk_stored[s], (first + g) * 16 * PARTS)
                        nc.gpsimd.tensor_tensor(lo[:, s, :], rest[:, s, :], mid[:, s, :], ALU.subtract).then_inc(lo_done, 1)

        @block.tensor
        def _(pe):
            ident, mean = CONSTANTS.of(c, "ident"), CONSTANTS.of(c, "mean")
            cv_out, cv3, qkv = DERIVED.of(d, "cv_out"), WEIGHTS.of(w, "cv3"), WEIGHTS.of(w, "qkv")
            with pe.Fori(0, IMAGES) as b:
                first = b * CHUNKS
                pe.wait_ge(added, (b + 1) * 3)
                pe.wait_ge(v_copied, first)
                for g in range(CHUNKS + 1):
                    if g < CHUNKS:
                        pe.wait_ge(centred, first + g)
                        nc.tensor.matmul(ps_mean[:, :], mean, y[0][:, cols(g)], start=True, stop=True).then_inc(mean_done, 1)
                    if g:
                        pe.wait_ge(squared, first + g)
                        pe.wait_ge(log_done, first + g - 1)
                        nc.tensor.matmul(ps_var[:, :], mean, square[:, (g - 1) % 2, :], start=True, stop=True).then_inc(var_done, 1)
                for g in range(CHUNKS + 2):
                    if g < CHUNKS:
                        pe.wait_ge(gated, first + g + 1)
                        pe.wait_ge(xr_silu, first + g)
                        nc.tensor.matmul(ps_xr[:, :], cv_out, y[2][:, cols(g)], start=True, stop=True).then_inc(xr_done, 1)
                    if 0 < g < CHUNKS + 1:
                        h = g - 1
                        pe.wait_ge(xr_silu, first + h + 1)
                        pe.wait_ge(left_loaded[h % 2], (b * (CHUNKS // 2) + h // 2) * 16 + 16)
                        pe.wait_ge(out_silu, first + h)
                        nc.tensor.matmul(ps_out[:, :], cv3, both[:, h % 2, :], start=True, stop=True).then_inc(out_done, 1)
                    if g > 1:
                        h = g - 2
                        pe.wait_ge(out_silu, first + h + 1)
                        pe.wait_ge(t_added, first + h)
                        for t in range(BLOCK_TILES):
                            last = nc.tensor.transpose(ps_tok[:, t * P:(t + 1) * P], o_ch[:, h % 2, t * P:(t + 1) * P], ident)
                        last.then_inc(tok_done, 1)
                for g in range(CHUNKS + 1):
                    if g < CHUNKS:
                        pe.wait_ge(xn_done, first + g + 1)
                        pe.wait_ge(xn_copied, first + g)
                        for t in range(BLOCK_TILES):
                            last = nc.tensor.transpose(ps_xn[:, t * P:(t + 1) * P], xn_tok[:, g % 2, t * P:(t + 1) * P], ident)
                        last.then_inc(xn_turned, 1)
                    if g:
                        h = g - 1
                        pe.wait_ge(xn_copied, first + h + 1)
                        for s, done in ((0, q_done), (1, k_done)):
                            pe.wait_ge(rest_done, 2 * (first + h) - 1 + s if h else 2 * first)
                            nc.tensor.matmul(ps_qk[s][:, :], qkv[:, s * P:(s + 1) * P], xn_ch[:, h % 2, :], start=True, stop=True).then_inc(done, 1)
                        pe.wait_ge(v_copied, first + h)
                        for t in range(BLOCK_TILES):
                            last = nc.tensor.matmul(ps_v[:, t * P:(t + 1) * P], xn_ch[:, h % 2, t * P:(t + 1) * P],
                                                    qkv[:, 2 * P:3 * P], start=True, stop=True)
                        last.then_inc(v_done, 1)

        @block.scalar
        def _(act):
            act.wait_ge(ready, 3)
            with act.Fori(0, IMAGES) as b:
                first = b * CHUNKS
                for g in range(CHUNKS + 1):
                    if g < CHUNKS:
                        act.wait_ge(centred, first + g + 1)
                        act.wait_ge(var_done, first + max(g - 1, 0))
                        nc.scalar.activation(square[:, g % 2, :], centre[:, g % 2, :], ACT.Square).then_inc(squared, 1)
                    if g:
                        h = g - 1
                        act.wait_ge(var_done, first + h + 1)
                        act.wait_ge(rstd_done, first + h)
                        nc.scalar.activation(log_var[:, :], ps_var[:, :], ACT.Ln, bias=eps[:, :]).then_inc(log_done, 1)
                        act.wait_ge(log_done, first + h + 1)
                        act.wait_ge(norm_done, first + h)
                        nc.scalar.activation(rstd[:, :], log_var[:, :], ACT.Exp, scale=-0.5).then_inc(rstd_done, 1)
                        act.wait_ge(norm_done, first + h + 1)
                        act.wait_ge(gated, first + max(h - 1, 0))
                        nc.scalar.activation(scaled[:, h % 2, :], normed[:, h % 2, :], ACT.Identity, bias=WEIGHTS.of(w, "ln_b"),
                                             scale=WEIGHTS.of(w, "ln_g")).then_inc(scale_done, 1)
                for g in range(CHUNKS + 1):
                    if g < CHUNKS:
                        act.wait_ge(xr_done, first + g + 1)
                        act.wait_ge(out_done, first + max(g - 1, 0))
                        nc.scalar.activation(both[HALF:P, g % 2, :], ps_xr[HALF:P, :], ACT.Silu, bias=WEIGHTS.of(w, "cv_b", start=HALF),
                                             scale=WEIGHTS.of(w, "cv_g", start=HALF)).then_inc(xr_silu, 1)
                    if g:
                        h = g - 1
                        act.wait_ge(out_done, first + h + 1)
                        act.wait_ge(tok_done, first + max(h - 1, 0))
                        nc.scalar.activation(o_ch[:, h % 2, :], ps_out[:, :], ACT.Silu, bias=WEIGHTS.of(w, "cv3_b"),
                                             scale=WEIGHTS.of(w, "cv3_g")).then_inc(out_silu, 1)
                act.wait_ge(moments_done, (b + 1) * TILES)
                act.wait_ge(t_rstd_done, b)
                nc.scalar.activation(t_log[:, :], moments[:, :, 1], ACT.Ln, bias=eps[:, :]).then_inc(t_log_done, 1)
                act.wait_ge(t_log_done, b + 1)
                act.wait_ge(xn_done, first)
                nc.scalar.activation(t_rstd[:, :], t_log[:, :], ACT.Exp, scale=-0.5).then_inc(t_rstd_done, 1)
                for g in range(CHUNKS):
                    act.wait_ge(xn_turned, first + g + 1)
                    act.wait_ge(v_done, first + max(g - 1, 0))
                    nc.scalar.activation(xn_ch[:, g % 2, :], ps_xn[:, :], ACT.Copy).then_inc(xn_copied, 1)
                    for s, done in ((0, q_done), (1, k_done)):
                        n = 2 * (first + g) + s
                        act.wait_ge(done, first + g + 1)
                        act.wait_ge(qk_stored[s], (first + g) * 16 * PARTS)
                        nc.scalar.activation(hi[:, s, :], ps_qk[s][:, :], ACT.Copy, scale=HEAD_SCALE if s == 0 else 1.0).then_inc(hi_done, 1)
                    for s in range(2):
                        n = 2 * (first + g) + s
                        act.wait_ge(rest_done, n + 1)
                        nc.scalar.activation(mid[:, s, :], rest[:, s, :], ACT.Copy).then_inc(mid_done, 1)
                    act.wait_ge(v_done, first + g + 1)
                    act.wait_ge(v_stored[g % 2], (b * (CHUNKS // 2) + g // 2) * 16 * GROUPS)
                    for r in range(GROUPS):
                        last = nc.scalar.activation(
                            v_sb[:, g % 2, r, :, :, 0:HEAD],
                            ps_v[:, :].rearrange("p (t r h v) -> p r t h v", r=GROUPS, h=GROUP_HEADS, v=HEAD)[:, r], ACT.Copy)
                    last.then_inc(v_copied, 1)

        @block.vector
        def _(dve):
            dve.wait_ge(ready, 3)
            with dve.Fori(0, IMAGES) as b:
                first = b * CHUNKS
                dve.wait_ge(y_loaded, b * 16 * DIRS + 16 * DIRS)
                nc.vector.tensor_tensor(y[0][:, :], y[0][:, :], y[2][:, ::-1], ALU.add).then_inc(added, 1)
                nc.vector.tensor_tensor(y[1][:, :], y[1][:, :], y[3][:, ::-1], ALU.add).then_inc(added, 1)
                dve.wait_ge(added, b * 3 + 2)
                rows = y[0][:, :].rearrange("p (r s) -> p r s", s=SIDE)
                nc.vector.tensor_tensor(rows, rows, y[1][:, :].rearrange("p (s r) -> p r s", r=SIDE), ALU.add).then_inc(added, 1)
                for g in range(CHUNKS + 1):
                    if g < CHUNKS:
                        dve.wait_ge(mean_done, first + g + 1)
                        dve.wait_ge(squared, first + max(g - 1, 0))
                        dve.wait_ge(norm_done, first + max(g - 1, 0))
                        nc.vector.tensor_tensor(centre[:, g % 2, :], y[0][:, cols(g)], ps_mean[:, :], ALU.subtract).then_inc(centred, 1)
                    if g:
                        h = g - 1
                        dve.wait_ge(rstd_done, first + h + 1)
                        dve.wait_ge(scale_done, first + max(h - 1, 0))
                        nc.vector.tensor_tensor(normed[:, h % 2, :], centre[:, h % 2, :], rstd[:, :], ALU.mult).then_inc(norm_done, 1)
                dve.wait_ge(x_loaded, b * X_COUNT + X_COUNT)
                dve.wait_ge(t_stored, b * 16)
                dve.wait_ge(xn_done, first)
                for g in range(CHUNKS):
                    tiles = slice(g * BLOCK_TILES, (g + 1) * BLOCK_TILES)
                    dve.wait_ge(tok_done, first + g + 1)
                    nc.vector.tensor_tensor(t_tok[:, tiles, :], x_tok[:, tiles, :], ps_tok[:, :].rearrange("p (t c) -> p t c", c=CH),
                                            ALU.add).then_inc(t_added, 1)
                    dve.wait_ge(t_added, first + g + 1)
                    dve.wait_ge(t_log_done, b)
                    for t in range(g * BLOCK_TILES, (g + 1) * BLOCK_TILES):
                        nc.vector.bn_stats(stats[:, t, :], t_tok[:, t, :]).then_inc(stats_done, 1)
                    stats_done_due = worked_out(dve, b * TILES + (g + 1) * BLOCK_TILES)
                    dve.wait_ge(ready, 3)
                    dve.wait_ge(stats_done, stats_done_due)
                    for t in range(g * BLOCK_TILES, (g + 1) * BLOCK_TILES):
                        nc.vector.bn_aggr(moments[:, t, :], stats[:, t, :]).then_inc(moments_done, 1)
                dve.wait_ge(moments_done, (b + 1) * TILES)
                dve.wait_ge(t_rstd_done, b + 1)
                for g in range(CHUNKS + 1):
                    if g < CHUNKS:
                        dve.wait_ge(xn_turned, first + max(g - 1, 0))
                        for t in range(BLOCK_TILES):
                            n = g * BLOCK_TILES + t
                            last = nc.vector.tensor_scalar(xn_tok[:, g % 2, t * P:(t + 1) * P], t_tok[:, n, :], moments[:, n, 0:1],
                                                           t_rstd[:, n:n + 1], ALU.subtract, ALU.mult)
                        last.then_inc(xn_done, 1)
                    if g:
                        h = g - 1
                        for s in range(2):
                            n = 2 * (first + h) + s
                            dve.wait_ge(hi_done, n + 1)
                            dve.wait_ge(lo_done, n - 1 if h or s else 2 * first)
                            nc.vector.scalar_tensor_tensor(out=rest[:, s, :], in0=ps_qk[s][:, :], scalar=HEAD_SCALE if s == 0 else 1.0,
                                                           in1=hi[:, s, :], op0=ALU.mult, op1=ALU.subtract).then_inc(rest_done, 1)


Q_PARTS, K_PARTS = (0, 0, 1, 0, 1, 2), (0, 1, 0, 2, 1, 0)
SCORE_ROWS = HEAD * len(Q_PARTS)
ROWS_MAX = SCORE_ROWS + PARTS
UNITS = IMAGES * GROUPS
QBLOCKS = TOK // BANK
BLOCK_STEPS = [BLOCK_TILES * (i + 1) for i in range(QBLOCKS)]
STEPS = [BLOCK_TILES * i * (i + 1) // 2 for i in range(QBLOCKS + 1)]
TOP = GROUP_HEADS * BLOCK_TILES
Q_AHEAD = QBLOCKS // 2
AHEAD = 3
TARGETS = [(j + AHEAD) % QBLOCKS for j in range(QBLOCKS)]
ITEMS = [(j, kk, n) for j in TARGETS for kk in range(j + 1) for n in range(TOP)]
OWN_ITEMS = sum(TOP * (j + 1) for j in range(AHEAD, QBLOCKS))
OWN_STEPS = STEPS[QBLOCKS - 1] - 6
NEXT_START, NEXT_END = STEPS[QBLOCKS - 1] + 10, STEPS[QBLOCKS] - 2
K_CHUNKS = [(0, 1), (1, 2), (2, 3), (3, 4), (4, QBLOCKS)]
STEP_COLUMNS = [P + P * (BLOCK_TILES - max(0, y - i * BLOCK_TILES)) - (P if i and 1 <= y <= BLOCK_TILES else 0) for i in range(QBLOCKS) for y in range(BLOCK_STEPS[i])]


def items_until(x):
    columns = lambda a, b: sum(STEP_COLUMNS[a:b])
    own = OWN_ITEMS * columns(0, min(x, OWN_STEPS)) // columns(0, OWN_STEPS)
    after = columns(NEXT_START, min(x, NEXT_END)) if x > NEXT_START else 0
    return own + (len(ITEMS) - OWN_ITEMS) * after // columns(NEXT_START, NEXT_END)


def items_of(x):
    return [(m, *ITEMS[m]) for m in range(items_until(x), items_until(x + 1))]


def completed(x):
    return [(k, j) for k, j in enumerate(TARGETS)
            if x >= 0 and items_until(x) < sum(TOP * (t + 1) for t in TARGETS[:k + 1]) <= items_until(x + 1)]


def attention(nc, c, c16, q_parts, k_parts, values, maxima, attended):
    with ExitStack() as ctx:
        sb = lambda name, shape, dt=F32: ctx.enter_context(nc.sbuf_tensor("at_" + name, shape, dt))
        pb = lambda name, n=BANK: ctx.enter_context(nc.psum_tensor("at_" + name, [P, n], F32))
        sem = lambda name: ctx.enter_context(nc.semaphore("at_" + name))
        k_sb = sb("k_sb", [ROWS_MAX, GROUP_HEADS, TOK], BF16)
        q_sb = sb("q_sb", [ROWS_MAX, QBLOCKS, GROUP_HEADS, BANK], BF16)
        v_sb = sb("v_sb", [P, TILES, P])
        weights = sb("weights", [P, 2, 2, 2, BANK])
        top, neg = sb("top", [P, TOP, QBLOCKS]), sb("neg", [P, TOP])
        m_rest, m_row = sb("m_rest", [TOP, P]), sb("m_row", [TOP, PARTS, P], BF16)
        o_sb, inverse, o_out = sb("o_sb", [P, BANK]), sb("inverse", [P, BANK]), sb("o_out", [P, BANK])
        ps_s = [pb(f"ps_s{i}", 2 * BANK) for i in range(2)]
        ps_m = [pb(f"ps_m{i}") for i in range(2)]
        ps_o, ps_x = pb("ps_o"), pb("ps_x")
        names = ("ones k_loaded q_loaded v_loaded scored weighed summed max_scored maxed negated turned "
                 "m_hi_done m_rest_done m_mid_done m_lo_done m_stored m_loaded o_copied sums_done inverted scaled o_stored").split()
        (ones, k_loaded, q_loaded, v_loaded, scored, weighed, summed, max_scored, maxed, negated, turned,
         m_hi_done, m_rest_done, m_mid_done, m_lo_done, m_stored, m_loaded, o_copied, sums_done, inverted, scaled, o_stored) = map(sem, names)
        block = ctx.enter_context(nc.Block())
        PROLOGUE = TOP * AHEAD * (AHEAD + 1) // 2
        PROLOGUE_ITEMS = [(m, j, kk, n) for m, (j, kk, n) in
                          enumerate((j, kk, n) for j in range(AHEAD) for kk in range(j + 1) for n in range(TOP))]
        Q_COUNT, K_COUNT = 16 * len(Q_PARTS), 16 * len(K_PARTS)

        def at_least(engine, semaphore, value):
            if not isinstance(value, int) or value > 0:
                engine.wait_ge(semaphore, value)

        def step(u, x):
            return u * STEPS[-1] + x

        def block_of(u, i):
            return u * QBLOCKS + i

        def item(u, m):
            return u * len(ITEMS) + (PROLOGUE + m)

        def target(u, k):
            return u * QBLOCKS + (AHEAD + k)

        @block.sync
        def _(sp):
            def load_k(u, first, end):
                source = k_parts.rearrange("b s (r h d) t -> b r s d h t", r=GROUPS, h=GROUP_HEADS)[u // GROUPS, u % GROUPS]
                for g, part in enumerate(K_PARTS):
                    sp.dma_start(k_sb[g * HEAD:(g + 1) * HEAD, :, first * BANK:end * BANK],
                                 source[part, :, :, first * BANK:end * BANK]).then_inc(k_loaded, 16)
                tiles = slice(first * BLOCK_TILES, end * BLOCK_TILES)
                sp.dma_start(v_sb[:, tiles, :], values[u // GROUPS, u % GROUPS, :, tiles, :]).then_inc(v_loaded, 16)

            def load_q(u, i):
                source = q_parts.rearrange("b s (r h d) t -> b r s d h t", r=GROUPS, h=GROUP_HEADS)[u // GROUPS, u % GROUPS]
                for g, part in enumerate(Q_PARTS):
                    sp.dma_start(q_sb[g * HEAD:(g + 1) * HEAD, i], source[part, :, :, i * BANK:(i + 1) * BANK]).then_inc(q_loaded, 16)

            def move_maxima(number, i):
                at_least(sp, m_loaded, number * 16)
                sp.wait_ge(m_lo_done, number + 1)
                sp.dma_start(maxima, m_row[:, :, :]).then_inc(m_stored, 16)
                sp.wait_ge(m_stored, number * 16 + 16)
                sp.dma_start(q_sb[SCORE_ROWS:ROWS_MAX, i].rearrange("s h (t q) -> s (h t) q", q=P),
                             maxima.rearrange("n s q -> s n q")).then_inc(m_loaded, 16)

            for i in range(AHEAD):
                at_least(sp, q_loaded, i * Q_COUNT)
                load_q(0, i)
                at_least(sp, k_loaded, i * K_COUNT)
                at_least(sp, v_loaded, i * 16)
                load_k(0, *K_CHUNKS[i])
            sp.wait_ge(k_loaded, AHEAD * K_COUNT)
            sp.wait_ge(v_loaded, AHEAD * 16)
            load_k(0, *K_CHUNKS[AHEAD])
            for i in range(AHEAD, Q_AHEAD):
                sp.wait_ge(q_loaded, i * Q_COUNT)
                load_q(0, i)
            for i in range(AHEAD):
                move_maxima(i, i)
            with sp.Fori(0, UNITS) as u:
                nc.cur_bb.disable_value_cache()
                for i in range(QBLOCKS):
                    n = block_of(u, i)
                    q_loaded_due, summed_due = worked_out(sp, (n + Q_AHEAD) * Q_COUNT), worked_out(sp, step(u, STEPS[i]))
                    sp.wait_ge(v_loaded, 16)
                    sp.wait_ge(q_loaded, q_loaded_due)
                    sp.wait_ge(summed, summed_due)
                    load_q((u + 1) % UNITS if i + Q_AHEAD >= QBLOCKS else u, (i + Q_AHEAD) % QBLOCKS)
                    if i == 0:
                        sp.wait_ge(k_loaded, (u * len(K_CHUNKS) + (AHEAD + 1)) * K_COUNT)
                        sp.wait_ge(v_loaded, (u * len(K_CHUNKS) + (AHEAD + 1)) * 16)
                        load_k(u, *K_CHUNKS[AHEAD + 1])
                    moves = [(k, j) for x in range(STEPS[i], STEPS[i + 1]) for k, j in completed(x - 2)]
                    for g in range(AHEAD + 1):
                        if i == QBLOCKS - 1:
                            sp.wait_ge(k_loaded, (u * len(K_CHUNKS) + (len(K_CHUNKS) + g)) * K_COUNT)
                            sp.wait_ge(v_loaded, (u * len(K_CHUNKS) + (len(K_CHUNKS) + g)) * 16)
                            sp.wait_ge(summed, step(u, STEPS[i] + K_CHUNKS[g][1] * BLOCK_TILES))
                            load_k((u + 1) % UNITS, *K_CHUNKS[g])
                            for k, j in moves:
                                if j == g - 2:
                                    move_maxima(target(u, k), j)
                    for k, j in moves:
                        if i < QBLOCKS - 1 or j not in (0, 1):
                            move_maxima(target(u, k), j)
                    sp.wait_ge(scaled, n + 1)
                    sp.dma_start(attended[u % GROUPS, (u // GROUPS) * QBLOCKS + i], o_out[:, :]).then_inc(o_stored, 16)
            sp.wait_ge(o_stored, 16 * UNITS * QBLOCKS)
            sp.wait_ge(m_loaded, 16 * (UNITS * QBLOCKS + AHEAD))
            sp.wait_ge(q_loaded, Q_COUNT * (UNITS * QBLOCKS + Q_AHEAD))
            sp.wait_ge(k_loaded, K_COUNT * (UNITS * len(K_CHUNKS) + (AHEAD + 1)))
            sp.wait_ge(v_loaded, 16 * (UNITS * len(K_CHUNKS) + (AHEAD + 1)))

        @block.tensor
        def _(pe):
            ident, head_sum = CONSTANTS.of(c, "ident"), CONSTANTS.of(c, "head_sum")
            ident16, above, below = (CONSTANTS16.of(c16, n) for n in ("ident", "above", "below"))

            def max_scores(number, m, i, kk, n):
                h, t = n // BLOCK_TILES, n % BLOCK_TILES
                diag = kk == i
                width = (t + 1) * P if diag else BANK
                at_least(pe, maxed, number - 1)
                out = ps_m[m % 2]
                last = nc.tensor.matmul(out[:, 0:width], q_sb[0:SCORE_ROWS, i, h, t * P:(t + 1) * P],
                                        k_sb[0:SCORE_ROWS, h, kk * BANK:kk * BANK + width], start=True, stop=not diag)
                if diag:
                    last = nc.tensor.matmul(out[:, width - P:width], ident16, below, start=False, stop=True)
                last.then_inc(max_scored, 1)

            def unit_max_scores(u, items):
                for m, j, kk, n in items:
                    if kk == 0 and n == 0:
                        pe.wait_ge(q_loaded, (target(u, TARGETS.index(j)) + 1) * Q_COUNT)
                        if j < AHEAD:
                            pe.wait_ge(k_loaded, (u * len(K_CHUNKS) + (len(K_CHUNKS) + 1 + j)) * K_COUNT)
                    if n == 0 and kk == j and j in (AHEAD, AHEAD + 1):
                        pe.wait_ge(k_loaded, (u * len(K_CHUNKS) + (j + 1)) * K_COUNT)
                    max_scores(item(u, m), m, j, kk, n)

            def scores(u, i, y, p):
                diag, off = y >= i * BLOCK_TILES, max(0, y - i * BLOCK_TILES) * P
                pe.wait_ge(weighed, (step(u, STEPS[i] + y) * 2) - 1 + p) if (i or y) else at_least(pe, weighed, step(u, 0) * 2)
                for h in (2 * p, 2 * p + 1):
                    out = ps_s[p][:, (h % 2) * BANK + off:(h % 2 + 1) * BANK]
                    last = nc.tensor.matmul(out, k_sb[:, h, y * P:(y + 1) * P], q_sb[:, i, h, off:BANK], start=True, stop=not diag)
                    if diag:
                        last = nc.tensor.matmul(out[:, 0:P], ident16, above, start=False, stop=True)
                last.then_inc(scored, 1)

            def weighted_sum(u, i, y):
                off = max(0, y - i * BLOCK_TILES) * P
                end = y + 1 == BLOCK_STEPS[i]
                if end:
                    pe.wait_ge(weighed, step(u, STEPS[i] + y) * 2 + 2)
                if y == 0:
                    at_least(pe, o_copied, block_of(u, i))
                for h in range(GROUP_HEADS):
                    last = nc.tensor.matmul(ps_o[h * SLOT:(h + 1) * SLOT, off:BANK], v_sb[:, y, h * SLOT:(h + 1) * SLOT],
                                            weights[:, y % 2, h // 2, h % 2, off:BANK], start=(y == 0), stop=end, skip_group_check=True)
                last.then_inc(summed, 1)

            def turn_maxima(number, blocks_done):
                pe.wait_ge(negated, number + 1)
                at_least(pe, m_rest_done, number)
                at_least(pe, inverted, blocks_done * BLOCK_TILES)
                nc.tensor.transpose(ps_x[0:TOP, 0:P], neg[:, :], ident).then_inc(turned, 1)

            def head_sums(u, i):
                n = block_of(u, i)
                pe.wait_ge(o_copied, n + 1)
                turns = sum(len(completed(z)) for z in range(STEPS[i + 1] if i + 1 < QBLOCKS else STEPS[-1] - 1))
                pe.wait_ge(m_rest_done, target(u, turns))
                at_least(pe, inverted, n * BLOCK_TILES)
                nc.tensor.matmul(ps_x[:, :], head_sum, o_sb[:, :], start=True, stop=True).then_inc(sums_done, 1)

            pe.wait_ge(ones, 1)
            for m, j, kk, n in PROLOGUE_ITEMS:
                if kk == 0 and n == 0:
                    pe.wait_ge(q_loaded, (j + 1) * Q_COUNT)
                    pe.wait_ge(k_loaded, (j + 1) * K_COUNT)
                max_scores(m, m, j, kk, n)
                if kk == j and n == TOP - 1:
                    turn_maxima(j, 0)
            with pe.Fori(0, UNITS) as u:
                nc.cur_bb.disable_value_cache()
                for i in range(QBLOCKS):
                    pe.wait_ge(m_loaded, block_of(u, i) * 16 + 16)
                    if i in (0, AHEAD, AHEAD + 1):
                        pe.wait_ge(v_loaded, (u * len(K_CHUNKS) + (i + 1 if i else AHEAD)) * 16)
                    for p in range(2):
                        scores(u, i, 0, p)
                    for y in range(BLOCK_STEPS[i]):
                        x = STEPS[i] + y
                        items = items_of(x)
                        early = min(2, len(items))
                        late = max(early, len(items) - 2)
                        unit_max_scores(u, items[:early])
                        if y + 1 < BLOCK_STEPS[i]:
                            scores(u, i, y + 1, 0)
                        for k, _ in completed(x - 1):
                            turn_maxima(target(u, k), block_of(u, i) - (1 if y == 0 and i else 0))
                        unit_max_scores(u, items[early:late])
                        if y + 1 < BLOCK_STEPS[i]:
                            scores(u, i, y + 1, 1)
                        unit_max_scores(u, items[late:])
                        weighted_sum(u, i, y)
                        if y == 0 and i:
                            head_sums(u, i - 1)
                head_sums(u, QBLOCKS - 1)

        @block.scalar
        def _(act):
            def weigh(u, i, y):
                s = step(u, STEPS[i] + y)
                off = max(0, y - i * BLOCK_TILES) * P
                if STEPS[i] + y >= 2:
                    act.wait_ge(summed, s - 1)
                else:
                    act.wait_ge(summed, step(u, 0))
                for p in range(2):
                    act.wait_ge(scored, s * 2 + p + 1)
                    nc.scalar.activation(weights[:, y % 2, p, :, off:BANK], ps_s[p][:, :].rearrange("p (h q) -> p h q", q=BANK)[:, :, off:BANK],
                                         ACT.Exp).then_inc(weighed, 1)

            def first_part(number):
                act.wait_ge(turned, number + 1)
                at_least(act, m_stored, number * 16)
                nc.scalar.activation(m_row[:, 0, :], ps_x[0:TOP, 0:P], ACT.Copy).then_inc(m_hi_done, 1)

            def second_part(number):
                act.wait_ge(m_rest_done, number + 1)
                nc.scalar.activation(m_row[:, 1, :], m_rest[:, :], ACT.Copy).then_inc(m_mid_done, 1)

            for k in range(AHEAD):
                first_part(k)
                second_part(k)
            with act.Fori(0, UNITS) as u:
                nc.cur_bb.disable_value_cache()
                for i in range(QBLOCKS):
                    for y in range(BLOCK_STEPS[i]):
                        x = STEPS[i] + y
                        weigh(u, i, y)
                        for k, _ in completed(x - 2):
                            second_part(target(u, k))
                        for k, _ in completed(x - 1):
                            first_part(target(u, k))
                    act.wait_ge(summed, step(u, STEPS[i + 1]))
                    at_least(act, scaled, block_of(u, i))
                    act.wait_ge(sums_done, block_of(u, i))
                    nc.scalar.activation(o_sb[:, :], ps_o[:, :], ACT.Copy).then_inc(o_copied, 1)

        @block.gpsimd
        def _(pool):
            nc.gpsimd.memset(k_sb[SCORE_ROWS:ROWS_MAX, :, :], 1.0).then_inc(ones, 1)
            with pool.Fori(0, UNITS * QBLOCKS) as n:
                pool.wait_ge(inverted, n * BLOCK_TILES + BLOCK_TILES)
                pool.wait_ge(o_stored, n * 16)
                nc.gpsimd.tensor_tensor(o_out[:, :], o_sb[:, :], inverse[:, :], ALU.mult).then_inc(scaled, 1)

        @block.vector
        def _(dve):
            def maximum(number, m, i, kk, n):
                t = n % BLOCK_TILES
                width = (t + 1) * P if kk == i else BANK
                dve.wait_ge(max_scored, number + 1)
                nc.vector.reduce_max(top[:, n, kk:kk + 1], ps_m[m % 2][:, 0:width], AX.X).then_inc(maxed, 1)

            def negate_maxima(count, number, i):
                dve.wait_ge(maxed, count)
                at_least(dve, turned, number)
                nc.vector.tensor_reduce(neg[:, :], top[:, :, 0:i + 1], AX.X, ALU.max, negate=True).then_inc(negated, 1)

            def after_first_part(number):
                dve.wait_ge(m_hi_done, number + 1)
                at_least(dve, m_lo_done, number)
                nc.vector.tensor_tensor(m_rest[:, :], ps_x[0:TOP, 0:P], m_row[:, 0, :], ALU.subtract).then_inc(m_rest_done, 1)

            def third_part(number):
                dve.wait_ge(m_mid_done, number + 1)
                nc.vector.tensor_tensor(m_row[:, 2, :], m_rest[:, :], m_row[:, 1, :], ALU.subtract).then_inc(m_lo_done, 1)

            def invert(u, i, t):
                dve.wait_ge(sums_done, block_of(u, i) + 1)
                dve.wait_ge(scaled, block_of(u, i))
                nc.vector.reciprocal(inverse[:, t * P:(t + 1) * P], ps_x[:, t * P:(t + 1) * P]).then_inc(inverted, 1)

            def parts_at(i, y):
                turns = [z for z in range(1, BLOCK_TILES + 1) if completed(STEPS[i] + z - 1)]
                last = min([BLOCK_TILES] + turns)
                return [t for t in range(BLOCK_TILES) if i and min(t + 1, last) == y]

            def unit_maxima(u, items):
                for m, j, kk, n in items:
                    if kk == 0 and n == 0:
                        dve.wait_ge(negated, target(u, TARGETS.index(j)))
                    maximum(item(u, m), m, j, kk, n)
                    if kk == j and n == TOP - 1:
                        negate_maxima(item(u, m + 1), target(u, TARGETS.index(j)), j)

            for m, j, kk, n in PROLOGUE_ITEMS:
                if kk == 0 and n == 0:
                    at_least(dve, negated, j)
                maximum(m, m, j, kk, n)
                if kk == j and n == TOP - 1:
                    negate_maxima(m + 1, j, j)
                    after_first_part(j)
                    third_part(j)
            with dve.Fori(0, UNITS) as u:
                nc.cur_bb.disable_value_cache()
                for i in range(QBLOCKS):
                    for y in range(BLOCK_STEPS[i]):
                        x = STEPS[i] + y
                        items = items_of(x)
                        unit_maxima(u, items[:2])
                        for t in parts_at(i, y):
                            invert(u, i - 1, t)
                        for k, _ in completed(x - 1):
                            after_first_part(target(u, k))
                        for k, _ in completed(x - 2):
                            third_part(target(u, k))
                        unit_maxima(u, items[2:])
                for t in range(BLOCK_TILES):
                    invert(u, QBLOCKS - 1, t)


ALL_BLOCKS = IMAGES * CHUNKS


def experts(nc, w, c, c16, bias16, attended, tokens, out):
    with ExitStack() as ctx:
        sb = lambda name, shape, dt=F32: ctx.enter_context(nc.sbuf_tensor("ex_" + name, shape, dt))
        pb = lambda name, n=BANK: ctx.enter_context(nc.psum_tensor("ex_" + name, [P, n], F32))
        sem = lambda name: ctx.enter_context(nc.semaphore("ex_" + name))
        att, tok = sb("att", [P, 2, GROUPS, BANK]), sb("tok", [P, 2, BANK])
        t_sb, xn_tok, xn_ch = sb("t_sb", [P, 2, BANK]), sb("xn_tok", [P, BANK]), sb("xn_ch", [P, 2, BANK])
        stats, moments = sb("stats", [P, BLOCK_TILES, 6]), sb("moments", [P, BLOCK_TILES, 2])
        log_var, rstd, eps = sb("log_var", [P, BLOCK_TILES]), sb("rstd", [P, BLOCK_TILES]), sb("eps", [P, 1])
        tile_by = lambda name, n, dt=F32: sb(name, [P, BLOCK_TILES, n], dt)
        logits, best, index = tile_by("logits", EXPERTS), tile_by("best", 8), tile_by("index", 8, mybir.dt.uint32)
        index_f, order = tile_by("index_f", 8), sb("order", [P, EXPERTS])
        order_i = sb("order_i", [P, EXPERTS], mybir.dt.int32)
        is_first, is_second, first_w, second_w = (tile_by(n, EXPERTS) for n in ("is_first", "is_second", "first_w", "second_w"))
        gap, ratio, total, share1, share2 = (sb(n, [P, BLOCK_TILES]) for n in ("gap", "ratio", "total", "share1", "share2"))
        mix = sb("mix", [P, 2, BLOCK_TILES, EXPERTS])
        product = sb("product", [P, 2, EXPERTS * CH])
        half, quarter = sb("half", [P, 2, EXPERTS * CH // 2]), sb("quarter", [P, 2, EXPERTS * CH // 4])
        mixed, out_sb = sb("mixed", [P, 2, BANK]), sb("out_sb", [P, 2, BANK])
        ps_proj, ps_xn, ps_router = pb("ps_proj"), pb("ps_xn"), pb("ps_router")
        ps_e = [pb(f"ps_e{i}", 2 * BANK) for i in range(2)]
        names = ("ready att_loaded tok_loaded projected added stats_done moments_done log_done rstd_done xn_done xn_turned xn_copied "
                 "routed logits_done best_done index_done small second_done gap_done ratio_done mix_done expert_done product_done halved quartered "
                 "tile_mixed out_done").split()
        (ready, att_loaded, tok_loaded, projected, added, stats_done, moments_done, log_done, rstd_done, xn_done, xn_turned, xn_copied,
         routed, logits_done, best_done, index_done, small, second_done, gap_done, ratio_done, mix_done, expert_done, product_done, halved, quartered,
         tile_mixed, out_done) = map(sem, names)
        stored = [sem(f"stored{i}") for i in range(2)]
        block = ctx.enter_context(nc.Block())
        SMALL = 7
        tile_cols = lambda t: slice(t * P, (t + 1) * P)

        @block.sync
        def _(sp):
            def load(n, source, i):
                for r in range(GROUPS):
                    sp.dma_start(att[:, i, r, :], attended[r, source]).then_inc(att_loaded, 16)
                sp.dma_start(tok[:, i, :], tokens[source]).then_inc(tok_loaded, 16)

            load(0, 0, 0)
            with sp.Fori(0, ALL_BLOCKS // 2) as k:
                for i in range(2):
                    n = k * 2 + i
                    sp.wait_ge(att_loaded, n * (16 * GROUPS) + 16 * GROUPS)
                    sp.wait_ge(tok_loaded, n * 16 + 16)
                    sp.wait_ge(added, n)
                    load(n + 1, (n + 1) % ALL_BLOCKS, 1 - i)
                    sp.wait_ge(out_done, n + 1)
                    sp.dma_start(out[n], out_sb[:, i, :].rearrange("p (t c) -> p t c", c=CH)).then_inc(stored[i], 16)
            for i in range(2):
                sp.wait_ge(stored[i], 16 * ALL_BLOCKS // 2)
            sp.wait_ge(att_loaded, 16 * GROUPS * (ALL_BLOCKS + 1))
            sp.wait_ge(tok_loaded, 16 * (ALL_BLOCKS + 1))

        @block.tensor
        def _(pe):
            ident, w_proj = CONSTANTS.of(c, "ident"), WEIGHTS.of(w, "w_proj")
            router, expert_w, ones16 = WEIGHTS.of(w, "router"), WEIGHTS.of(w, "experts"), CONSTANTS16.of(c16, "ones")

            def project(n, i):
                pe.wait_ge(att_loaded, n * (16 * GROUPS) + 16 * GROUPS)
                pe.wait_ge(added, n)
                for t in range(BLOCK_TILES):
                    for r in range(GROUPS):
                        last = nc.tensor.matmul(ps_proj[:, tile_cols(t)], att[:, i, r, tile_cols(t)], w_proj[:, r * P:(r + 1) * P],
                                                start=(r == 0), stop=(r == GROUPS - 1))
                last.then_inc(projected, 1)

            def turn(n, i):
                pe.wait_ge(xn_done, n + 1)
                pe.wait_ge(xn_copied, n)
                for t in range(BLOCK_TILES):
                    last = nc.tensor.transpose(ps_xn[:, tile_cols(t)], xn_tok[:, tile_cols(t)], ident)
                last.then_inc(xn_turned, 1)

            def route(n, i):
                pe.wait_ge(xn_copied, n + 1)
                pe.wait_ge(logits_done, n)
                for t in range(BLOCK_TILES):
                    last = nc.tensor.matmul(ps_router[:, t * EXPERTS:(t + 1) * EXPERTS], xn_ch[:, i, tile_cols(t)], router,
                                            start=True, stop=True)
                last.then_inc(routed, 1)

            def expert_products(n, i, t):
                pe.wait_ge(product_done, n * BLOCK_TILES + max(t - 1, 0))
                for e in range(2):
                    columns = slice(e * BANK, (e + 1) * BANK)
                    nc.tensor.matmul(ps_e[t % 2][:, columns], xn_ch[:, i, tile_cols(t)], expert_w[:, columns], start=True, stop=False)
                    last = nc.tensor.matmul(ps_e[t % 2][:, columns], ones16, bias16[:, columns], start=False, stop=True)
                last.then_inc(expert_done, 1)

            pe.wait_ge(ready, 2)
            project(0, 0)
            turn(0, 0)
            route(0, 0)
            with pe.Fori(0, ALL_BLOCKS // 2) as k:
                for i in range(2):
                    n = k * 2 + i
                    project(n + 1, 1 - i)
                    expert_products(n, i, 0)
                    expert_products(n, i, 1)
                    turn(n + 1, 1 - i)
                    expert_products(n, i, 2)
                    route(n + 1, 1 - i)
                    expert_products(n, i, 3)

        @block.scalar
        def _(act):
            def front(n, i):
                act.wait_ge(moments_done, n * BLOCK_TILES + BLOCK_TILES)
                act.wait_ge(rstd_done, n)
                nc.scalar.activation(log_var[:, :], moments[:, :, 1], ACT.Ln, bias=eps[:, :]).then_inc(log_done, 1)
                act.wait_ge(log_done, n + 1)
                act.wait_ge(xn_done, n)
                nc.scalar.activation(rstd[:, :], log_var[:, :], ACT.Exp, scale=-0.5).then_inc(rstd_done, 1)
                act.wait_ge(xn_turned, n + 1)
                if not (isinstance(n, int) and n == 0):
                    act.wait_ge(expert_done, (n - 1) * BLOCK_TILES)
                nc.scalar.activation(xn_ch[:, i, :], ps_xn[:, :], ACT.Copy).then_inc(xn_copied, 1)
                act.wait_ge(gap_done, n + 1)
                nc.scalar.activation(ratio[:, :], gap[:, :], ACT.Exp).then_inc(ratio_done, 1)

            act.wait_ge(ready, 2)
            front(0, 0)
            with act.Fori(0, ALL_BLOCKS // 2) as k:
                for i in range(2):
                    front(k * 2 + i + 1, 1 - i)

        @block.gpsimd
        def _(pool):
            nc.gpsimd.memset(eps[:, :], LN_EPS).then_inc(ready, 1)
            nc.gpsimd.iota(order_i[:, :], pattern=[[1, EXPERTS]], base=0, channel_multiplier=0).then_inc(ready, 1)
            with pool.Fori(0, ALL_BLOCKS // 2) as k:
                for i in range(2):
                    n = k * 2 + i
                    for t in range(BLOCK_TILES):
                        s, m = t % 2, n * BLOCK_TILES + t
                        w2, w4 = EXPERTS * CH // 2, EXPERTS * CH // 4
                        pool.wait_ge(product_done, m + 1)
                        pool.wait_ge(quartered, n * BLOCK_TILES + max(t - 1, 0))
                        nc.gpsimd.tensor_tensor(half[:, s, :], product[:, s, 0:w2], product[:, s, w2:2 * w2], ALU.add).then_inc(halved, 1)
                        pool.wait_ge(halved, m + 1)
                        pool.wait_ge(tile_mixed, n * BLOCK_TILES + max(t - 1, 0))
                        nc.gpsimd.tensor_tensor(quarter[:, s, :], half[:, s, 0:w4], half[:, s, w4:2 * w4], ALU.add).then_inc(quartered, 1)
                        pool.wait_ge(quartered, m + 1)
                        pool.wait_ge(out_done, n)
                        nc.gpsimd.tensor_tensor(mixed[:, i, tile_cols(t)], quarter[:, s, 0:CH], quarter[:, s, CH:2 * CH], ALU.add).then_inc(tile_mixed, 1)

        @block.vector
        def _(dve):
            spread = lambda v: v.unsqueeze(2).to_broadcast([P, BLOCK_TILES, EXPERTS])

            def norm(n, i):
                dve.wait_ge(projected, n + 1)
                dve.wait_ge(tok_loaded, n * 16 + 16)
                if not (isinstance(n, int) and n == 0):
                    dve.wait_ge(out_done, n - 1)
                nc.vector.tensor_tensor(t_sb[:, i, :], tok[:, i, :], ps_proj[:, :], ALU.add).then_inc(added, 1)
                dve.wait_ge(added, n + 1)
                dve.wait_ge(moments_done, n * BLOCK_TILES)
                for t in range(BLOCK_TILES):
                    nc.vector.bn_stats(stats[:, t, :], t_sb[:, i, tile_cols(t)]).then_inc(stats_done, 1)
                stats_done_due = worked_out(dve, n * BLOCK_TILES + BLOCK_TILES)
                xn_done_due = worked_out(dve, n)
                dve.wait_ge(ready, 3)
                dve.wait_ge(stats_done, stats_done_due)
                dve.wait_ge(xn_done, xn_done_due)
                for t in range(BLOCK_TILES):
                    nc.vector.bn_aggr(moments[:, t, :], stats[:, t, :]).then_inc(moments_done, 1)

            def normalise(n, i):
                dve.wait_ge(rstd_done, n + 1)
                dve.wait_ge(moments_done, n * BLOCK_TILES + BLOCK_TILES)
                dve.wait_ge(xn_turned, n)
                for t in range(BLOCK_TILES):
                    last = nc.vector.tensor_scalar(xn_tok[:, tile_cols(t)], t_sb[:, i, tile_cols(t)], moments[:, t, 0:1], rstd[:, t:t + 1],
                                                   ALU.subtract, ALU.mult)
                last.then_inc(xn_done, 1)

            def choose(n, i):
                dve.wait_ge(routed, n + 1)
                dve.wait_ge(index_done, n * BLOCK_TILES)
                nc.vector.tensor_tensor(logits[:, :, :], ps_router[:, 0:BLOCK_TILES * EXPERTS].rearrange("p (t e) -> p t e", e=EXPERTS),
                                        WEIGHTS.of(w, "router_b").unsqueeze(1).to_broadcast([P, BLOCK_TILES, EXPERTS]), ALU.add).then_inc(logits_done, 1)
                logits_done_due = worked_out(dve, n + 1)
                gap_done_due = worked_out(dve, n)
                dve.wait_ge(ready, 3)
                dve.wait_ge(logits_done, logits_done_due)
                dve.wait_ge(gap_done, gap_done_due)
                for t in range(BLOCK_TILES):
                    nc.vector.max(best[:, t, :], logits[:, t, :]).then_inc(best_done, 1)
                best_done_due = worked_out(dve, n * BLOCK_TILES + BLOCK_TILES)
                small_due = worked_out(dve, n * SMALL)
                dve.wait_ge(ready, 3)
                dve.wait_ge(best_done, best_done_due)
                dve.wait_ge(small, small_due)
                for t in range(BLOCK_TILES):
                    nc.vector.max_index(index[:, t, :], best[:, t, :], logits[:, t, :]).then_inc(index_done, 1)
                dve.wait_ge(ratio_done, n)
                nc.vector.tensor_tensor(gap[:, :], best[:, :, 1], best[:, :, 0], ALU.subtract).then_inc(gap_done, 1)
                dve.wait_ge(index_done, n * BLOCK_TILES + BLOCK_TILES)
                nc.vector.tensor_copy(index_f[:, :, :], index[:, :, :]).then_inc(small, 1)
                dve.wait_ge(small, n * SMALL + 1)
                dve.wait_ge(mix_done, n)
                expert = order[:, :].unsqueeze(1).to_broadcast([P, BLOCK_TILES, EXPERTS])
                nc.vector.tensor_tensor(is_first[:, :, :], expert, spread(index_f[:, :, 0]), ALU.is_equal).then_inc(small, 1)
                nc.vector.tensor_tensor(is_second[:, :, :], expert, spread(index_f[:, :, 1]), ALU.is_equal).then_inc(small, 1)

            def shares(n, i):
                dve.wait_ge(ratio_done, n + 1)
                nc.vector.tensor_scalar(total[:, :], ratio[:, :], 1.0, None, ALU.add).then_inc(small, 1)
                dve.wait_ge(small, n * SMALL + 4)
                nc.vector.reciprocal(share1[:, :], total[:, :]).then_inc(small, 1)
                dve.wait_ge(small, n * SMALL + 5)
                nc.vector.tensor_tensor(share2[:, :], ratio[:, :], share1[:, :], ALU.mult).then_inc(small, 1)
                nc.vector.tensor_tensor(first_w[:, :, :], is_first[:, :, :], spread(share1[:, :]), ALU.mult).then_inc(small, 1)
                dve.wait_ge(small, n * SMALL + SMALL)
                nc.vector.tensor_tensor(second_w[:, :, :], is_second[:, :, :], spread(share2[:, :]), ALU.mult).then_inc(second_done, 1)
                dve.wait_ge(second_done, n + 1)
                if not (isinstance(n, int) and n == 0):
                    dve.wait_ge(product_done, (n - 1) * BLOCK_TILES)
                nc.vector.tensor_tensor(mix[:, i], first_w[:, :, :], second_w[:, :, :], ALU.add).then_inc(mix_done, 1)

            def weigh(n, i, t):
                m = n * BLOCK_TILES + t
                dve.wait_ge(expert_done, m + 1)
                dve.wait_ge(mix_done, n + 1)
                dve.wait_ge(halved, n * BLOCK_TILES + max(t - 1, 0))
                nc.vector.tensor_tensor(product[:, t % 2, :].rearrange("p (e c) -> p e c", c=CH),
                                        ps_e[t % 2][:, :].rearrange("p (e c) -> p e c", c=CH),
                                        mix[:, i, t, :].unsqueeze(2).to_broadcast([P, EXPERTS, CH]), ALU.mult).then_inc(product_done, 1)

            dve.wait_ge(ready, 2)
            nc.vector.tensor_copy(order[:, :], order_i[:, :]).then_inc(ready, 1)
            dve.wait_ge(ready, 3)
            norm(0, 0)
            normalise(0, 0)
            choose(0, 0)
            shares(0, 0)
            with dve.Fori(0, ALL_BLOCKS // 2) as k:
                for i in range(2):
                    n = k * 2 + i
                    norm(n + 1, 1 - i)
                    weigh(n, i, 0)
                    normalise(n + 1, 1 - i)
                    weigh(n, i, 1)
                    weigh(n, i, 2)
                    choose(n + 1, 1 - i)
                    weigh(n, i, 3)
                    shares(n + 1, 1 - i)
                    dve.wait_ge(tile_mixed, n * BLOCK_TILES + BLOCK_TILES)
                    dve.wait_ge(stored[i], k * 16)
                    nc.vector.tensor_tensor(out_sb[:, i, :], t_sb[:, i, :], mixed[:, i, :], ALU.add).then_inc(out_done, 1)


def build(nc, x, weights, constants, constants16, out):
    dram = lambda name, shape, dt=F32: nc.dram_tensor(name, shape, dt).ap()
    scan_in = dram("scan_in", (ALL_CHUNKS, P, STEP))
    scan_out = dram("scan_out", (ALL_CHUNKS, P, STEP))
    gate = dram("gate_dram", (IMAGES, P, TOK))
    left = dram("left_dram", (IMAGES, HALF, TOK))
    tokens = dram("tokens", (ALL_BLOCKS, P, BANK))
    q_parts, k_parts = (dram(n, (IMAGES, PARTS, P, TOK), BF16) for n in ("q_parts", "k_parts"))
    values = dram("values", (IMAGES, GROUPS, P, TILES, P))
    maxima = dram("maxima", (TOP, PARTS, P), BF16)
    attended = dram("attended", (GROUPS, ALL_BLOCKS, P, BANK))
    by_direction = lambda t: t.rearrange("(b k c) p t -> b k p c t", k=DIRS, c=SCAN_CHUNKS)
    x_images = x.rearrange("b h w c -> b (h w) c")
    with ExitStack() as ctx:
        sb = lambda name, shape, dt=F32: ctx.enter_context(nc.sbuf_tensor(name, shape, dt))
        w, c, c16 = sb("w", [P, WEIGHTS.n]), sb("c", [P, CONSTANTS.n]), sb("c16", [P, CONSTANTS16.n], BF16)
        d, bias16 = sb("d", [P, DERIVED.n]), sb("bias16", [P, EXPERTS * P], BF16)
        prepare(nc, weights, constants, constants16, w, c, c16, d, bias16)
        conv_front(nc, x_images, w, c, d, by_direction(scan_in), gate, left)
        state_scan(nc, w, c, c16, d, scan_in, scan_out)
        conv_back(nc, x_images, w, c, d, by_direction(scan_out), gate, left, tokens, q_parts, k_parts, values)
        attention(nc, c, c16, q_parts, k_parts, values, maxima, attended)
        experts(nc, w, c, c16, bias16, attended, tokens, out.rearrange("b h w c -> (b h w) c").rearrange("(n t p) c -> n p t c", p=P, t=BLOCK_TILES))


def lay_out_weights(i):
    w = np.zeros((P, WEIGHTS.n), np.float32)
    col = lambda name: WEIGHTS.of(w, name)
    L, R = slice(0, HALF), slice(HALF, P)
    g = lambda name: np.asarray(i["L0_conv_" + name])
    col("in1x1")[L, L], col("in1x1")[R, R] = g("cv2_w").T, g("cv1_w").T
    col("in_scale")[:, 0] = np.concatenate([g("cv2_g"), g("cv1_g")])
    col("in_bias")[:, 0] = np.concatenate([g("cv2_b"), g("cv1_b")])
    col("bn0_scale")[:, 0] = np.concatenate([g("bn0_g"), np.ones(HALF, np.float32)])
    col("bn0_bias")[L, 0] = g("bn0_b")
    col("xh")[R], col("gate")[R] = g("in_proj_w")[:P].T, g("in_proj_w")[P:].T
    col("dw")[:] = np.broadcast_to(g("dw_w").reshape(1, TAPS * P), (P, TAPS * P))
    col("dw_b")[:, 0] = g("dw_b")
    for n in ("1", "2"):
        col("c" + n)[L] = g(f"c{n}_w").reshape(TAPS, HALF, HALF).transpose(1, 0, 2).reshape(HALF, TAPS * HALF)
        for v in (f"c{n}_b", f"bn{n}_g", f"bn{n}_b"):
            col(v)[L, 0] = g(v)
    col("c3")[L], col("c3_b")[L, 0] = g("c3_w").T, g("c3_b")
    xp = g("x_proj_w")
    bc = xp[:, DT_RANK:].transpose(2, 0, 1)
    col("bc")[:] = np.concatenate([bc] * PARTS, axis=2).reshape(P, DIRS * 96)
    col("xp_dt")[:DT_RANK] = xp[:, :DT_RANK].transpose(1, 0, 2).reshape(DT_RANK, DIRS * P)
    col("dt_w")[:DT_RANK] = g("dt_w").transpose(2, 0, 1).reshape(DT_RANK, DIRS * P)
    col("dt_b")[:] = g("dt_b").T
    col("a_logs")[:] = g("A_logs").reshape(DIRS, P, STATES).transpose(1, 0, 2).reshape(P, DIRS * STATES)
    col("skip")[:] = g("Ds").reshape(DIRS, P).T
    col("ln_g")[:, 0], col("ln_b")[:, 0] = g("ln_g"), g("ln_b")
    col("out_proj")[L] = g("out_proj_w")
    col("cv")[L, HALF:] = g("cv_w").T
    col("cv_g")[R, 0], col("cv_b")[R, 0] = g("cv_g"), g("cv_b")
    shuffle = np.arange(P).reshape(2, HALF).T.reshape(P)
    col("cv3")[:] = g("cv3_w")[shuffle].T
    col("cv3_g")[:, 0], col("cv3_b")[:, 0] = g("cv3_g")[shuffle], g("cv3_b")[shuffle]
    col("qkv")[:] = i["L1_attn_w_attn"]
    wp = np.zeros((2, HEADS // 2, 2 * HEAD, P), np.float32)
    wp[:, :, :HEAD] = np.asarray(i["L1_attn_w_proj"]).reshape(2, HEADS // 2, HEAD, P)
    col("w_proj")[:] = wp.reshape(2, P, P).transpose(1, 0, 2).reshape(P, 2 * P)
    col("router")[:] = i["L1_ffn_router_w"]
    col("router_b")[:] = np.broadcast_to(i["L1_ffn_router_b"], (P, EXPERTS))
    col("experts")[:] = np.asarray(i["L1_ffn_expert_w"]).transpose(1, 0, 2).reshape(P, EXPERTS * P)
    col("expert_b")[:PARTS] = np.broadcast_to(np.asarray(i["L1_ffn_expert_b"]).reshape(1, EXPERTS * P), (PARTS, EXPERTS * P))
    return w


def lay_out_constants():
    c, c16 = np.zeros((P, CONSTANTS.n), np.float32), np.zeros((P, CONSTANTS16.n), np.float32)
    CONSTANTS.of(c, "ident")[:] = np.eye(P)
    CONSTANTS.of(c, "mean")[:] = 1.0 / P
    CONSTANTS.of(c, "part_a")[32:96] = -1.0
    CONSTANTS.of(c, "part_b")[64:96] = -1.0
    CONSTANTS.of(c, "row_a")[1:3] = -1.0
    CONSTANTS.of(c, "row_b")[2:3] = -1.0
    for h in range(HEADS // 2):
        CONSTANTS.of(c, "head_sum")[32 * h + HEAD, 32 * h:32 * h + 32] = 1.0
    for n in range(2 * STATES):
        CONSTANTS16.of(c16, "select")[n:96:32, n * P:(n + 1) * P] = 1.0
    CONSTANTS16.of(c16, "ident")[:] = np.eye(P)
    CONSTANTS16.of(c16, "above")[:] = np.where(np.arange(P)[:, None] > np.arange(P)[None, :], MASKED, 0.0)
    CONSTANTS16.of(c16, "below")[:] = np.where(np.arange(P)[:, None] < np.arange(P)[None, :], MASKED, 0.0)
    CONSTANTS16.of(c16, "ones")[:PARTS] = 1.0
    return c, c16.astype(mybir.dt.np(BF16))


def kernel(**inputs):
    import concourse.bacc as bacc
    from concourse.bass_utils import run_bass_kernel_spmd

    nc = bacc.Bacc("TRN2", target_bir_lowering=False, num_devices=1)
    c, c16 = lay_out_constants()
    arrays = {"x_in": np.ascontiguousarray(inputs["x"]), "weights": lay_out_weights(inputs), "constants": c, "constants16": c16}
    args = [nc.dram_tensor(n, a.shape, mybir.dt.from_np(a.dtype), kind="ExternalInput").ap() for n, a in arrays.items()]
    out = nc.dram_tensor("out", (IMAGES, SIDE, SIDE, CH), F32, kind="ExternalOutput").ap()
    build(nc, *args, out)
    result = run_bass_kernel_spmd(nc, [arrays], core_ids=[0])
    return result.results[0]["out"]
```

```python
import numpy as np
from contextlib import ExitStack

import concourse.bass as bass
from concourse import mybir

F32 = mybir.dt.float32
BF16 = mybir.dt.bfloat16
ALU = mybir.AluOpType
ACT = mybir.ActivationFunctionType
AX = mybir.AxisListType
ds = bass.ds

P = 128
IMAGES, SIDE, CH = 4, 64, 128
HALF = CH // 2
TOK = SIDE * SIDE
BANK = 512
PAD = SIDE + 2
ROWS = BANK // SIDE
CHUNKS = TOK // BANK
TILES = TOK // P
PRODUCTS = 6

DIRS, STATES, DT_RANK = 4, 16, 4
STEP = 1024
SCAN_CHUNKS = TOK // STEP
ALL_CHUNKS = IMAGES * DIRS * SCAN_CHUNKS
PARTS = 3

HEADS, HEAD = 8, 16
EXPERTS = 8


class Columns:

    def __init__(self, widths):
        self.at, self.n = {}, 0
        for name, width in widths:
            self.at[name] = (self.n, width)
            self.n += width

    def of(self, tensor, name, rows=P, start=0):
        at, width = self.at[name]
        return tensor[start:rows, at:at + width]


WEIGHTS = Columns([
    ("in1x1", P), ("in_scale", 1), ("in_bias", 1), ("bn0_scale", 1), ("bn0_bias", 1),
    ("xh", P), ("gate", P), ("dw", PRODUCTS * P), ("dw_b", 1),
    ("c1", PRODUCTS * HALF), ("c1_b", 1), ("bn1_g", 1), ("bn1_b", 1),
    ("c2", PRODUCTS * HALF), ("c2_b", 1), ("bn2_g", 1), ("bn2_b", 1),
    ("c3", HALF), ("c3_b", 1),
    ("bc", DIRS * 96), ("xp_dt", DIRS * P), ("dt_w", DIRS * P), ("dt_b", DIRS),
    ("a_logs", DIRS * STATES), ("skip", DIRS),
    ("ln_g", 1), ("ln_b", 1), ("out_proj", P), ("cv", P), ("cv_g", 1), ("cv_b", 1),
    ("cv3", P), ("cv3_g", 1), ("cv3_b", 1),
    ("qkv", 3 * P), ("w_proj", 2 * P),
    ("router", EXPERTS), ("router_b", EXPERTS), ("experts", EXPERTS * P), ("expert_b", EXPERTS * P),
])
CONSTANTS = Columns([
    ("ident", P), ("mean", P), ("part_a", 1), ("part_b", 1), ("row_a", 1), ("row_b", 1),
    ("head_sum", P),
])
CONSTANTS16 = Columns([("select", 2 * STATES * P), ("ident", P), ("above", P), ("below", P), ("ones", P)])
MASKED = -1e30
DERIVED = Columns([
    ("taps", PRODUCTS * P), ("dt", DIRS * P), ("neg_a", DIRS * STATES), ("cv_out", P),
    ("c1_bias", 1), ("c2_bias", 1),
])


def scan_slot(tensor):
    return tensor[:, 0:P], tensor[:, P:P + 96], tensor[:, P + 96:P + 97]


def prepare(nc, weights, constants, constants16, w, c, c16, d, bias16):
    with ExitStack() as ctx:
        sb = lambda name, shape, dt=F32: ctx.enter_context(nc.sbuf_tensor(name, shape, dt))
        sem = lambda name: ctx.enter_context(nc.semaphore(name))
        hi = sb("pre_hi", [P, EXPERTS * P], BF16)
        rest = sb("pre_rest", [P, EXPERTS * P])
        exp_a = sb("pre_exp_a", [P, DIRS * STATES])
        ps = ctx.enter_context(nc.psum_tensor("pre_ps", [P, (DIRS + 1) * BANK], F32))
        loaded, products, exp_done, chain = (sem(f"pre_{n}") for n in ("loaded", "products", "exp", "chain"))
        block = ctx.enter_context(nc.Block())

        @block.sync
        def _(sp):
            sp.dma_start(w[:, :], weights).then_inc(loaded, 16)
            sp.dma_start(c[:, :], constants).then_inc(loaded, 16)
            sp.dma_start(c16[:, :], constants16).then_inc(loaded, 16)
            sp.wait_ge(loaded, 48)

        @block.tensor
        def _(pe):
            pe.wait_ge(loaded, 48)
            xp, dt = WEIGHTS.of(w, "xp_dt"), WEIGHTS.of(w, "dt_w")
            for k in range(DIRS):
                nc.tensor.matmul(ps[:, k * BANK:k * BANK + P], xp[:, k * P:(k + 1) * P],
                                 dt[:, k * P:(k + 1) * P], start=True, stop=True)
            nc.tensor.matmul(ps[:, DIRS * BANK:DIRS * BANK + P], WEIGHTS.of(w, "out_proj"),
                             WEIGHTS.of(w, "cv"), start=True, stop=True).then_inc(products, 1)

        @block.scalar
        def _(act):
            act.wait_ge(loaded, 48)
            nc.scalar.activation(exp_a[:, :], WEIGHTS.of(w, "a_logs"), ACT.Exp).then_inc(exp_done, 1)
            nc.scalar.activation(hi[:, :], WEIGHTS.of(w, "expert_b"), ACT.Copy).then_inc(exp_done, 1)

        @block.vector
        def _(dve):
            dve.wait_ge(loaded, 48)
            for t in range(PRODUCTS):
                nc.vector.tensor_tensor(DERIVED.of(d, "taps")[:, t * P:(t + 1) * P], WEIGHTS.of(w, "xh"),
                                        WEIGHTS.of(w, "dw")[:, t * P:(t + 1) * P], ALU.mult)
            for n in ("1", "2"):
                nc.vector.scalar_tensor_tensor(
                    out=DERIVED.of(d, f"c{n}_bias"), in0=WEIGHTS.of(w, f"c{n}_b"),
                    scalar=WEIGHTS.of(w, f"bn{n}_g"), in1=WEIGHTS.of(w, f"bn{n}_b"),
                    op0=ALU.mult, op1=ALU.add)
            dve.wait_ge(exp_done, 1)
            nc.vector.tensor_scalar(DERIVED.of(d, "neg_a"), exp_a[:, :], -1.0, None, ALU.mult)
            dve.wait_ge(exp_done, 2)
            part_a, part_b = CONSTANTS.of(c, "row_a"), CONSTANTS.of(c, "row_b")
            nc.vector.scalar_tensor_tensor(out=rest[:, :], in0=hi[:, :], scalar=part_a,
                                           in1=WEIGHTS.of(w, "expert_b"), op0=ALU.mult, op1=ALU.add).then_inc(chain, 1)
            dve.wait_ge(chain, 1)
            nc.vector.tensor_copy(hi[:, :], rest[:, :]).then_inc(chain, 1)
            dve.wait_ge(chain, 2)
            nc.vector.scalar_tensor_tensor(out=bias16[:, :], in0=hi[:, :], scalar=part_b, in1=rest[:, :],
                                           op0=ALU.mult, op1=ALU.add)
            dve.wait_ge(products, 1)
            nc.vector.tensor_copy(DERIVED.of(d, "dt").rearrange("p (k n) -> p k n", n=P),
                                  ps[:, 0:DIRS * BANK].rearrange("p (k n) -> p k n", n=BANK)[:, :, 0:P])
            nc.vector.tensor_copy(DERIVED.of(d, "cv_out"), ps[:, DIRS * BANK:DIRS * BANK + P])


X_PARTS = [(slice(t, t + 4), slice(t * P, (t + 4) * P)) for t in range(0, TILES, 4)]
X_COUNT = 16 * len(X_PARTS)


def worked_out(engine, value):
    return value if isinstance(value, int) else engine.to_reg(value)


def conv_front(nc, x, w, c, d, scan_in, gate, left):
    with ExitStack() as ctx:
        sb = lambda name, shape: ctx.enter_context(nc.sbuf_tensor("cf_" + name, shape, F32))
        pb = lambda name: ctx.enter_context(nc.psum_tensor("cf_" + name, [P, BANK], F32))
        sem = lambda name: ctx.enter_context(nc.semaphore("cf_" + name))
        x_tok = sb("x_tok", [P, TILES, CH])
        x_ch = sb("x_ch", [P, TOK])
        act_in = sb("act_in", [P, 2, BANK])
        pad_l, pad_r, pad2 = (sb(n, [P, PAD, PAD]) for n in ("pad_l", "pad_r", "pad2"))
        conv2 = sb("conv2", [P, 2, BANK])
        left_sb = sb("left_sb", [P, 2, BANK])
        gate_sb = sb("gate_sb", [P, 2, BANK])
        dirs = [sb(f"dir{k}", [P, TOK]) for k in range(DIRS)]
        ps_tr = [pb(f"ps_tr{i}") for i in range(2)]
        ps_in, ps_xh, ps_gate, ps_c1, ps_c2, ps_c3 = (pb(n) for n in ("ps_in", "ps_xh", "ps_gate", "ps_c1", "ps_c2", "ps_c3"))

        x_loaded, cleared = sem("x_loaded"), sem("cleared")
        transposed, x_copied = sem("transposed"), sem("x_copied")
        in_done, in_silu, padded = sem("in_done"), sem("in_silu"), sem("padded")
        xh_done, xh_silu, gate_done, gate_silu = sem("xh_done"), sem("xh_silu"), sem("gate_done"), sem("gate_silu")
        c1_done, c1_relu, c2_done, c2_relu = sem("c1_done"), sem("c1_relu"), sem("c2_done"), sem("c2_relu")
        c3_done, c3_relu, turned = sem("c3_done"), sem("c3_relu"), sem("turned")
        gate_stored, left_stored = [sem(f"gate_stored{i}") for i in range(2)], [sem(f"left_stored{i}") for i in range(2)]
        dirs_stored = sem("dirs_stored")
        block = ctx.enter_context(nc.Block())

        def window(pad, g, dy, dx):
            return pad[:, g * ROWS + dy:g * ROWS + dy + ROWS, dx:dx + SIDE]

        def inner(pad, g, part, higher=0):
            return pad[part, g * ROWS + 1 - higher:(g + 1) * ROWS + 1 - higher, 1:SIDE + 1]

        LOW, HIGH = slice(0, HALF), slice(HALF, P)

        def rows_of(tile):
            return tile.rearrange("p (r s) -> p r s", s=SIDE)

        @block.sync
        def _(sp):
            def load_x(b):
                for tiles, rows in X_PARTS:
                    sp.dma_start(x_tok[:, tiles, :], x[b, rows].rearrange("(t p) c -> p t c", p=P)).then_inc(x_loaded, 16)

            load_x(0)
            with sp.Fori(0, IMAGES) as b:
                sp.wait_ge(transposed, b * CHUNKS + CHUNKS)
                load_x((b + 1) % IMAGES)
                for g in range(CHUNKS + 3):
                    if g < CHUNKS:
                        sp.wait_ge(gate_silu, b * CHUNKS + g + 1)
                        sp.dma_start(gate[b, :, g * BANK:(g + 1) * BANK], gate_sb[:, g % 2, :]).then_inc(gate_stored[g % 2], 16)
                    if g == CHUNKS:
                        sp.dma_start(scan_in[b, 0], dirs[0][:, :].rearrange("p (c t) -> p c t", t=STEP)).then_inc(dirs_stored, 16)
                    if g > CHUNKS:
                        k = g - CHUNKS
                        sp.wait_ge(turned, b * (DIRS - 1) + k)
                        sp.dma_start(scan_in[b, k], dirs[k][:, :].rearrange("p (c t) -> p c t", t=STEP)).then_inc(dirs_stored, 16)
                    if g >= 3:
                        h = g - 3
                        sp.wait_ge(c3_relu, b * CHUNKS + h + 1)
                        sp.dma_start(left[b, :, h * BANK:(h + 1) * BANK], left_sb[0:HALF, h % 2, :]).then_inc(left_stored[h % 2], 16)
                sp.wait_ge(turned, b * (DIRS - 1) + 3)
                sp.dma_start(scan_in[b, 3], dirs[3][:, :].rearrange("p (c t) -> p c t", t=STEP)).then_inc(dirs_stored, 16)
            sp.wait_ge(x_loaded, X_COUNT * (IMAGES + 1))
            sp.wait_ge(dirs_stored, 16 * IMAGES * DIRS)
            for i in range(2):
                sp.wait_ge(gate_stored[i], 16 * IMAGES * CHUNKS // 2)
                sp.wait_ge(left_stored[i], 16 * IMAGES * CHUNKS // 2)

        @block.gpsimd
        def _(pool):
            for tile in (pad_l, pad_r, pad2, conv2):
                nc.gpsimd.memset(tile[:, :, :], 0.0).then_inc(cleared, 1)

        @block.tensor
        def _(pe):
            in1x1, gate_w, c3 = WEIGHTS.of(w, "in1x1"), WEIGHTS.of(w, "gate"), WEIGHTS.of(w, "c3")
            taps, c1, c2 = DERIVED.of(d, "taps"), WEIGHTS.of(w, "c1"), WEIGHTS.of(w, "c2")
            ident = CONSTANTS.of(c, "ident")

            def product(out, pad, g, stationary, width, t):
                return nc.tensor.matmul(out, stationary[:, t * width:(t + 1) * width], window(pad, g, t // 3 * 2, t % 3),
                                        start=(t == 0), stop=(t == PRODUCTS - 1))

            pe.wait_ge(cleared, 4)
            with pe.Fori(0, IMAGES) as b:
                first = b * CHUNKS
                pe.wait_ge(x_loaded, b * X_COUNT + X_COUNT)
                for g in range(CHUNKS):
                    pe.wait_ge(x_copied, first + max(g - 1, 0))
                    for t in range(BANK // P):
                        last = nc.tensor.transpose(ps_tr[g % 2][:, t * P:(t + 1) * P], x_tok[:, g * (BANK // P) + t, :], ident)
                    last.then_inc(transposed, 1)
                for g in range(CHUNKS):
                    pe.wait_ge(x_copied, first + g + 1)
                    pe.wait_ge(in_silu, first + g)
                    nc.tensor.matmul(ps_in[:, :], in1x1, x_ch[:, g * BANK:(g + 1) * BANK], start=True, stop=True).then_inc(in_done, 1)
                for g in range(CHUNKS + 3):
                    if g < CHUNKS:
                        pe.wait_ge(padded, first + min(g + 2, CHUNKS))
                        pe.wait_ge(xh_silu, first + g)
                        for t in range(PRODUCTS):
                            last = product(ps_xh[:, :], pad_r, g, taps, P, t)
                        last.then_inc(xh_done, 1)
                        pe.wait_ge(gate_silu, first + g)
                        nc.tensor.matmul(ps_gate[:, :], gate_w, window(pad_r, g, 1, 1), start=True, stop=True).then_inc(gate_done, 1)
                        pe.wait_ge(c1_relu, first + g)
                    elif g - 2 < CHUNKS:
                        pe.wait_ge(c1_relu, first + CHUNKS)
                    if 2 <= g < CHUNKS + 2:
                        pe.wait_ge(c2_relu, first + g - 2)
                    for t in range(PRODUCTS):
                        if g < CHUNKS:
                            last1 = product(ps_c1[LOW, :], pad_l, g, c1, HALF, t)
                        if 2 <= g < CHUNKS + 2:
                            last2 = product(ps_c2[HIGH, :], pad2, g - 2, c2, HALF, t)
                    if g < CHUNKS:
                        last1.then_inc(c1_done, 1)
                    if 2 <= g < CHUNKS + 2:
                        last2.then_inc(c2_done, 1)
                    if g >= 3:
                        pe.wait_ge(c2_relu, first + g - 2)
                        pe.wait_ge(c3_relu, first + g - 3)
                        nc.tensor.matmul(ps_c3[LOW, :], c3, conv2[:, (g - 3) % 2, :], start=True, stop=True).then_inc(c3_done, 1)

        @block.scalar
        def _(act):
            act.wait_ge(cleared, 4)
            with act.Fori(0, IMAGES) as b:
                first = b * CHUNKS
                for g in range(CHUNKS):
                    act.wait_ge(in_done, first + g + 1)
                    act.wait_ge(padded, first + max(g - 1, 0))
                    nc.scalar.activation(act_in[:, g % 2, :], ps_in[:, :], ACT.Silu, bias=WEIGHTS.of(w, "in_bias"),
                                         scale=WEIGHTS.of(w, "in_scale")).then_inc(in_silu, 1)
                act.wait_ge(dirs_stored, b * DIRS * 16)
                act.wait_ge(c2_done, first)
                for g in range(CHUNKS + 3):
                    if g < CHUNKS:
                        act.wait_ge(xh_done, first + g + 1)
                        nc.scalar.activation(dirs[0][:, g * BANK:(g + 1) * BANK], ps_xh[:, :], ACT.Silu,
                                             bias=WEIGHTS.of(w, "dw_b")).then_inc(xh_silu, 1)
                        act.wait_ge(gate_done, first + g + 1)
                        act.wait_ge(gate_stored[g % 2], (b * (CHUNKS // 2) + g // 2) * 16)
                        nc.scalar.activation(gate_sb[:, g % 2, :], ps_gate[:, :], ACT.Silu).then_inc(gate_silu, 1)
                        act.wait_ge(c1_done, first + g + 1)
                        for part, higher in ((HIGH, 1), (LOW, 0)):
                            last = nc.scalar.activation(inner(pad2, g, part, higher), rows_of(ps_c1[LOW, :]), ACT.Relu,
                                                        bias=DERIVED.of(d, "c1_bias", HALF), scale=WEIGHTS.of(w, "bn1_g", HALF))
                        last.then_inc(c1_relu, 1)
                    if 2 <= g < CHUNKS + 2:
                        h = g - 2
                        act.wait_ge(c2_done, first + h + 1)
                        act.wait_ge(c3_done, first + max(h - 1, 0))
                        nc.scalar.activation(conv2[HIGH, h % 2, :], ps_c2[HIGH, :], ACT.Relu, bias=DERIVED.of(d, "c2_bias", start=HALF),
                                             scale=WEIGHTS.of(w, "bn2_g", start=HALF)).then_inc(c2_relu, 1)
                    if g >= 3:
                        h = g - 3
                        act.wait_ge(c3_done, first + h + 1)
                        act.wait_ge(left_stored[h % 2], (b * (CHUNKS // 2) + h // 2) * 16)
                        nc.scalar.activation(left_sb[LOW, h % 2, :], ps_c3[LOW, :], ACT.Relu,
                                             bias=WEIGHTS.of(w, "c3_b", HALF)).then_inc(c3_relu, 1)

        @block.vector
        def _(dve):
            dve.wait_ge(cleared, 4)
            with dve.Fori(0, IMAGES) as b:
                first = b * CHUNKS
                dve.wait_ge(in_done, first)
                for g in range(CHUNKS):
                    dve.wait_ge(transposed, first + g + 1)
                    nc.vector.tensor_copy(x_ch[:, g * BANK:(g + 1) * BANK], ps_tr[g % 2][:, :]).then_inc(x_copied, 1)
                dve.wait_ge(c1_done, first)
                dve.wait_ge(gate_done, first)
                for g in range(CHUNKS):
                    dve.wait_ge(in_silu, first + g + 1)
                    for part, higher in ((LOW, 0), (HIGH, 1)):
                        nc.vector.tensor_scalar(inner(pad_l, g, part, higher), rows_of(act_in[LOW, g % 2, :]), WEIGHTS.of(w, "bn0_scale", HALF),
                                                WEIGHTS.of(w, "bn0_bias", HALF), ALU.mult, ALU.add)
                    for part, higher in ((LOW, 1), (HIGH, 0)):
                        last = nc.vector.tensor_copy(inner(pad_r, g, part, higher), rows_of(act_in[HIGH, g % 2, :]))
                    last.then_inc(padded, 1)
                dve.wait_ge(xh_silu, first + CHUNKS)
                nc.vector.tensor_copy(dirs[1][:, :].rearrange("p (s r) -> p s r", r=SIDE),
                                      dirs[0][:, :].rearrange("p (r s) -> p s r", s=SIDE)).then_inc(turned, 1)
                nc.vector.tensor_copy(dirs[2][:, :], dirs[0][:, ::-1]).then_inc(turned, 1)
                dve.wait_ge(turned, b * (DIRS - 1) + 1)
                nc.vector.tensor_copy(dirs[3][:, :], dirs[1][:, ::-1]).then_inc(turned, 1)


RING = 4


def state_scan(nc, w, c, c16, d, scan_in, scan_out):
    with ExitStack() as ctx:
        sb = lambda name, shape, dt=F32: ctx.enter_context(nc.sbuf_tensor("ss_" + name, shape, dt))
        pb = lambda name: ctx.enter_context(nc.psum_tensor("ss_" + name, [P, STEP], F32))
        sem = lambda name: ctx.enter_context(nc.semaphore("ss_" + name))
        x_in = sb("x_in", [P, 3 * STEP])
        slot = sb("slot", [P, P + 96 + 1])
        mag, pos, small, log1 = (sb(n, [P, STEP]) for n in ("mag", "pos", "small", "log1"))
        one, rest_e, main = (sb(n, [P, STEP]) for n in ("one", "rest_e", "main"))
        hi, mid, rest = sb("hi", [96, STEP], BF16), sb("mid", [96, STEP], BF16), sb("rest", [96, STEP])
        delta, dx = sb("delta", [P, 2 * STEP]), sb("dx", [P, 2 * STEP])
        bc = sb("bc", [96, 2 * STEP], BF16)
        b_sb, decay, drive = (sb(n, [P, RING, STEP]) for n in ("b_sb", "decay", "drive"))
        h, hc = sb("h", [P, 2, STEP]), sb("hc", [P, 2, STEP])
        carry = sb("carry", [P, 2 * STATES])
        y_sb = sb("y_sb", [P, STEP])
        ps_prep, ps_b, ps_c, ps_y = pb("ps_prep"), pb("ps_b"), pb("ps_c"), pb("ps_y")

        x_loaded, y_stored, start = sem("x_loaded"), sem("y_stored"), sem("start")
        slot_filled, dt_done, dt_read, exp_small, log_done = (sem(n) for n in ("slot_filled", "dt_done", "dt_read", "exp_small", "log_done"))
        bc_done, hi_done, rest_done, mid_done, bc_split = (sem(n) for n in ("bc_done", "hi_done", "rest_done", "mid_done", "bc_split"))
        one_done, rest_e_done, main_done, delta_done, dx_done = (sem(n) for n in ("one_done", "rest_e_done", "main_done", "delta_done", "dx_done"))
        b_done, b_copied, decayed, driven = (sem(n) for n in ("b_done", "b_copied", "decayed", "driven"))
        scanned, carried, c_done, multiplied, summed, y_done = (sem(n) for n in ("scanned", "carried", "c_done", "multiplied", "summed", "y_done"))
        abs_done = sem("abs_done")
        block = ctx.enter_context(nc.Block())

        slot_dt, slot_bc, slot_bias = scan_slot(slot)

        SPREAD_AHEAD, COPY_AHEAD, AHEAD = RING + 1, RING, RING - 1
        DT, ABS, RELU, SMALL, LOG, ONE, REST_E, MAIN, DELTA, DX = 1, 1, 2, 4, 6, 5, 6, 8, 10, 12
        BC, HI, REST, MID, SPLIT = 3, 5, 7, 7, 9

        def direction(q):
            return (q // SCAN_CHUNKS) % DIRS

        def half(q):
            return (q % 2) * STEP

        def third(q):
            return (q % 3) * STEP

        @block.sync
        def _(sp):
            sp.dma_start(x_in[:, 0:STEP], scan_in[0]).then_inc(x_loaded, 16)
            sp.wait_ge(x_loaded, 16)
            sp.dma_start(x_in[:, STEP:2 * STEP], scan_in[1]).then_inc(x_loaded, 16)
            with sp.Fori(0, ALL_CHUNKS) as j:
                q = j + 2
                sp.wait_ge(x_loaded, j * 16 + 32)
                sp.wait_ge(y_done, j)
                sp.dma_start(x_in[:, ds(third(q), STEP)], scan_in[q % ALL_CHUNKS]).then_inc(x_loaded, 16)
                sp.wait_ge(y_done, j + 1)
                sp.dma_start(scan_out[j], y_sb[:, :]).then_inc(y_stored, 16)
            sp.wait_ge(y_stored, 16 * ALL_CHUNKS)
            sp.wait_ge(x_loaded, 16 * (ALL_CHUNKS + 2))

        @block.tensor
        def _(pe):
            ident = CONSTANTS.of(c, "ident")
            select = CONSTANTS16.of(c16, "select", 96)

            def prep_dt(q):
                pe.wait_ge(slot_filled, q + 1)
                pe.wait_ge(x_loaded, q * 16 + 16)
                pe.wait_ge(rest_done, q)
                for i in range(STEP // BANK):
                    last = nc.tensor.matmul(ps_prep[:, i * BANK:(i + 1) * BANK], slot_dt,
                                            x_in[:, ds(third(q) + i * BANK, BANK)], start=True, stop=True)
                last.then_inc(dt_done, 1)

            def prep_bc(q):
                pe.wait_ge(dt_read, q + 1)
                for i in range(STEP // BANK):
                    last = nc.tensor.matmul(ps_prep[0:96, i * BANK:(i + 1) * BANK], slot_bc,
                                            x_in[:, ds(third(q) + i * BANK, BANK)], start=True, stop=True)
                last.then_inc(bc_done, 1)

            def spread(out, n, q):
                for i in range(STEP // BANK):
                    last = nc.tensor.matmul(out[:, i * BANK:(i + 1) * BANK], select[:, n * P:(n + 1) * P],
                                            bc[:, ds(half(q) + i * BANK, BANK)], start=True, stop=True)
                return last

            prep_dt(0)
            prep_bc(0)
            pe.wait_ge(bc_split, 1)
            for n in range(SPREAD_AHEAD):
                if n:
                    pe.wait_ge(b_copied, n)
                spread(ps_b, n, 0).then_inc(b_done, 1)
            spread(ps_c, STATES, 0).then_inc(c_done, 1)

            def sum_state(n, m):
                for i in range(STEP // BANK):
                    last = nc.tensor.matmul(ps_y[:, i * BANK:(i + 1) * BANK], ident, hc[:, n % 2, i * BANK:(i + 1) * BANK],
                                            start=(n == 0), stop=(n == STATES - 1))
                last.then_inc(summed, 1)

            def next_c(n, m, j):
                pe.wait_ge(multiplied, m + 1)
                spread(ps_c, STATES + (n + 1) % STATES, j + (n + 1) // STATES).then_inc(c_done, 1)

            def next_b(n, m, j):
                if n + SPREAD_AHEAD == STATES:
                    pe.wait_ge(bc_split, j + 2)
                pe.wait_ge(b_copied, m + SPREAD_AHEAD)
                spread(ps_b, (n + SPREAD_AHEAD) % STATES, j + (n + SPREAD_AHEAD) // STATES).then_inc(b_done, 1)

            next_c(0, 0, 0)
            next_b(0, 0, 0)
            sum_state(0, 0)
            with pe.Fori(0, ALL_CHUNKS) as j:
                m0 = j * STATES
                for s in range(1, STATES + 1):
                    n, m, q = s % STATES, m0 + s, j + s // STATES
                    next_c(n, m, q)
                    if n == 0:
                        next_b(n, m, q)
                        pe.wait_ge(y_done, j + 1)
                    sum_state(n, m)
                    if n == DT:
                        prep_dt(j + 1)
                    if n == BC:
                        prep_bc(j + 1)
                    if n:
                        next_b(n, m, q)
            sum_state(STATES - 1, ALL_CHUNKS * STATES)

        @block.scalar
        def _(act):
            neg_a, dt, bc_w, dt_b = DERIVED.of(d, "neg_a"), DERIVED.of(d, "dt"), WEIGHTS.of(w, "bc"), WEIGHTS.of(w, "dt_b")

            def prep_slot(q):
                k = direction(q)
                act.wait_ge(bc_done, q)
                act.wait_ge(dt_read, q)
                nc.scalar.activation(slot_dt, dt[:, ds(k * P, P)], ACT.Copy)
                nc.scalar.activation(slot_bc, bc_w[:, ds(k * 96, 96)], ACT.Copy)
                nc.scalar.activation(slot_bias, dt_b[:, ds(k, 1)], ACT.Copy).then_inc(slot_filled, 1)

            def prep_abs(q):
                act.wait_ge(slot_filled, q + 1)
                act.wait_ge(dt_done, q + 1)
                act.wait_ge(exp_small, q)
                nc.scalar.activation(mag[:, :], ps_prep[:, :], ACT.Abs, bias=slot_bias).then_inc(abs_done, 1)

            def prep_relu(q):
                act.wait_ge(main_done, q)
                nc.scalar.activation(pos[:, :], ps_prep[:, :], ACT.Relu, bias=slot_bias).then_inc(dt_read, 1)

            def prep_small(q):
                act.wait_ge(rest_e_done, q)
                act.wait_ge(abs_done, q + 1)
                act.wait_ge(log_done, q)
                nc.scalar.activation(small[:, :], mag[:, :], ACT.Exp, scale=-1.0).then_inc(exp_small, 1)

            def prep_log(q):
                act.wait_ge(exp_small, q + 1)
                nc.scalar.activation(log1[:, :], small[:, :], ACT.Ln, bias=1.0).then_inc(log_done, 1)

            def prep_hi(q):
                act.wait_ge(bc_done, q + 1)
                act.wait_ge(rest_done, q)
                nc.scalar.activation(hi[:, :], ps_prep[0:96, :], ACT.Copy).then_inc(hi_done, 1)

            def prep_mid(q):
                act.wait_ge(rest_done, q + 1)
                act.wait_ge(bc_split, q)
                nc.scalar.activation(mid[:, :], rest[:, :], ACT.Copy).then_inc(mid_done, 1)

            def copy_b(n, m):
                act.wait_ge(b_done, m + 1)
                nc.scalar.activation(b_sb[:, n % RING, :], ps_b[:, :], ACT.Copy).then_inc(b_copied, 1)

            def decays(n, q):
                nc.scalar.activation(decay[:, n % RING, :], delta[:, ds(half(q), STEP)], ACT.Exp,
                                     scale=neg_a[:, ds(direction(q) * STATES + n, 1)]).then_inc(decayed, 1)

            prep_slot(0)
            prep_abs(0)
            prep_relu(0)
            prep_small(0)
            prep_log(0)
            prep_hi(0)
            prep_mid(0)
            for n in range(COPY_AHEAD):
                copy_b(n, n)
            act.wait_ge(dx_done, 1)
            for n in range(AHEAD):
                decays(n, 0)
            with act.Fori(0, ALL_CHUNKS) as j:
                m0 = j * STATES
                for n in range(STATES):
                    act.wait_ge(driven, m0 + n + 1)
                    copy_b((n + COPY_AHEAD) % STATES, m0 + n + COPY_AHEAD)
                    nn = (n + AHEAD) % STATES
                    if nn == 0:
                        act.wait_ge(dx_done, j + 2)
                    act.wait_ge(scanned, m0 + n)
                    decays(nn, j + (n + AHEAD) // STATES)
                    if n == 0:
                        prep_slot(j + 1)
                    if n == ABS:
                        prep_abs(j + 1)
                    if n == RELU:
                        prep_relu(j + 1)
                    if n == SMALL:
                        prep_small(j + 1)
                    if n == LOG:
                        prep_log(j + 1)
                    if n == HI:
                        prep_hi(j + 1)
                    if n == MID:
                        prep_mid(j + 1)
            act.wait_ge(driven, ALL_CHUNKS * STATES + 1)
            copy_b(COPY_AHEAD, ALL_CHUNKS * STATES + COPY_AHEAD)

        @block.gpsimd
        def _(pool):
            def drives(n, m, q):
                b_copied_due = worked_out(pool, m + 1)
                pool.wait_ge(start, 1)
                pool.wait_ge(b_copied, b_copied_due)
                nc.gpsimd.tensor_tensor(drive[:, n % RING, :], b_sb[:, n % RING, :], dx[:, ds(half(q), STEP)],
                                        ALU.mult).then_inc(driven, 1)

            def prep_main(q):
                pool.wait_ge(log_done, q + 1)
                pool.wait_ge(delta_done, q)
                nc.gpsimd.tensor_tensor(main[:, :], log1[:, :], pos[:, :], ALU.add).then_inc(main_done, 1)

            def prep_rest_e(q):
                pool.wait_ge(one_done, q + 1)
                nc.gpsimd.tensor_tensor(rest_e[:, :], small[:, :], one[:, :], ALU.subtract).then_inc(rest_e_done, 1)

            nc.gpsimd.memset(carry[:, :], 0.0).then_inc(start, 1)
            pool.wait_ge(start, 1)
            prep_main(0)
            prep_rest_e(0)
            pool.wait_ge(dx_done, 1)
            for n in range(AHEAD):
                drives(n, n, 0)
            with pool.Fori(0, ALL_CHUNKS) as j:
                m0 = j * STATES
                for n in range(STATES):
                    nn = (n + AHEAD) % STATES
                    scanned_due = worked_out(pool, m0 + n + 1)
                    pool.wait_ge(start, 1)
                    pool.wait_ge(scanned, scanned_due)
                    nc.gpsimd.tensor_copy(carry[:, STATES + n:STATES + n + 1], h[:, n % 2, STEP - 1:STEP]).then_inc(carried, 1)
                    if nn == 0:
                        pool.wait_ge(dx_done, j + 2)
                    drives(nn, m0 + n + AHEAD, j + (n + AHEAD) // STATES)
                    if n == MAIN:
                        prep_main(j + 1)
                    if n == REST_E:
                        prep_rest_e(j + 1)

        @block.vector
        def _(dve):
            part_a, part_b = CONSTANTS.of(c, "part_a", 96), CONSTANTS.of(c, "part_b", 96)
            skip = WEIGHTS.of(w, "skip")

            def prep_one(q):
                dve.wait_ge(rest_e_done, q)
                dve.wait_ge(exp_small, q + 1)
                nc.vector.tensor_scalar(one[:, :], small[:, :], 1.0, -1.0, ALU.add, ALU.add).then_inc(one_done, 1)

            def prep_delta(q, j=None):
                dve.wait_ge(main_done, q + 1)
                dve.wait_ge(rest_e_done, q + 1)
                dve.wait_ge(dx_done, q)
                if j is not None:
                    dve.wait_ge(decayed, j * STATES)
                nc.vector.tensor_tensor(delta[:, ds(half(q), STEP)], main[:, :], rest_e[:, :], ALU.add).then_inc(delta_done, 1)

            def prep_dx(q, j=None):
                if j is not None:
                    dve.wait_ge(driven, j * STATES)
                dve.wait_ge(delta_done, q + 1)
                dve.wait_ge(x_loaded, q * 16 + 16)
                nc.vector.tensor_tensor(dx[:, ds(half(q), STEP)], delta[:, ds(half(q), STEP)], x_in[:, ds(third(q), STEP)],
                                        ALU.mult).then_inc(dx_done, 1)

            def prep_rest(q):
                dve.wait_ge(hi_done, q + 1)
                dve.wait_ge(bc_split, q)
                nc.vector.scalar_tensor_tensor(out=rest[:, :], in0=hi[:, :], scalar=part_a, in1=ps_prep[0:96, :],
                                               op0=ALU.mult, op1=ALU.add).then_inc(rest_done, 1)

            def prep_split(q, j=None):
                if j is not None:
                    dve.wait_ge(c_done, j * STATES)
                dve.wait_ge(mid_done, q + 1)
                nc.vector.scalar_tensor_tensor(out=bc[:, ds(half(q), STEP)], in0=mid[:, :], scalar=part_b, in1=rest[:, :],
                                               op0=ALU.mult, op1=ALU.add).then_inc(bc_split, 1)

            def scan(n, m, q):
                dve.wait_ge(decayed, m + 1)
                dve.wait_ge(driven, m + 1)
                nc.vector.tensor_tensor_scan(h[:, n % 2, :], decay[:, n % RING, :], drive[:, n % RING, :],
                                             initial=carry[:, ds(((q % SCAN_CHUNKS + SCAN_CHUNKS - 1) // SCAN_CHUNKS) * STATES + n, 1)],
                                             op0=ALU.mult, op1=ALU.add).then_inc(scanned, 1)

            prep_one(0)
            prep_delta(0)
            prep_dx(0)
            prep_rest(0)
            prep_split(0)
            def multiply(n, m):
                dve.wait_ge(scanned, m + 1)
                dve.wait_ge(c_done, m + 1)
                if not isinstance(m, int):
                    dve.wait_ge(summed, m - 1)
                nc.vector.tensor_tensor(hc[:, n % 2, :], h[:, n % 2, :], ps_c[:, :], ALU.mult).then_inc(multiplied, 1)

            def next_scan(n, m, j):
                if not isinstance(m, int):
                    dve.wait_ge(carried, m)
                    dve.wait_ge(multiplied, m)
                scan((n + 1) % STATES, m + 1, j + (n + 1) // STATES)

            dve.wait_ge(start, 1)
            scan(0, 0, 0)
            multiply(0, 0)
            next_scan(0, 0, 0)
            with dve.Fori(0, ALL_CHUNKS) as j:
                m0 = j * STATES
                for s in range(1, STATES + 1):
                    n, m, q = s % STATES, m0 + s, j + s // STATES
                    multiply(n, m)
                    if n == 0:
                        dve.wait_ge(summed, m)
                        dve.wait_ge(y_stored, j * 16)
                        nc.vector.scalar_tensor_tensor(out=y_sb[:, :], in0=x_in[:, ds(third(j), STEP)], scalar=skip[:, ds(direction(j), 1)],
                                                       in1=ps_y[:, :], op0=ALU.mult, op1=ALU.add).then_inc(y_done, 1)
                    next_scan(n, m, q)
                    if n == ONE:
                        prep_one(j + 1)
                    if n == REST:
                        prep_rest(j + 1)
                    if n == SPLIT:
                        prep_split(j + 1, j)
                    if n == DELTA:
                        prep_delta(j + 1, j)
                    if n == DX:
                        prep_dx(j + 1, j)


LN_EPS_SCAN = 1e-5
LN_EPS = 1e-5
HEAD_SCALE = HEAD ** -0.5
GROUPS = 2
GROUP_HEADS = HEADS // GROUPS
SLOT = P // GROUP_HEADS
BLOCK_TILES = BANK // P


def conv_back(nc, x, w, c, d, scan_out, gate, left, tokens, q_parts, k_parts, values):
    with ExitStack() as ctx:
        sb = lambda name, shape, dt=F32: ctx.enter_context(nc.sbuf_tensor("cb_" + name, shape, dt))
        pb = lambda name: ctx.enter_context(nc.psum_tensor("cb_" + name, [P, BANK], F32))
        sem = lambda name: ctx.enter_context(nc.semaphore("cb_" + name))
        y = [sb(f"y{k}", [P, TOK]) for k in range(DIRS)]
        x_tok, t_tok = sb("x_tok", [P, TILES, CH]), sb("t_tok", [P, TILES, CH])
        gate_in, both, o_ch = (sb(n, [P, 2, BANK]) for n in ("gate_in", "both", "o_ch"))
        stats, moments = sb("stats", [P, TILES, 6]), sb("moments", [P, TILES, 2])
        t_log, t_rstd = sb("t_log", [P, TILES]), sb("t_rstd", [P, TILES])
        xn_tok = sb("xn_tok", [P, 2, BANK])
        xn_ch = sb("xn_ch", [P, 2, BANK])
        hi, mid, lo = (sb(n, [P, 2, 2, BANK], BF16) for n in ("hi", "mid", "lo"))
        rest = sb("rest", [P, 2, 2, BANK])
        v_sb = sb("v_sb", [P, 2, GROUPS, BLOCK_TILES, GROUP_HEADS, SLOT])
        eps = sb("eps", [P, 1])
        ps_mean, ps_var, ps_xr, ps_out, ps_tok, ps_xn, ps_q, ps_k = (
            pb(n) for n in ("ps_mean", "ps_var", "ps_xr", "ps_out", "ps_tok", "ps_xn", "ps_q", "ps_k"))
        ps_qk, ps_v = ((ps_q, ps_k), (ps_var, ps_xr)), ps_mean

        names = ("y_loaded x_loaded ready added mean_done centred squared var_done log_done rstd_done norm_done scale_done "
                 "gated xr_done xr_silu out_done out_silu tok_done t_added stats_done moments_done t_log_done t_rstd_done "
                 "xn_done xn_turned xn_copied q_done k_done v_done hi_done rest_done mid_done lo_done v_copied t_stored").split()
        (y_loaded, x_loaded, ready, added, mean_done, centred, squared, var_done, log_done, rstd_done, norm_done, scale_done,
         gated, xr_done, xr_silu, out_done, out_silu, tok_done, t_added, stats_done, moments_done, t_log_done, t_rstd_done,
         xn_done, xn_turned, xn_copied, q_done, k_done, v_done, hi_done, rest_done, mid_done, lo_done, v_copied, t_stored) = map(sem, names)
        gate_loaded, left_loaded, v_stored, qk_stored = ([sem(f"{n}{i}") for i in range(2)] for n in ("gate_loaded", "left_loaded", "v_stored", "qk_stored"))
        block = ctx.enter_context(nc.Block())
        cols = lambda g: slice(g * BANK, (g + 1) * BANK)

        @block.sync
        def _(sp):
            def load_y(b, k):
                sp.dma_start(y[k][:, :].rearrange("p (c t) -> p c t", t=STEP), scan_out[b, k]).then_inc(y_loaded, 16)

            def load_x(b):
                for tiles, rows in X_PARTS:
                    sp.dma_start(x_tok[:, tiles, :], x[b, rows].rearrange("(t p) c -> p t c", p=P)).then_inc(x_loaded, 16)

            for k in range(DIRS):
                load_y(0, k)
            load_x(0)
            with sp.Fori(0, IMAGES) as b:
                first = b * CHUNKS
                for g in range(CHUNKS):
                    sp.wait_ge(gated, first + max(g - 1, 0))
                    sp.dma_start(gate_in[:, g % 2, :], gate[b, :, cols(g)]).then_inc(gate_loaded[g % 2], 16)
                for g in range(CHUNKS):
                    if g == 2:
                        sp.wait_ge(gated, first + CHUNKS)
                    sp.wait_ge(out_done, first + max(g - 1, 0))
                    sp.dma_start(both[0:HALF, g % 2, :], left[b, :, cols(g)]).then_inc(left_loaded[g % 2], 16)
                    if g in (3, 5, 7):
                        load_y((b + 1) % IMAGES, (3, 0, 1)[g // 2 - 1])
                sp.wait_ge(xr_done, first + CHUNKS)
                load_y((b + 1) % IMAGES, 2)
                sp.wait_ge(t_added, first + CHUNKS)
                for g in range(CHUNKS):
                    i = g % 2
                    for s, dram in ((0, q_parts), (1, k_parts)):
                        sp.wait_ge(lo_done, 2 * (first + g) + s + 1)
                        for part, tile in enumerate((hi, mid, lo)):
                            sp.dma_start(dram[b, part, :, cols(g)], tile[:, i, s, :]).then_inc(qk_stored[i], 16)
                    sp.wait_ge(v_copied, first + g + 1)
                    for r in range(GROUPS):
                        sp.dma_start(values[b, r, :, g * BLOCK_TILES:(g + 1) * BLOCK_TILES, :],
                                     v_sb[:, i, r].rearrange("p t h v -> p t (h v)")).then_inc(v_stored[i], 16)
                sp.dma_start(tokens.rearrange("(b g) p t -> b p g t", g=CHUNKS)[b],
                             t_tok[:, :, :].rearrange("p (g t) c -> p g (t c)", g=CHUNKS)).then_inc(t_stored, 16)
                load_x((b + 1) % IMAGES)
            sp.wait_ge(y_loaded, 16 * DIRS * (IMAGES + 1))
            sp.wait_ge(x_loaded, X_COUNT * (IMAGES + 1))
            sp.wait_ge(t_stored, 16 * IMAGES)
            for i in range(2):
                sp.wait_ge(qk_stored[i], 16 * PARTS * IMAGES * CHUNKS)
                sp.wait_ge(v_stored[i], 16 * GROUPS * IMAGES * CHUNKS // 2)

        @block.gpsimd
        def _(pool):
            nc.gpsimd.memset(v_sb[:, :, :, :, :, :], 0.0).then_inc(ready, 1)
            pool.wait_ge(ready, 1)
            nc.gpsimd.memset(v_sb[:, :, :, :, :, HEAD:HEAD + 1].rearrange("p a b t h v -> p (a b t h) v"), 1.0).then_inc(ready, 1)
            nc.gpsimd.memset(eps[:, :], LN_EPS_SCAN).then_inc(ready, 1)
            with pool.Fori(0, IMAGES) as b:
                first = b * CHUNKS
                for g in range(CHUNKS):
                    for s in range(2):
                        n = 2 * (first + g) + s
                        pool.wait_ge(mid_done, n + 1)
                        pool.wait_ge(qk_stored[g % 2], (b * (CHUNKS // 2) + g // 2) * (2 * 16 * PARTS))
                        nc.gpsimd.tensor_tensor(lo[:, g % 2, s, :], rest[:, g % 2, s, :], mid[:, g % 2, s, :], ALU.subtract).then_inc(lo_done, 1)

        @block.tensor
        def _(pe):
            ident, mean = CONSTANTS.of(c, "ident"), CONSTANTS.of(c, "mean")
            cv_out, cv3, qkv = DERIVED.of(d, "cv_out"), WEIGHTS.of(w, "cv3"), WEIGHTS.of(w, "qkv")
            with pe.Fori(0, IMAGES) as b:
                first = b * CHUNKS
                pe.wait_ge(added, (b + 1) * 3)
                pe.wait_ge(v_copied, first)
                pe.wait_ge(rest_done, 2 * first)
                for g in range(CHUNKS + 1):
                    if g < CHUNKS:
                        pe.wait_ge(centred, first + g)
                        nc.tensor.matmul(ps_mean[:, :], mean, y[0][:, cols(g)], start=True, stop=True).then_inc(mean_done, 1)
                    if g:
                        pe.wait_ge(squared, first + g)
                        pe.wait_ge(log_done, first + g - 1)
                        nc.tensor.matmul(ps_var[:, :], mean, y[1][:, cols(g - 1)], start=True, stop=True).then_inc(var_done, 1)
                for g in range(CHUNKS + 2):
                    if g < CHUNKS:
                        pe.wait_ge(gated, first + g + 1)
                        pe.wait_ge(xr_silu, first + g)
                        nc.tensor.matmul(ps_xr[:, :], cv_out, y[2][:, cols(g)], start=True, stop=True).then_inc(xr_done, 1)
                    if 0 < g < CHUNKS + 1:
                        h = g - 1
                        pe.wait_ge(xr_silu, first + h + 1)
                        pe.wait_ge(left_loaded[h % 2], (b * (CHUNKS // 2) + h // 2) * 16 + 16)
                        pe.wait_ge(out_silu, first + h)
                        nc.tensor.matmul(ps_out[:, :], cv3, both[:, h % 2, :], start=True, stop=True).then_inc(out_done, 1)
                    if g > 1:
                        h = g - 2
                        pe.wait_ge(out_silu, first + h + 1)
                        pe.wait_ge(t_added, first + h)
                        for t in range(BLOCK_TILES):
                            last = nc.tensor.transpose(ps_tok[:, t * P:(t + 1) * P], o_ch[:, h % 2, t * P:(t + 1) * P], ident)
                        last.then_inc(tok_done, 1)
                pe.wait_ge(log_done, first + CHUNKS)
                for g in range(CHUNKS + 1):
                    if g < CHUNKS:
                        pe.wait_ge(xn_done, first + g + 1)
                        pe.wait_ge(xn_copied, first + g)
                        for t in range(BLOCK_TILES):
                            last = nc.tensor.transpose(ps_xn[:, t * P:(t + 1) * P], xn_tok[:, g % 2, t * P:(t + 1) * P], ident)
                        last.then_inc(xn_turned, 1)
                    if g:
                        h = g - 1
                        pe.wait_ge(xn_copied, first + h + 1)
                        for s, done in ((0, q_done), (1, k_done)):
                            if h >= 2:
                                pe.wait_ge(rest_done, 2 * (first + h) - 3 + s)
                            nc.tensor.matmul(ps_qk[h % 2][s][:, :], qkv[:, s * P:(s + 1) * P], xn_ch[:, h % 2, :], start=True, stop=True).then_inc(done, 1)
                        pe.wait_ge(v_copied, first + h)
                        for t in range(BLOCK_TILES):
                            last = nc.tensor.matmul(ps_v[:, t * P:(t + 1) * P], xn_ch[:, h % 2, t * P:(t + 1) * P],
                                                    qkv[:, 2 * P:3 * P], start=True, stop=True)
                        last.then_inc(v_done, 1)

        @block.scalar
        def _(act):
            act.wait_ge(ready, 3)
            with act.Fori(0, IMAGES) as b:
                first = b * CHUNKS
                for g in range(CHUNKS + 1):
                    if g < CHUNKS:
                        act.wait_ge(centred, first + g + 1)
                        nc.scalar.activation(y[1][:, cols(g)], y[0][:, cols(g)], ACT.Square).then_inc(squared, 1)
                    if g:
                        act.wait_ge(var_done, first + g)
                        nc.scalar.activation(y[3][:, cols(g - 1)], ps_var[:, :], ACT.Ln, bias=eps[:, :]).then_inc(log_done, 1)
                for g in range(CHUNKS + 1):
                    if g < CHUNKS:
                        act.wait_ge(log_done, first + g + 1)
                        nc.scalar.activation(y[3][:, cols(g)], y[3][:, cols(g)], ACT.Exp, scale=-0.5).then_inc(rstd_done, 1)
                    if g:
                        act.wait_ge(norm_done, first + g)
                        nc.scalar.activation(y[1][:, cols(g - 1)], y[0][:, cols(g - 1)], ACT.Identity, bias=WEIGHTS.of(w, "ln_b"),
                                             scale=WEIGHTS.of(w, "ln_g")).then_inc(scale_done, 1)
                for g in range(CHUNKS + 1):
                    if g < CHUNKS:
                        act.wait_ge(xr_done, first + g + 1)
                        act.wait_ge(out_done, first + max(g - 1, 0))
                        nc.scalar.activation(both[HALF:P, g % 2, :], ps_xr[HALF:P, :], ACT.Silu, bias=WEIGHTS.of(w, "cv_b", start=HALF),
                                             scale=WEIGHTS.of(w, "cv_g", start=HALF)).then_inc(xr_silu, 1)
                    if g:
                        h = g - 1
                        act.wait_ge(out_done, first + h + 1)
                        act.wait_ge(tok_done, first + max(h - 1, 0))
                        nc.scalar.activation(o_ch[:, h % 2, :], ps_out[:, :], ACT.Silu, bias=WEIGHTS.of(w, "cv3_b"),
                                             scale=WEIGHTS.of(w, "cv3_g")).then_inc(out_silu, 1)
                act.wait_ge(moments_done, (b + 1) * TILES)
                act.wait_ge(t_rstd_done, b)
                nc.scalar.activation(t_log[:, :], moments[:, :, 1], ACT.Ln, bias=eps[:, :]).then_inc(t_log_done, 1)
                act.wait_ge(t_log_done, b + 1)
                act.wait_ge(xn_done, first)
                nc.scalar.activation(t_rstd[:, :], t_log[:, :], ACT.Exp, scale=-0.5).then_inc(t_rstd_done, 1)
                for g in range(CHUNKS + 1):
                    if g < CHUNKS:
                        act.wait_ge(xn_turned, first + g + 1)
                        act.wait_ge(v_done, first + max(g - 1, 0))
                        nc.scalar.activation(xn_ch[:, g % 2, :], ps_xn[:, :], ACT.Copy).then_inc(xn_copied, 1)
                    if g:
                        h, i = g - 1, (g - 1) % 2
                        act.wait_ge(qk_stored[i], (b * (CHUNKS // 2) + h // 2) * (2 * 16 * PARTS))
                        for s, done in ((0, q_done), (1, k_done)):
                            act.wait_ge(done, first + h + 1)
                            nc.scalar.activation(hi[:, i, s, :], ps_qk[i][s][:, :], ACT.Copy, scale=HEAD_SCALE if s == 0 else 1.0).then_inc(hi_done, 1)
                        act.wait_ge(v_done, first + h + 1)
                        act.wait_ge(v_stored[i], (b * (CHUNKS // 2) + h // 2) * 16 * GROUPS)
                        for r in range(GROUPS):
                            last = nc.scalar.activation(
                                v_sb[:, i, r, :, :, 0:HEAD],
                                ps_v[:, :].rearrange("p (t r h v) -> p r t h v", r=GROUPS, h=GROUP_HEADS, v=HEAD)[:, r], ACT.Copy)
                        last.then_inc(v_copied, 1)
                        for s in range(2):
                            act.wait_ge(rest_done, 2 * (first + h) + s + 1)
                            nc.scalar.activation(mid[:, i, s, :], rest[:, i, s, :], ACT.Copy).then_inc(mid_done, 1)

        @block.vector
        def _(dve):
            def add_directions(b, k):
                dve.wait_ge(y_loaded, b * 16 * DIRS + 16 * DIRS)
                if k < 2:
                    nc.vector.tensor_tensor(y[k][:, :], y[k][:, :], y[k + 2][:, ::-1], ALU.add).then_inc(added, 1)
                else:
                    dve.wait_ge(added, b * 3 + 2)
                    rows = y[0][:, :].rearrange("p (r s) -> p r s", s=SIDE)
                    nc.vector.tensor_tensor(rows, rows, y[1][:, :].rearrange("p (s r) -> p r s", r=SIDE), ALU.add).then_inc(added, 1)

            dve.wait_ge(ready, 3)
            for k in range(3):
                add_directions(0, k)
            with dve.Fori(0, IMAGES) as b:
                first = b * CHUNKS
                for g in range(CHUNKS):
                    dve.wait_ge(mean_done, first + g + 1)
                    dve.wait_ge(added, b * 3 + 3)
                    nc.vector.tensor_tensor(y[0][:, cols(g)], y[0][:, cols(g)], ps_mean[:, :], ALU.subtract).then_inc(centred, 1)
                for g in range(CHUNKS + 1):
                    if g < CHUNKS:
                        dve.wait_ge(rstd_done, first + g + 1)
                        dve.wait_ge(centred, first + g + 1)
                        nc.vector.tensor_tensor(y[0][:, cols(g)], y[0][:, cols(g)], y[3][:, cols(g)], ALU.mult).then_inc(norm_done, 1)
                    if g:
                        h = g - 1
                        dve.wait_ge(scale_done, first + h + 1)
                        dve.wait_ge(gate_loaded[h % 2], (b * (CHUNKS // 2) + h // 2) * 16 + 16)
                        nc.vector.tensor_tensor(y[2][:, cols(h)], y[1][:, cols(h)], gate_in[:, h % 2, :], ALU.mult).then_inc(gated, 1)
                dve.wait_ge(x_loaded, b * X_COUNT + X_COUNT)
                dve.wait_ge(t_stored, b * 16)
                dve.wait_ge(xn_done, first)
                for g in range(CHUNKS):
                    tiles = slice(g * BLOCK_TILES, (g + 1) * BLOCK_TILES)
                    dve.wait_ge(tok_done, first + g + 1)
                    nc.vector.tensor_tensor(t_tok[:, tiles, :], x_tok[:, tiles, :], ps_tok[:, :].rearrange("p (t c) -> p t c", c=CH),
                                            ALU.add).then_inc(t_added, 1)
                    dve.wait_ge(t_added, first + g + 1)
                    dve.wait_ge(t_log_done, b)
                    for t in range(g * BLOCK_TILES, (g + 1) * BLOCK_TILES):
                        nc.vector.bn_stats(stats[:, t, :], t_tok[:, t, :]).then_inc(stats_done, 1)
                    stats_done_due = worked_out(dve, b * TILES + (g + 1) * BLOCK_TILES)
                    dve.wait_ge(ready, 3)
                    dve.wait_ge(stats_done, stats_done_due)
                    for t in range(g * BLOCK_TILES, (g + 1) * BLOCK_TILES):
                        nc.vector.bn_aggr(moments[:, t, :], stats[:, t, :]).then_inc(moments_done, 1)
                dve.wait_ge(moments_done, (b + 1) * TILES)
                dve.wait_ge(t_rstd_done, b + 1)
                for g in range(CHUNKS + 1):
                    if g < CHUNKS:
                        dve.wait_ge(xn_turned, first + max(g - 1, 0))
                        for t in range(BLOCK_TILES):
                            n = g * BLOCK_TILES + t
                            last = nc.vector.tensor_scalar(xn_tok[:, g % 2, t * P:(t + 1) * P], t_tok[:, n, :], moments[:, n, 0:1],
                                                           t_rstd[:, n:n + 1], ALU.subtract, ALU.mult)
                        last.then_inc(xn_done, 1)
                    if g:
                        h = g - 1
                        for s in range(2):
                            n = 2 * (first + h) + s
                            dve.wait_ge(hi_done, n + 1)
                            dve.wait_ge(lo_done, n - 3 if h >= 2 else 2 * first)
                            nc.vector.scalar_tensor_tensor(out=rest[:, h % 2, s, :], in0=ps_qk[h % 2][s][:, :], scalar=HEAD_SCALE if s == 0 else 1.0,
                                                           in1=hi[:, h % 2, s, :], op0=ALU.mult, op1=ALU.subtract).then_inc(rest_done, 1)
                        if g >= CHUNKS - 2:
                            add_directions(b + 1, g - (CHUNKS - 2))


Q_PARTS, K_PARTS = (0, 0, 1, 0, 1, 2), (0, 1, 0, 2, 1, 0)
SCORE_ROWS = HEAD * len(Q_PARTS)
ROWS_MAX = SCORE_ROWS + PARTS
UNITS = IMAGES * GROUPS
QBLOCKS = TOK // BANK
BLOCK_STEPS = [BLOCK_TILES * (i + 1) for i in range(QBLOCKS)]
STEPS = [BLOCK_TILES * i * (i + 1) // 2 for i in range(QBLOCKS + 1)]
TOP = GROUP_HEADS * BLOCK_TILES
Q_AHEAD = QBLOCKS // 2
AHEAD = 3
TARGETS = [(j + AHEAD) % QBLOCKS for j in range(QBLOCKS)]
ITEMS = [(j, kk, n) for j in TARGETS for kk in range(j + 1) for n in range(TOP)]
OWN_ITEMS = sum(TOP * (j + 1) for j in range(AHEAD, QBLOCKS))
OWN_STEPS = STEPS[QBLOCKS - 1] - 5
NEXT_START, NEXT_END = STEPS[QBLOCKS - 1] + 10, STEPS[QBLOCKS] - 2
K_CHUNKS = [(0, 1), (1, 2), (2, 3), (3, 4), (4, QBLOCKS)]
STEP_COLUMNS = [P + P * (BLOCK_TILES - max(0, y - i * BLOCK_TILES)) - (P if i and 1 <= y <= BLOCK_TILES else 0) for i in range(QBLOCKS) for y in range(BLOCK_STEPS[i])]


def items_until(x):
    columns = lambda a, b: sum(STEP_COLUMNS[a:b])
    own = OWN_ITEMS * columns(0, min(x, OWN_STEPS)) // columns(0, OWN_STEPS)
    after = columns(NEXT_START, min(x, NEXT_END)) if x > NEXT_START else 0
    return own + (len(ITEMS) - OWN_ITEMS) * after // columns(NEXT_START, NEXT_END)


def items_of(x):
    return [(m, *ITEMS[m]) for m in range(items_until(x), items_until(x + 1))]


def completed(x):
    return [(k, j) for k, j in enumerate(TARGETS)
            if x >= 0 and items_until(x) < sum(TOP * (t + 1) for t in TARGETS[:k + 1]) <= items_until(x + 1)]


def attention(nc, c, c16, q_parts, k_parts, values, maxima, attended):
    with ExitStack() as ctx:
        sb = lambda name, shape, dt=F32: ctx.enter_context(nc.sbuf_tensor("at_" + name, shape, dt))
        pb = lambda name, n=BANK: ctx.enter_context(nc.psum_tensor("at_" + name, [P, n], F32))
        sem = lambda name: ctx.enter_context(nc.semaphore("at_" + name))
        k_sb = sb("k_sb", [ROWS_MAX, GROUP_HEADS, TOK], BF16)
        q_sb = sb("q_sb", [ROWS_MAX, QBLOCKS, GROUP_HEADS, BANK], BF16)
        v_sb = sb("v_sb", [P, TILES, P])
        weights = sb("weights", [P, 2, 2, 2, BANK])
        top, neg = sb("top", [P, TOP, QBLOCKS]), sb("neg", [P, TOP])
        m_rest, m_row = sb("m_rest", [TOP, P]), sb("m_row", [TOP, PARTS, P], BF16)
        o_sb, inverse, o_out = sb("o_sb", [P, BANK]), sb("inverse", [P, BANK]), sb("o_out", [P, BANK])
        ps_s = [pb(f"ps_s{i}", 2 * BANK) for i in range(2)]
        ps_m = [pb(f"ps_m{i}") for i in range(2)]
        ps_o, ps_x = pb("ps_o"), pb("ps_x")
        names = ("ones k_loaded q_loaded v_loaded scored weighed summed max_scored maxed negated turned "
                 "m_hi_done m_rest_done m_mid_done m_lo_done m_stored m_loaded o_copied sums_done inverted scaled o_stored").split()
        (ones, k_loaded, q_loaded, v_loaded, scored, weighed, summed, max_scored, maxed, negated, turned,
         m_hi_done, m_rest_done, m_mid_done, m_lo_done, m_stored, m_loaded, o_copied, sums_done, inverted, scaled, o_stored) = map(sem, names)
        block = ctx.enter_context(nc.Block())
        PROLOGUE = TOP * AHEAD * (AHEAD + 1) // 2
        PROLOGUE_ITEMS = [(m, j, kk, n) for m, (j, kk, n) in
                          enumerate((j, kk, n) for j in range(AHEAD) for kk in range(j + 1) for n in range(TOP))]
        Q_COUNT, K_COUNT = 16 * len(Q_PARTS), 16 * len(K_PARTS)

        def at_least(engine, semaphore, value):
            if not isinstance(value, int) or value > 0:
                engine.wait_ge(semaphore, value)

        def step(u, x):
            return u * STEPS[-1] + x

        def block_of(u, i):
            return u * QBLOCKS + i

        def item(u, m):
            return u * len(ITEMS) + (PROLOGUE + m)

        def target(u, k):
            return u * QBLOCKS + (AHEAD + k)

        @block.sync
        def _(sp):
            def load_k(u, first, end):
                source = k_parts.rearrange("b s (r h d) t -> b r s d h t", r=GROUPS, h=GROUP_HEADS)[u // GROUPS, u % GROUPS]
                for g, part in enumerate(K_PARTS):
                    sp.dma_start(k_sb[g * HEAD:(g + 1) * HEAD, :, first * BANK:end * BANK],
                                 source[part, :, :, first * BANK:end * BANK]).then_inc(k_loaded, 16)
                tiles = slice(first * BLOCK_TILES, end * BLOCK_TILES)
                sp.dma_start(v_sb[:, tiles, :], values[u // GROUPS, u % GROUPS, :, tiles, :]).then_inc(v_loaded, 16)

            def load_q(u, i):
                source = q_parts.rearrange("b s (r h d) t -> b r s d h t", r=GROUPS, h=GROUP_HEADS)[u // GROUPS, u % GROUPS]
                for g, part in enumerate(Q_PARTS):
                    sp.dma_start(q_sb[g * HEAD:(g + 1) * HEAD, i], source[part, :, :, i * BANK:(i + 1) * BANK]).then_inc(q_loaded, 16)

            def move_maxima(number, i):
                at_least(sp, m_loaded, number * 16)
                sp.wait_ge(m_lo_done, number + 1)
                sp.dma_start(maxima, m_row[:, :, :]).then_inc(m_stored, 16)
                sp.wait_ge(m_stored, number * 16 + 16)
                sp.dma_start(q_sb[SCORE_ROWS:ROWS_MAX, i].rearrange("s h (t q) -> s (h t) q", q=P),
                             maxima.rearrange("n s q -> s n q")).then_inc(m_loaded, 16)

            for i in range(AHEAD):
                at_least(sp, q_loaded, i * Q_COUNT)
                load_q(0, i)
                at_least(sp, k_loaded, i * K_COUNT)
                at_least(sp, v_loaded, i * 16)
                load_k(0, *K_CHUNKS[i])
            sp.wait_ge(k_loaded, AHEAD * K_COUNT)
            sp.wait_ge(v_loaded, AHEAD * 16)
            load_k(0, *K_CHUNKS[AHEAD])
            for i in range(AHEAD, Q_AHEAD):
                sp.wait_ge(q_loaded, i * Q_COUNT)
                load_q(0, i)
            for i in range(AHEAD):
                move_maxima(i, i)
            with sp.Fori(0, UNITS) as u:
                nc.cur_bb.disable_value_cache()
                for i in range(QBLOCKS):
                    n = block_of(u, i)
                    q_loaded_due, summed_due = worked_out(sp, (n + Q_AHEAD) * Q_COUNT), worked_out(sp, step(u, STEPS[i]))
                    sp.wait_ge(v_loaded, 16)
                    sp.wait_ge(q_loaded, q_loaded_due)
                    sp.wait_ge(summed, summed_due)
                    load_q((u + 1) % UNITS if i + Q_AHEAD >= QBLOCKS else u, (i + Q_AHEAD) % QBLOCKS)
                    if i == 0:
                        sp.wait_ge(k_loaded, (u * len(K_CHUNKS) + (AHEAD + 1)) * K_COUNT)
                        sp.wait_ge(v_loaded, (u * len(K_CHUNKS) + (AHEAD + 1)) * 16)
                        load_k(u, *K_CHUNKS[AHEAD + 1])
                    moves = [(k, j) for x in range(STEPS[i], STEPS[i + 1]) for k, j in completed(x - 2)]
                    for g in range(AHEAD + 1):
                        if i == QBLOCKS - 1:
                            sp.wait_ge(k_loaded, (u * len(K_CHUNKS) + (len(K_CHUNKS) + g)) * K_COUNT)
                            sp.wait_ge(v_loaded, (u * len(K_CHUNKS) + (len(K_CHUNKS) + g)) * 16)
                            sp.wait_ge(summed, step(u, STEPS[i] + K_CHUNKS[g][1] * BLOCK_TILES))
                            load_k((u + 1) % UNITS, *K_CHUNKS[g])
                            for k, j in moves:
                                if j == g - 2:
                                    move_maxima(target(u, k), j)
                    for k, j in moves:
                        if i < QBLOCKS - 1 or j not in (0, 1):
                            move_maxima(target(u, k), j)
                    sp.wait_ge(scaled, n + 1)
                    sp.dma_start(attended[u % GROUPS, (u // GROUPS) * QBLOCKS + i], o_out[:, :]).then_inc(o_stored, 16)
            sp.wait_ge(o_stored, 16 * UNITS * QBLOCKS)
            sp.wait_ge(m_loaded, 16 * (UNITS * QBLOCKS + AHEAD))
            sp.wait_ge(q_loaded, Q_COUNT * (UNITS * QBLOCKS + Q_AHEAD))
            sp.wait_ge(k_loaded, K_COUNT * (UNITS * len(K_CHUNKS) + (AHEAD + 1)))
            sp.wait_ge(v_loaded, 16 * (UNITS * len(K_CHUNKS) + (AHEAD + 1)))

        @block.tensor
        def _(pe):
            ident, head_sum = CONSTANTS.of(c, "ident"), CONSTANTS.of(c, "head_sum")
            ident16, above, below = (CONSTANTS16.of(c16, n) for n in ("ident", "above", "below"))

            def max_scores(number, m, i, kk, n):
                h, t = n // BLOCK_TILES, n % BLOCK_TILES
                diag = kk == i
                width = (t + 1) * P if diag else BANK
                at_least(pe, maxed, number - 1)
                out = ps_m[m % 2]
                last = nc.tensor.matmul(out[:, 0:width], q_sb[0:SCORE_ROWS, i, h, t * P:(t + 1) * P],
                                        k_sb[0:SCORE_ROWS, h, kk * BANK:kk * BANK + width], start=True, stop=not diag)
                if diag:
                    last = nc.tensor.matmul(out[:, width - P:width], ident16, below, start=False, stop=True)
                last.then_inc(max_scored, 1)

            def unit_max_scores(u, items):
                for m, j, kk, n in items:
                    if kk == 0 and n == 0:
                        pe.wait_ge(q_loaded, (target(u, TARGETS.index(j)) + 1) * Q_COUNT)
                        if j < AHEAD:
                            pe.wait_ge(k_loaded, (u * len(K_CHUNKS) + (len(K_CHUNKS) + 1 + j)) * K_COUNT)
                    if n == 0 and kk == j and j in (AHEAD, AHEAD + 1):
                        pe.wait_ge(k_loaded, (u * len(K_CHUNKS) + (j + 1)) * K_COUNT)
                    max_scores(item(u, m), m, j, kk, n)

            def scores(u, i, y, p):
                diag, off = y >= i * BLOCK_TILES, max(0, y - i * BLOCK_TILES) * P
                pe.wait_ge(weighed, (step(u, STEPS[i] + y) * 2) - 1 + p) if (i or y) else at_least(pe, weighed, step(u, 0) * 2)
                for h in (2 * p, 2 * p + 1):
                    out = ps_s[p][:, (h % 2) * BANK + off:(h % 2 + 1) * BANK]
                    last = nc.tensor.matmul(out, k_sb[:, h, y * P:(y + 1) * P], q_sb[:, i, h, off:BANK], start=True, stop=not diag)
                    if diag:
                        last = nc.tensor.matmul(out[:, 0:P], ident16, above, start=False, stop=True)
                last.then_inc(scored, 1)

            def weighted_sum(u, i, y):
                off = max(0, y - i * BLOCK_TILES) * P
                end = y + 1 == BLOCK_STEPS[i]
                if end:
                    pe.wait_ge(weighed, step(u, STEPS[i] + y) * 2 + 2)
                if y == 0:
                    at_least(pe, o_copied, block_of(u, i))
                for h in range(GROUP_HEADS):
                    last = nc.tensor.matmul(ps_o[h * SLOT:(h + 1) * SLOT, off:BANK], v_sb[:, y, h * SLOT:(h + 1) * SLOT],
                                            weights[:, y % 2, h // 2, h % 2, off:BANK], start=(y == 0), stop=end, skip_group_check=True)
                last.then_inc(summed, 1)

            def turn_maxima(number, blocks_done):
                pe.wait_ge(negated, number + 1)
                at_least(pe, m_rest_done, number)
                at_least(pe, inverted, blocks_done * BLOCK_TILES)
                nc.tensor.transpose(ps_x[0:TOP, 0:P], neg[:, :], ident).then_inc(turned, 1)

            def head_sums(u, i):
                n = block_of(u, i)
                pe.wait_ge(o_copied, n + 1)
                turns = sum(len(completed(z)) for z in range(STEPS[i + 1] if i + 1 < QBLOCKS else STEPS[-1] - 1))
                pe.wait_ge(m_rest_done, target(u, turns))
                at_least(pe, inverted, n * BLOCK_TILES)
                nc.tensor.matmul(ps_x[:, :], head_sum, o_sb[:, :], start=True, stop=True).then_inc(sums_done, 1)

            pe.wait_ge(ones, 1)
            for m, j, kk, n in PROLOGUE_ITEMS:
                if kk == 0 and n == 0:
                    pe.wait_ge(q_loaded, (j + 1) * Q_COUNT)
                    pe.wait_ge(k_loaded, (j + 1) * K_COUNT)
                max_scores(m, m, j, kk, n)
                if kk == j and n == TOP - 1:
                    turn_maxima(j, 0)
            with pe.Fori(0, UNITS) as u:
                nc.cur_bb.disable_value_cache()
                for i in range(QBLOCKS):
                    pe.wait_ge(m_loaded, block_of(u, i) * 16 + 16)
                    if i in (0, AHEAD, AHEAD + 1):
                        pe.wait_ge(v_loaded, (u * len(K_CHUNKS) + (i + 1 if i else AHEAD)) * 16)
                    for p in range(2):
                        scores(u, i, 0, p)
                    for y in range(BLOCK_STEPS[i]):
                        x = STEPS[i] + y
                        items = items_of(x)
                        early = min(2, len(items))
                        late = max(early, len(items) - 2)
                        unit_max_scores(u, items[:early])
                        if y + 1 < BLOCK_STEPS[i]:
                            scores(u, i, y + 1, 0)
                        for k, _ in completed(x - 1):
                            turn_maxima(target(u, k), block_of(u, i) - (1 if y == 0 and i else 0))
                        unit_max_scores(u, items[early:late])
                        if y + 1 < BLOCK_STEPS[i]:
                            scores(u, i, y + 1, 1)
                        unit_max_scores(u, items[late:])
                        weighted_sum(u, i, y)
                        if y == 0 and i:
                            head_sums(u, i - 1)
                head_sums(u, QBLOCKS - 1)

        @block.scalar
        def _(act):
            def weigh(u, i, y):
                s = step(u, STEPS[i] + y)
                off = max(0, y - i * BLOCK_TILES) * P
                if STEPS[i] + y >= 2:
                    act.wait_ge(summed, s - 1)
                else:
                    act.wait_ge(summed, step(u, 0))
                for p in range(2):
                    act.wait_ge(scored, s * 2 + p + 1)
                    nc.scalar.activation(weights[:, y % 2, p, :, off:BANK], ps_s[p][:, :].rearrange("p (h q) -> p h q", q=BANK)[:, :, off:BANK],
                                         ACT.Exp).then_inc(weighed, 1)

            def first_part(number):
                act.wait_ge(turned, number + 1)
                at_least(act, m_stored, number * 16)
                nc.scalar.activation(m_row[:, 0, :], ps_x[0:TOP, 0:P], ACT.Copy).then_inc(m_hi_done, 1)

            def second_part(number):
                act.wait_ge(m_rest_done, number + 1)
                nc.scalar.activation(m_row[:, 1, :], m_rest[:, :], ACT.Copy).then_inc(m_mid_done, 1)

            for k in range(AHEAD):
                first_part(k)
                second_part(k)
            with act.Fori(0, UNITS) as u:
                nc.cur_bb.disable_value_cache()
                for i in range(QBLOCKS):
                    for y in range(BLOCK_STEPS[i]):
                        x = STEPS[i] + y
                        weigh(u, i, y)
                        for k, _ in completed(x - 2):
                            second_part(target(u, k))
                        for k, _ in completed(x - 1):
                            first_part(target(u, k))
                    act.wait_ge(summed, step(u, STEPS[i + 1]))
                    at_least(act, scaled, block_of(u, i))
                    act.wait_ge(sums_done, block_of(u, i))
                    nc.scalar.activation(o_sb[:, :], ps_o[:, :], ACT.Copy).then_inc(o_copied, 1)

        @block.gpsimd
        def _(pool):
            nc.gpsimd.memset(k_sb[SCORE_ROWS:ROWS_MAX, :, :], 1.0).then_inc(ones, 1)
            with pool.Fori(0, UNITS * QBLOCKS) as n:
                pool.wait_ge(inverted, n * BLOCK_TILES + BLOCK_TILES)
                pool.wait_ge(o_stored, n * 16)
                nc.gpsimd.tensor_tensor(o_out[:, :], o_sb[:, :], inverse[:, :], ALU.mult).then_inc(scaled, 1)

        @block.vector
        def _(dve):
            def maximum(number, m, i, kk, n):
                t = n % BLOCK_TILES
                width = (t + 1) * P if kk == i else BANK
                dve.wait_ge(max_scored, number + 1)
                nc.vector.reduce_max(top[:, n, kk:kk + 1], ps_m[m % 2][:, 0:width], AX.X).then_inc(maxed, 1)

            def negate_maxima(count, number, i):
                dve.wait_ge(maxed, count)
                at_least(dve, turned, number)
                nc.vector.tensor_reduce(neg[:, :], top[:, :, 0:i + 1], AX.X, ALU.max, negate=True).then_inc(negated, 1)

            def after_first_part(number):
                dve.wait_ge(m_hi_done, number + 1)
                at_least(dve, m_lo_done, number)
                nc.vector.tensor_tensor(m_rest[:, :], ps_x[0:TOP, 0:P], m_row[:, 0, :], ALU.subtract).then_inc(m_rest_done, 1)

            def third_part(number):
                dve.wait_ge(m_mid_done, number + 1)
                nc.vector.tensor_tensor(m_row[:, 2, :], m_rest[:, :], m_row[:, 1, :], ALU.subtract).then_inc(m_lo_done, 1)

            def invert(u, i, t):
                dve.wait_ge(sums_done, block_of(u, i) + 1)
                dve.wait_ge(scaled, block_of(u, i))
                nc.vector.reciprocal(inverse[:, t * P:(t + 1) * P], ps_x[:, t * P:(t + 1) * P]).then_inc(inverted, 1)

            def parts_at(i, y):
                turns = [z for z in range(1, BLOCK_TILES + 1) if completed(STEPS[i] + z - 1)]
                last = min([BLOCK_TILES] + turns)
                return [t for t in range(BLOCK_TILES) if i and min(t + 1, last) == y]

            def unit_maxima(u, items):
                for m, j, kk, n in items:
                    if kk == 0 and n == 0:
                        dve.wait_ge(negated, target(u, TARGETS.index(j)))
                    maximum(item(u, m), m, j, kk, n)
                    if kk == j and n == TOP - 1:
                        negate_maxima(item(u, m + 1), target(u, TARGETS.index(j)), j)

            for m, j, kk, n in PROLOGUE_ITEMS:
                if kk == 0 and n == 0:
                    at_least(dve, negated, j)
                maximum(m, m, j, kk, n)
                if kk == j and n == TOP - 1:
                    negate_maxima(m + 1, j, j)
                    after_first_part(j)
                    third_part(j)
            with dve.Fori(0, UNITS) as u:
                nc.cur_bb.disable_value_cache()
                for i in range(QBLOCKS):
                    for y in range(BLOCK_STEPS[i]):
                        x = STEPS[i] + y
                        items = items_of(x)
                        unit_maxima(u, items[:2])
                        for t in parts_at(i, y):
                            invert(u, i - 1, t)
                        for k, _ in completed(x - 1):
                            after_first_part(target(u, k))
                        for k, _ in completed(x - 2):
                            third_part(target(u, k))
                        unit_maxima(u, items[2:])
                for t in range(BLOCK_TILES):
                    invert(u, QBLOCKS - 1, t)


ALL_BLOCKS = IMAGES * CHUNKS


def experts(nc, w, c, c16, bias16, attended, tokens, out):
    with ExitStack() as ctx:
        sb = lambda name, shape, dt=F32: ctx.enter_context(nc.sbuf_tensor("ex_" + name, shape, dt))
        pb = lambda name, n=BANK: ctx.enter_context(nc.psum_tensor("ex_" + name, [P, n], F32))
        sem = lambda name: ctx.enter_context(nc.semaphore("ex_" + name))
        att, tok = sb("att", [P, 2, GROUPS, BANK]), sb("tok", [P, 2, BANK])
        t_sb, xn_tok, xn_ch = sb("t_sb", [P, 2, BANK]), sb("xn_tok", [P, BANK]), sb("xn_ch", [P, 2, BANK])
        stats, moments = sb("stats", [P, BLOCK_TILES, 6]), sb("moments", [P, BLOCK_TILES, 2])
        log_var, rstd, eps = sb("log_var", [P, BLOCK_TILES]), sb("rstd", [P, BLOCK_TILES]), sb("eps", [P, 1])
        tile_by = lambda name, n, dt=F32: sb(name, [P, BLOCK_TILES, n], dt)
        logits, best, index = tile_by("logits", EXPERTS), tile_by("best", 8), tile_by("index", 8, mybir.dt.uint32)
        index_f, order = tile_by("index_f", 8), sb("order", [P, EXPERTS])
        order_i = sb("order_i", [P, EXPERTS], mybir.dt.int32)
        is_first, is_second, first_w, second_w = (tile_by(n, EXPERTS) for n in ("is_first", "is_second", "first_w", "second_w"))
        gap, ratio, total, share1, share2 = (sb(n, [P, BLOCK_TILES]) for n in ("gap", "ratio", "total", "share1", "share2"))
        mix = sb("mix", [P, 2, BLOCK_TILES, EXPERTS])
        product = sb("product", [P, 2, EXPERTS * CH])
        half, quarter = sb("half", [P, 2, EXPERTS * CH // 2]), sb("quarter", [P, 2, EXPERTS * CH // 4])
        mixed, out_sb = sb("mixed", [P, 2, BANK]), sb("out_sb", [P, 2, BANK])
        ps_proj, ps_xn, ps_router = pb("ps_proj"), pb("ps_xn"), pb("ps_router")
        ps_e = [pb(f"ps_e{i}", 2 * BANK) for i in range(2)]
        names = ("ready att_loaded tok_loaded projected added stats_done moments_done log_done rstd_done xn_done xn_turned xn_copied "
                 "routed logits_done best_done index_done small second_done gap_done ratio_done mix_done expert_done product_done halved quartered "
                 "tile_mixed out_done").split()
        (ready, att_loaded, tok_loaded, projected, added, stats_done, moments_done, log_done, rstd_done, xn_done, xn_turned, xn_copied,
         routed, logits_done, best_done, index_done, small, second_done, gap_done, ratio_done, mix_done, expert_done, product_done, halved, quartered,
         tile_mixed, out_done) = map(sem, names)
        stored = [sem(f"stored{i}") for i in range(2)]
        block = ctx.enter_context(nc.Block())
        SMALL = 7
        tile_cols = lambda t: slice(t * P, (t + 1) * P)

        @block.sync
        def _(sp):
            def load(n, source, i):
                for r in range(GROUPS):
                    sp.dma_start(att[:, i, r, :], attended[r, source]).then_inc(att_loaded, 16)
                sp.dma_start(tok[:, i, :], tokens[source]).then_inc(tok_loaded, 16)

            load(0, 0, 0)
            sp.wait_ge(att_loaded, 16 * GROUPS)
            sp.wait_ge(tok_loaded, 16)
            load(1, 1, 1)
            with sp.Fori(0, ALL_BLOCKS // 2) as k:
                for i in range(2):
                    n = k * 2 + i
                    att_due, tok_due, added_due = (worked_out(sp, v) for v in (n * (16 * GROUPS) + 2 * 16 * GROUPS, n * 16 + 32, n + 1))
                    sp.wait_ge(tok_loaded, 16)
                    sp.wait_ge(att_loaded, att_due)
                    sp.wait_ge(tok_loaded, tok_due)
                    sp.wait_ge(added, added_due)
                    load(n + 2, (n + 2) % ALL_BLOCKS, i)
                    sp.wait_ge(out_done, n + 1)
                    sp.dma_start(out[n], out_sb[:, i, :].rearrange("p (t c) -> p t c", c=CH)).then_inc(stored[i], 16)
            for i in range(2):
                sp.wait_ge(stored[i], 16 * ALL_BLOCKS // 2)
            sp.wait_ge(att_loaded, 16 * GROUPS * (ALL_BLOCKS + 2))
            sp.wait_ge(tok_loaded, 16 * (ALL_BLOCKS + 2))

        @block.tensor
        def _(pe):
            ident, w_proj = CONSTANTS.of(c, "ident"), WEIGHTS.of(w, "w_proj")
            router, expert_w, ones16 = WEIGHTS.of(w, "router"), WEIGHTS.of(w, "experts"), CONSTANTS16.of(c16, "ones")

            def project(n, i):
                pe.wait_ge(att_loaded, n * (16 * GROUPS) + 16 * GROUPS)
                pe.wait_ge(added, n)
                for t in range(BLOCK_TILES):
                    for r in range(GROUPS):
                        last = nc.tensor.matmul(ps_proj[:, tile_cols(t)], att[:, i, r, tile_cols(t)], w_proj[:, r * P:(r + 1) * P],
                                                start=(r == 0), stop=(r == GROUPS - 1))
                last.then_inc(projected, 1)

            def turn(n, i):
                pe.wait_ge(xn_done, n + 1)
                pe.wait_ge(xn_copied, n)
                for t in range(BLOCK_TILES):
                    last = nc.tensor.transpose(ps_xn[:, tile_cols(t)], xn_tok[:, tile_cols(t)], ident)
                last.then_inc(xn_turned, 1)

            def route(n, i):
                pe.wait_ge(xn_copied, n + 1)
                pe.wait_ge(logits_done, n)
                for t in range(BLOCK_TILES):
                    last = nc.tensor.matmul(ps_router[:, t * EXPERTS:(t + 1) * EXPERTS], xn_ch[:, i, tile_cols(t)], router,
                                            start=True, stop=True)
                last.then_inc(routed, 1)

            def expert_products(n, i, t):
                pe.wait_ge(product_done, n * BLOCK_TILES + max(t - 1, 0))
                for e in range(2):
                    columns = slice(e * BANK, (e + 1) * BANK)
                    nc.tensor.matmul(ps_e[t % 2][:, columns], xn_ch[:, i, tile_cols(t)], expert_w[:, columns], start=True, stop=False)
                    last = nc.tensor.matmul(ps_e[t % 2][:, columns], ones16, bias16[:, columns], start=False, stop=True)
                last.then_inc(expert_done, 1)

            pe.wait_ge(ready, 2)
            project(0, 0)
            turn(0, 0)
            route(0, 0)
            with pe.Fori(0, ALL_BLOCKS // 2) as k:
                for i in range(2):
                    n = k * 2 + i
                    project(n + 1, 1 - i)
                    expert_products(n, i, 0)
                    expert_products(n, i, 1)
                    expert_products(n, i, 2)
                    turn(n + 1, 1 - i)
                    expert_products(n, i, 3)
                    route(n + 1, 1 - i)

        @block.scalar
        def _(act):
            def front(n, i):
                act.wait_ge(moments_done, n * BLOCK_TILES + BLOCK_TILES)
                act.wait_ge(rstd_done, n)
                nc.scalar.activation(log_var[:, :], moments[:, :, 1], ACT.Ln, bias=eps[:, :]).then_inc(log_done, 1)
                act.wait_ge(log_done, n + 1)
                act.wait_ge(xn_done, n)
                nc.scalar.activation(rstd[:, :], log_var[:, :], ACT.Exp, scale=-0.5).then_inc(rstd_done, 1)
                act.wait_ge(xn_turned, n + 1)
                if not (isinstance(n, int) and n == 0):
                    act.wait_ge(expert_done, (n - 1) * BLOCK_TILES)
                nc.scalar.activation(xn_ch[:, i, :], ps_xn[:, :], ACT.Copy).then_inc(xn_copied, 1)
                act.wait_ge(gap_done, n + 1)
                nc.scalar.activation(ratio[:, :], gap[:, :], ACT.Exp).then_inc(ratio_done, 1)

            act.wait_ge(ready, 2)
            front(0, 0)
            with act.Fori(0, ALL_BLOCKS // 2) as k:
                for i in range(2):
                    front(k * 2 + i + 1, 1 - i)

        @block.gpsimd
        def _(pool):
            nc.gpsimd.memset(eps[:, :], LN_EPS).then_inc(ready, 1)
            nc.gpsimd.iota(order_i[:, :], pattern=[[1, EXPERTS]], base=0, channel_multiplier=0).then_inc(ready, 1)
            with pool.Fori(0, ALL_BLOCKS // 2) as k:
                for i in range(2):
                    n = k * 2 + i
                    for t in range(BLOCK_TILES):
                        s, m = t % 2, n * BLOCK_TILES + t
                        w2, w4 = EXPERTS * CH // 2, EXPERTS * CH // 4
                        pool.wait_ge(product_done, m + 1)
                        pool.wait_ge(quartered, n * BLOCK_TILES + max(t - 1, 0))
                        nc.gpsimd.tensor_tensor(half[:, s, :], product[:, s, 0:w2], product[:, s, w2:2 * w2], ALU.add).then_inc(halved, 1)
                        pool.wait_ge(halved, m + 1)
                        pool.wait_ge(tile_mixed, n * BLOCK_TILES + max(t - 1, 0))
                        nc.gpsimd.tensor_tensor(quarter[:, s, :], half[:, s, 0:w4], half[:, s, w4:2 * w4], ALU.add).then_inc(quartered, 1)
                        pool.wait_ge(quartered, m + 1)
                        pool.wait_ge(out_done, n)
                        nc.gpsimd.tensor_tensor(mixed[:, i, tile_cols(t)], quarter[:, s, 0:CH], quarter[:, s, CH:2 * CH], ALU.add).then_inc(tile_mixed, 1)

        @block.vector
        def _(dve):
            spread = lambda v: v.unsqueeze(2).to_broadcast([P, BLOCK_TILES, EXPERTS])

            def norm(n, i):
                dve.wait_ge(projected, n + 1)
                dve.wait_ge(tok_loaded, n * 16 + 16)
                if not (isinstance(n, int) and n == 0):
                    dve.wait_ge(out_done, n - 1)
                nc.vector.tensor_tensor(t_sb[:, i, :], tok[:, i, :], ps_proj[:, :], ALU.add).then_inc(added, 1)
                dve.wait_ge(added, n + 1)
                dve.wait_ge(moments_done, n * BLOCK_TILES)
                for t in range(BLOCK_TILES):
                    nc.vector.bn_stats(stats[:, t, :], t_sb[:, i, tile_cols(t)]).then_inc(stats_done, 1)
                stats_done_due = worked_out(dve, n * BLOCK_TILES + BLOCK_TILES)
                xn_done_due = worked_out(dve, n)
                dve.wait_ge(ready, 3)
                dve.wait_ge(stats_done, stats_done_due)
                dve.wait_ge(xn_done, xn_done_due)
                for t in range(BLOCK_TILES):
                    nc.vector.bn_aggr(moments[:, t, :], stats[:, t, :]).then_inc(moments_done, 1)

            def normalise(n, i):
                dve.wait_ge(rstd_done, n + 1)
                dve.wait_ge(moments_done, n * BLOCK_TILES + BLOCK_TILES)
                dve.wait_ge(xn_turned, n)
                for t in range(BLOCK_TILES):
                    last = nc.vector.tensor_scalar(xn_tok[:, tile_cols(t)], t_sb[:, i, tile_cols(t)], moments[:, t, 0:1], rstd[:, t:t + 1],
                                                   ALU.subtract, ALU.mult)
                last.then_inc(xn_done, 1)

            def choose(n, i):
                dve.wait_ge(routed, n + 1)
                dve.wait_ge(index_done, n * BLOCK_TILES)
                nc.vector.tensor_tensor(logits[:, :, :], ps_router[:, 0:BLOCK_TILES * EXPERTS].rearrange("p (t e) -> p t e", e=EXPERTS),
                                        WEIGHTS.of(w, "router_b").unsqueeze(1).to_broadcast([P, BLOCK_TILES, EXPERTS]), ALU.add).then_inc(logits_done, 1)
                logits_done_due = worked_out(dve, n + 1)
                gap_done_due = worked_out(dve, n)
                dve.wait_ge(ready, 3)
                dve.wait_ge(logits_done, logits_done_due)
                dve.wait_ge(gap_done, gap_done_due)
                for t in range(BLOCK_TILES):
                    nc.vector.max(best[:, t, :], logits[:, t, :]).then_inc(best_done, 1)
                best_done_due = worked_out(dve, n * BLOCK_TILES + BLOCK_TILES)
                small_due = worked_out(dve, n * SMALL)
                dve.wait_ge(ready, 3)
                dve.wait_ge(best_done, best_done_due)
                dve.wait_ge(small, small_due)
                for t in range(BLOCK_TILES):
                    nc.vector.max_index(index[:, t, :], best[:, t, :], logits[:, t, :]).then_inc(index_done, 1)
                dve.wait_ge(ratio_done, n)
                nc.vector.tensor_tensor(gap[:, :], best[:, :, 1], best[:, :, 0], ALU.subtract).then_inc(gap_done, 1)
                dve.wait_ge(index_done, n * BLOCK_TILES + BLOCK_TILES)
                nc.vector.tensor_copy(index_f[:, :, :], index[:, :, :]).then_inc(small, 1)
                dve.wait_ge(small, n * SMALL + 1)
                dve.wait_ge(mix_done, n)
                expert = order[:, :].unsqueeze(1).to_broadcast([P, BLOCK_TILES, EXPERTS])
                nc.vector.tensor_tensor(is_first[:, :, :], expert, spread(index_f[:, :, 0]), ALU.is_equal).then_inc(small, 1)
                nc.vector.tensor_tensor(is_second[:, :, :], expert, spread(index_f[:, :, 1]), ALU.is_equal).then_inc(small, 1)

            def shares(n, i):
                dve.wait_ge(ratio_done, n + 1)
                nc.vector.tensor_scalar(total[:, :], ratio[:, :], 1.0, None, ALU.add).then_inc(small, 1)
                dve.wait_ge(small, n * SMALL + 4)
                nc.vector.reciprocal(share1[:, :], total[:, :]).then_inc(small, 1)
                dve.wait_ge(small, n * SMALL + 5)
                nc.vector.tensor_tensor(share2[:, :], ratio[:, :], share1[:, :], ALU.mult).then_inc(small, 1)
                nc.vector.tensor_tensor(first_w[:, :, :], is_first[:, :, :], spread(share1[:, :]), ALU.mult).then_inc(small, 1)
                dve.wait_ge(small, n * SMALL + SMALL)
                nc.vector.tensor_tensor(second_w[:, :, :], is_second[:, :, :], spread(share2[:, :]), ALU.mult).then_inc(second_done, 1)
                dve.wait_ge(second_done, n + 1)
                if not (isinstance(n, int) and n == 0):
                    dve.wait_ge(product_done, (n - 1) * BLOCK_TILES)
                nc.vector.tensor_tensor(mix[:, i], first_w[:, :, :], second_w[:, :, :], ALU.add).then_inc(mix_done, 1)

            def weigh(n, i, t):
                m = n * BLOCK_TILES + t
                dve.wait_ge(expert_done, m + 1)
                dve.wait_ge(mix_done, n + 1)
                dve.wait_ge(halved, n * BLOCK_TILES + max(t - 1, 0))
                nc.vector.tensor_tensor(product[:, t % 2, :].rearrange("p (e c) -> p e c", c=CH),
                                        ps_e[t % 2][:, :].rearrange("p (e c) -> p e c", c=CH),
                                        mix[:, i, t, :].unsqueeze(2).to_broadcast([P, EXPERTS, CH]), ALU.mult).then_inc(product_done, 1)

            dve.wait_ge(ready, 2)
            nc.vector.tensor_copy(order[:, :], order_i[:, :]).then_inc(ready, 1)
            dve.wait_ge(ready, 3)
            norm(0, 0)
            normalise(0, 0)
            choose(0, 0)
            shares(0, 0)
            with dve.Fori(0, ALL_BLOCKS // 2) as k:
                for i in range(2):
                    n = k * 2 + i
                    norm(n + 1, 1 - i)
                    weigh(n, i, 0)
                    weigh(n, i, 1)
                    normalise(n + 1, 1 - i)
                    weigh(n, i, 2)
                    weigh(n, i, 3)
                    choose(n + 1, 1 - i)
                    shares(n + 1, 1 - i)
                    dve.wait_ge(tile_mixed, n * BLOCK_TILES + BLOCK_TILES)
                    dve.wait_ge(stored[i], k * 16)
                    nc.vector.tensor_tensor(out_sb[:, i, :], t_sb[:, i, :], mixed[:, i, :], ALU.add).then_inc(out_done, 1)


def build(nc, x, weights, constants, constants16, out):
    dram = lambda name, shape, dt=F32: nc.dram_tensor(name, shape, dt).ap()
    scan_in = dram("scan_in", (ALL_CHUNKS, P, STEP))
    scan_out = dram("scan_out", (ALL_CHUNKS, P, STEP))
    gate = dram("gate_dram", (IMAGES, P, TOK))
    left = dram("left_dram", (IMAGES, HALF, TOK))
    tokens = dram("tokens", (ALL_BLOCKS, P, BANK))
    q_parts, k_parts = (dram(n, (IMAGES, PARTS, P, TOK), BF16) for n in ("q_parts", "k_parts"))
    values = dram("values", (IMAGES, GROUPS, P, TILES, P))
    maxima = dram("maxima", (TOP, PARTS, P), BF16)
    attended = dram("attended", (GROUPS, ALL_BLOCKS, P, BANK))
    by_direction = lambda t: t.rearrange("(b k c) p t -> b k p c t", k=DIRS, c=SCAN_CHUNKS)
    x_images = x.rearrange("b h w c -> b (h w) c")
    with ExitStack() as ctx:
        sb = lambda name, shape, dt=F32: ctx.enter_context(nc.sbuf_tensor(name, shape, dt))
        w, c, c16 = sb("w", [P, WEIGHTS.n]), sb("c", [P, CONSTANTS.n]), sb("c16", [P, CONSTANTS16.n], BF16)
        d, bias16 = sb("d", [P, DERIVED.n]), sb("bias16", [P, EXPERTS * P], BF16)
        prepare(nc, weights, constants, constants16, w, c, c16, d, bias16)
        conv_front(nc, x_images, w, c, d, by_direction(scan_in), gate, left)
        state_scan(nc, w, c, c16, d, scan_in, scan_out)
        conv_back(nc, x_images, w, c, d, by_direction(scan_out), gate, left, tokens, q_parts, k_parts, values)
        attention(nc, c, c16, q_parts, k_parts, values, maxima, attended)
        experts(nc, w, c, c16, bias16, attended, tokens, out.rearrange("b h w c -> (b h w) c").rearrange("(n t p) c -> n p t c", p=P, t=BLOCK_TILES))


def lay_out_weights(i):
    w = np.zeros((P, WEIGHTS.n), np.float32)
    col = lambda name: WEIGHTS.of(w, name)
    L, R = slice(0, HALF), slice(HALF, P)
    g = lambda name: np.asarray(i["L0_conv_" + name])
    col("in1x1")[L, L], col("in1x1")[R, R] = g("cv2_w").T, g("cv1_w").T
    col("in_scale")[:, 0] = np.concatenate([g("cv2_g"), g("cv1_g")])
    col("in_bias")[:, 0] = np.concatenate([g("cv2_b"), g("cv1_b")])
    col("bn0_scale")[:, 0] = np.concatenate([g("bn0_g"), np.ones(HALF, np.float32)])
    col("bn0_bias")[L, 0] = g("bn0_b")
    col("xh")[L], col("xh")[R], col("gate")[R] = g("in_proj_w")[:P].T, g("in_proj_w")[:P].T, g("in_proj_w")[P:].T
    dw = g("dw_w").reshape(3, 3 * P)
    col("dw")[R], col("dw")[L, :3 * P] = np.concatenate([dw[0], dw[2]]), dw[1]
    col("dw_b")[:, 0] = g("dw_b")
    for n in ("1", "2"):
        taps = g(f"c{n}_w").reshape(3, 3, HALF, HALF).transpose(2, 0, 1, 3).reshape(HALF, 3, 3 * HALF)
        col("c" + n)[L], col("c" + n)[R, :3 * HALF] = np.concatenate([taps[:, 0], taps[:, 2]], axis=1), taps[:, 1]
        for v in (f"c{n}_b", f"bn{n}_g", f"bn{n}_b"):
            col(v)[L, 0], col(v)[R, 0] = g(v), g(v)
    col("c3")[R], col("c3_b")[L, 0] = g("c3_w").T, g("c3_b")
    xp = g("x_proj_w")
    bc = xp[:, DT_RANK:].transpose(2, 0, 1)
    col("bc")[:] = np.concatenate([bc] * PARTS, axis=2).reshape(P, DIRS * 96)
    col("xp_dt")[:DT_RANK] = xp[:, :DT_RANK].transpose(1, 0, 2).reshape(DT_RANK, DIRS * P)
    col("dt_w")[:DT_RANK] = g("dt_w").transpose(2, 0, 1).reshape(DT_RANK, DIRS * P)
    col("dt_b")[:] = g("dt_b").T
    col("a_logs")[:] = g("A_logs").reshape(DIRS, P, STATES).transpose(1, 0, 2).reshape(P, DIRS * STATES)
    col("skip")[:] = g("Ds").reshape(DIRS, P).T
    col("ln_g")[:, 0], col("ln_b")[:, 0] = g("ln_g"), g("ln_b")
    col("out_proj")[L] = g("out_proj_w")
    col("cv")[L, HALF:] = g("cv_w").T
    col("cv_g")[R, 0], col("cv_b")[R, 0] = g("cv_g"), g("cv_b")
    shuffle = np.arange(P).reshape(2, HALF).T.reshape(P)
    col("cv3")[:] = g("cv3_w")[shuffle].T
    col("cv3_g")[:, 0], col("cv3_b")[:, 0] = g("cv3_g")[shuffle], g("cv3_b")[shuffle]
    col("qkv")[:] = i["L1_attn_w_attn"]
    wp = np.zeros((2, HEADS // 2, 2 * HEAD, P), np.float32)
    wp[:, :, :HEAD] = np.asarray(i["L1_attn_w_proj"]).reshape(2, HEADS // 2, HEAD, P)
    col("w_proj")[:] = wp.reshape(2, P, P).transpose(1, 0, 2).reshape(P, 2 * P)
    col("router")[:] = i["L1_ffn_router_w"]
    col("router_b")[:] = np.broadcast_to(i["L1_ffn_router_b"], (P, EXPERTS))
    col("experts")[:] = np.asarray(i["L1_ffn_expert_w"]).transpose(1, 0, 2).reshape(P, EXPERTS * P)
    col("expert_b")[:PARTS] = np.broadcast_to(np.asarray(i["L1_ffn_expert_b"]).reshape(1, EXPERTS * P), (PARTS, EXPERTS * P))
    return w


def lay_out_constants():
    c, c16 = np.zeros((P, CONSTANTS.n), np.float32), np.zeros((P, CONSTANTS16.n), np.float32)
    CONSTANTS.of(c, "ident")[:] = np.eye(P)
    CONSTANTS.of(c, "mean")[:] = 1.0 / P
    CONSTANTS.of(c, "part_a")[32:96] = -1.0
    CONSTANTS.of(c, "part_b")[64:96] = -1.0
    CONSTANTS.of(c, "row_a")[1:3] = -1.0
    CONSTANTS.of(c, "row_b")[2:3] = -1.0
    for h in range(HEADS // 2):
        CONSTANTS.of(c, "head_sum")[32 * h + HEAD, 32 * h:32 * h + 32] = 1.0
    for n in range(2 * STATES):
        CONSTANTS16.of(c16, "select")[n:96:32, n * P:(n + 1) * P] = 1.0
    CONSTANTS16.of(c16, "ident")[:] = np.eye(P)
    CONSTANTS16.of(c16, "above")[:] = np.where(np.arange(P)[:, None] > np.arange(P)[None, :], MASKED, 0.0)
    CONSTANTS16.of(c16, "below")[:] = np.where(np.arange(P)[:, None] < np.arange(P)[None, :], MASKED, 0.0)
    CONSTANTS16.of(c16, "ones")[:PARTS] = 1.0
    return c, c16.astype(mybir.dt.np(BF16))


def kernel(**inputs):
    import concourse.bacc as bacc
    from concourse.bass_utils import run_bass_kernel_spmd

    nc = bacc.Bacc("TRN2", target_bir_lowering=False, num_devices=1)
    c, c16 = lay_out_constants()
    arrays = {"x_in": np.ascontiguousarray(inputs["x"]), "weights": lay_out_weights(inputs), "constants": c, "constants16": c16}
    args = [nc.dram_tensor(n, a.shape, mybir.dt.from_np(a.dtype), kind="ExternalInput").ap() for n, a in arrays.items()]
    out = nc.dram_tensor("out", (IMAGES, SIDE, SIDE, CH), F32, kind="ExternalOutput").ap()
    build(nc, *args, out)
    result = run_bass_kernel_spmd(nc, [arrays], core_ids=[0])
    return result.results[0]["out"]
```
